# Optimizing a Trainium2 kernel written in Bass

```python
import numpy as np
import jax
import jax.numpy as jnp

def _softmax(x, axis=-1):
    return jax.nn.softmax(x, axis=axis)

def _gelu(x):
    return jax.nn.gelu(x, approximate=True)

def _silu(x):
    return jax.nn.silu(x)

def _sigmoid(x):
    return jax.nn.sigmoid(x)

def _layernorm(x, axis=-1, eps=1e-05):
    m = jnp.mean(x, axis=axis, keepdims=True)
    v = jnp.var(x, axis=axis, keepdims=True)
    return (x - m) / jnp.sqrt(v + eps)

def _scatter_add(tgt, idx, src, axis=0):
    return tgt.at[idx].add(src)

def _segment_sum(src, seg, n):
    return jax.ops.segment_sum(src, seg, n)
kernel_name = 'mk_xattn_ffn_d2_seqx_r4_91ab09'

def setup_inputs(seed: int=0):
    np.random.seed(seed)
    _w = jnp.asarray

    def _rec_inputs():
        import jax
        import jax.numpy as jnp
        _rk = jax.random.key(seed)
        x = -0.0002928 + 1 * jax.random.normal(jax.random.fold_in(_rk, 1), (4, 512, 256), jnp.float32)
        _lenS = 512 - jax.random.randint(jax.random.fold_in(_rk, 7), (4,), 0, max(1, 512 // 4) + 1, jnp.int32)
        _lenS2 = 1601 - jax.random.randint(jax.random.fold_in(_rk, 8), (4,), 0, max(1, 1601 // 4) + 1, jnp.int32)
        _ctx_512P = jax.random.normal(jax.random.fold_in(_rk, 11), (4, 16, 128), jnp.float32)
        _ctx_512c = jax.random.dirichlet(jax.random.fold_in(_rk, 511), 0.3 * jnp.ones((16,), jnp.float32), (4, 1601))
        _ctx_512t = jnp.einsum('bsk,bkd->bsd', _ctx_512c, _ctx_512P)
        _ctx_512t = _ctx_512t * jax.lax.rsqrt(jnp.mean(jnp.square(_ctx_512t)) + 1e-12) * 0.953939
        ctx_512 = 0.00222621 + 0.99962 * (_ctx_512t + 0.3 * jax.random.normal(jax.random.fold_in(_rk, 611), (4, 1601, 128), jnp.float32))
        return (x, ctx_512)
    x, ctx_512 = _rec_inputs()

    def _L0_xattn_setup():
        import jax, jax.numpy as jnp
        import numpy as np
        B, T, TC, C, CC, H = (2, 512, 128, 256, 128, 16)
        D = C // H

        def _heads(t):
            b, l, _ = t.shape
            return t.reshape(b, l, H, D).transpose(0, 2, 1, 3)
        key = jax.random.key(seed)
        ks = jax.random.split(key, 18)
        w = lambda k, i, o: jax.random.normal(k, (i, o), jnp.float32) / np.sqrt(i).astype(np.float32)
        return {'x': jax.random.normal(ks[0], (B, T, C), jnp.float32), 'cross_input': jax.random.normal(ks[1], (B, TC, CC), jnp.float32), 'Wk': w(ks[2], C, C), 'bk': jnp.zeros((C,), jnp.float32), 'Wq': w(ks[3], C, C), 'bq': jnp.zeros((C,), jnp.float32), 'Wv': w(ks[4], C, C), 'bv': jnp.zeros((C,), jnp.float32), 'Wck': w(ks[5], CC, C), 'bck': jnp.zeros((C,), jnp.float32), 'Wcq': w(ks[6], C, C), 'bcq': jnp.zeros((C,), jnp.float32), 'Wcv': w(ks[7], CC, C), 'bcv': jnp.zeros((C,), jnp.float32), 'Wp': w(ks[8], C, C), 'bp': jnp.zeros((C,), jnp.float32)}
    _L0_xattn_all = _L0_xattn_setup()
    _L0_xattn_in = {k: v for k, v in _L0_xattn_all.items() if k in ('Wk', 'bk', 'Wq', 'bq', 'Wv', 'bv', 'Wck', 'bck', 'Wcq', 'bcq', 'Wcv', 'bcv', 'Wp', 'bp')}
    del _L0_xattn_all

    def _L0_ffn_setup():
        import jax, jax.numpy as jnp
        import numpy as np
        DIM = 256
        DEPTH = 2
        HEADS = 8
        DIM_HEAD = 64
        WINDOW = 128
        INNER = HEADS * DIM_HEAD
        HID = int(DIM * 4 * 2 / 3)
        B, N = (2, 2048)
        QK_SCALE = 8.0

        def shift_token(t):
            t1, t2 = jnp.split(t, 2, axis=-1)
            t2 = jnp.pad(t2, ((0, 0), (1, 0), (0, 0)))[:, :-1]
            return jnp.concatenate([t1, t2], axis=-1)

        def l2norm(t):
            return t / jnp.clip(jnp.linalg.norm(t, axis=-1, keepdims=True), 1e-12)

        def rotate_half(x):
            x1, x2 = jnp.split(x, 2, axis=-1)
            return jnp.concatenate([-x2, x1], axis=-1)

        def rotary_xpos(q, k):
            n = q.shape[-2]
            half_idx = jnp.arange(0, DIM_HEAD, 2, dtype=jnp.float32)
            inv_freq = 1.0 / 10000.0 ** (half_idx / DIM_HEAD)
            t = jnp.arange(n, dtype=jnp.float32)
            freqs = t[:, None] * inv_freq[None, :]
            freqs = jnp.concatenate([freqs, freqs], axis=-1)
            base = (half_idx + 0.4 * DIM_HEAD) / (1.4 * DIM_HEAD)
            power = (t - n // 2) / float(WINDOW // 2)
            scale = base[None, :] ** power[:, None]
            scale = jnp.concatenate([scale, scale], axis=-1)
            cos, sin = (jnp.cos(freqs), jnp.sin(freqs))
            q = q * cos * scale + rotate_half(q) * sin * scale
            k = k * cos / scale + rotate_half(k) * sin / scale
            return (q, k)

        def local_attention(q, k, v):
            b, h, n, d = q.shape
            w = n // WINDOW
            bq = q.reshape(b, h, w, WINDOW, d) * QK_SCALE
            bk = k.reshape(b, h, w, WINDOW, d)
            bv = v.reshape(b, h, w, WINDOW, d)

            def look_around(t):
                p = jnp.pad(t, ((0, 0), (0, 0), (1, 0), (0, 0), (0, 0)))
                return jnp.concatenate([p[:, :, :w], p[:, :, 1:]], axis=3)
            bk, bv = (look_around(bk), look_around(bv))
            bt = jnp.arange(n).reshape(w, WINDOW)
            btp = jnp.pad(bt, ((1, 0), (0, 0)), constant_values=-1)
            btk = jnp.concatenate([btp[:w], btp[1:]], axis=1)
            sim = jnp.einsum('bhwid,bhwjd->bhwij', bq, bk)
            i = bt[:, :, None]
            j = btk[:, None, :]
            mask = (i < j) | (i > j + WINDOW) | (j == -1)
            sim = jnp.where(mask, -jnp.finfo(sim.dtype).max, sim)
            attn = jax.nn.softmax(sim, axis=-1)
            out = jnp.einsum('bhwij,bhwjd->bhwid', attn, bv)
            return out.reshape(b, h, n, d)

        def _layer(x, wqkv, qs, ksc, wo, lg, lb, w1, b1, w2, b2):
            b, n, _ = x.shape
            h = shift_token(x)
            qkv = h @ wqkv
            q, k, v = jnp.split(qkv, 3, axis=-1)
            to_heads = lambda t: t.reshape(b, n, HEADS, DIM_HEAD).transpose(0, 2, 1, 3)
            q, k, v = (to_heads(q), to_heads(k), to_heads(v))
            q = l2norm(q) * qs
            k = l2norm(k) * ksc
            q, k = rotary_xpos(q, k)
            o = local_attention(q, k, v)
            o = o.transpose(0, 2, 1, 3).reshape(b, n, INNER)
            x = x + o @ wo
            h = shift_token(x)
            mu = h.mean(-1, keepdims=True)
            var = h.var(-1, keepdims=True)
            h = (h - mu) / jnp.sqrt(var + 1e-05) * lg + lb
            h = h @ w1 + b1
            a, g = jnp.split(h, 2, axis=-1)
            h = a * jax.nn.gelu(g, approximate=False)
            x = x + h @ w2 + b2
            return x
        key = jax.random.key(seed)
        ks = jax.random.split(key, 6)
        return {'x': jax.random.normal(ks[0], (B, N, DIM), jnp.float32), 'wqkv': jax.random.normal(ks[1], (DEPTH, DIM, 3 * INNER), jnp.float32) * 0.02, 'q_scale': jnp.ones((DEPTH, DIM_HEAD), jnp.float32), 'k_scale': jnp.ones((DEPTH, DIM_HEAD), jnp.float32), 'wo': jax.random.normal(ks[2], (DEPTH, INNER, DIM), jnp.float32) * 0.02, 'ln_g': jnp.ones((DEPTH, DIM), jnp.float32), 'ln_b': jnp.zeros((DEPTH, DIM), jnp.float32), 'w1': jax.random.normal(ks[3], (DEPTH, DIM, 2 * HID), jnp.float32) * 0.02, 'b1': jnp.zeros((DEPTH, 2 * HID), jnp.float32), 'w2': jax.random.normal(ks[4], (DEPTH, HID, DIM), jnp.float32) * 0.02, 'b2': jnp.zeros((DEPTH, DIM), jnp.float32)}
    _L0_ffn_all = _L0_ffn_setup()
    _L0_ffn_in = {k: v for k, v in _L0_ffn_all.items() if k in ('wqkv', 'q_scale', 'k_scale', 'wo', 'ln_g', 'ln_b', 'w1', 'b1', 'w2', 'b2')}
    del _L0_ffn_all

    def _L1_xattn_setup():
        import jax, jax.numpy as jnp
        import numpy as np
        HEADS = 16
        D_MODEL = 256
        IMG_MODEL = 128
        D_K = D_MODEL // HEADS
        key = jax.random.key(seed)
        ks = jax.random.split(key, 12)
        B, LQ, LKV = (8, 512, 256)
        s_dm = 1.0 / np.sqrt(D_MODEL)
        s_im = 1.0 / np.sqrt(IMG_MODEL)
        return {'q': jax.random.normal(ks[0], (B, LQ, D_MODEL), jnp.float32), 'k': jax.random.normal(ks[1], (B, LKV, IMG_MODEL), jnp.float32), 'v': jax.random.normal(ks[2], (B, LKV, IMG_MODEL), jnp.float32), 'Wq': jax.random.normal(ks[3], (D_MODEL, D_MODEL), jnp.float32) * s_dm, 'bq': jnp.zeros((D_MODEL,), jnp.float32), 'Wk': jax.random.normal(ks[4], (IMG_MODEL, D_MODEL), jnp.float32) * s_im, 'bk': jnp.zeros((D_MODEL,), jnp.float32), 'Wv': jax.random.normal(ks[5], (IMG_MODEL, D_MODEL), jnp.float32) * s_im, 'bv': jnp.zeros((D_MODEL,), jnp.float32), 'Wo': jax.random.normal(ks[6], (D_MODEL, D_MODEL), jnp.float32) * s_dm, 'bo': jnp.zeros((D_MODEL,), jnp.float32)}
    _L1_xattn_all = _L1_xattn_setup()
    _L1_xattn_in = {k: v for k, v in _L1_xattn_all.items() if k in ('Wq', 'bq', 'Wk', 'bk', 'Wv', 'bv', 'Wo', 'bo')}
    del _L1_xattn_all

    def _L1_ffn_setup():
        import jax, jax.numpy as jnp
        import numpy as np
        E = 8
        K = 2
        CAPACITY_FACTOR = 1.25
        key = jax.random.key(seed)
        ks = jax.random.split(key, 4)
        B, T, C, H = (8, 512, 256, 1024)
        x = jax.random.normal(ks[0], (B, T, C), jnp.float32)
        Wr = jax.random.normal(ks[1], (C, E), jnp.float32) * 0.02
        br = jnp.zeros((E,), jnp.float32)
        W1 = jax.random.normal(ks[2], (E, C, H), jnp.float32) * 0.02
        b1 = jnp.zeros((E, H), jnp.float32)
        W2 = jax.random.normal(ks[3], (E, H, C), jnp.float32) * 0.02
        b2 = jnp.zeros((E, C), jnp.float32)
        return {'x': x, 'Wr': Wr, 'br': br, 'W1': W1, 'b1': b1, 'W2': W2, 'b2': b2}
    _L1_ffn_all = _L1_ffn_setup()
    _L1_ffn_in = {k: v for k, v in _L1_ffn_all.items() if k in ('Wr', 'br', 'W1', 'b1', 'W2', 'b2')}
    del _L1_ffn_all
    return {'x': x, 'ctx_512': ctx_512, 'L0_xattn_Wk': _L0_xattn_in['Wk'], 'L0_xattn_bk': _L0_xattn_in['bk'], 'L0_xattn_Wq': _L0_xattn_in['Wq'], 'L0_xattn_bq': _L0_xattn_in['bq'], 'L0_xattn_Wv': _L0_xattn_in['Wv'], 'L0_xattn_bv': _L0_xattn_in['bv'], 'L0_xattn_Wck': _L0_xattn_in['Wck'], 'L0_xattn_bck': _L0_xattn_in['bck'], 'L0_xattn_Wcq': _L0_xattn_in['Wcq'], 'L0_xattn_bcq': _L0_xattn_in['bcq'], 'L0_xattn_Wcv': _L0_xattn_in['Wcv'], 'L0_xattn_bcv': _L0_xattn_in['bcv'], 'L0_xattn_Wp': _L0_xattn_in['Wp'], 'L0_xattn_bp': _L0_xattn_in['bp'], 'L0_ffn_wqkv': _L0_ffn_in['wqkv'], 'L0_ffn_q_scale': _L0_ffn_in['q_scale'], 'L0_ffn_k_scale': _L0_ffn_in['k_scale'], 'L0_ffn_wo': _L0_ffn_in['wo'], 'L0_ffn_ln_g': _L0_ffn_in['ln_g'], 'L0_ffn_ln_b': _L0_ffn_in['ln_b'], 'L0_ffn_w1': _L0_ffn_in['w1'], 'L0_ffn_b1': _L0_ffn_in['b1'], 'L0_ffn_w2': _L0_ffn_in['w2'], 'L0_ffn_b2': _L0_ffn_in['b2'], 'L1_xattn_Wq': _L1_xattn_in['Wq'], 'L1_xattn_bq': _L1_xattn_in['bq'], 'L1_xattn_Wk': _L1_xattn_in['Wk'], 'L1_xattn_bk': _L1_xattn_in['bk'], 'L1_xattn_Wv': _L1_xattn_in['Wv'], 'L1_xattn_bv': _L1_xattn_in['bv'], 'L1_xattn_Wo': _L1_xattn_in['Wo'], 'L1_xattn_bo': _L1_xattn_in['bo'], 'L1_ffn_Wr': _L1_ffn_in['Wr'], 'L1_ffn_br': _L1_ffn_in['br'], 'L1_ffn_W1': _L1_ffn_in['W1'], 'L1_ffn_b1': _L1_ffn_in['b1'], 'L1_ffn_W2': _L1_ffn_in['W2'], 'L1_ffn_b2': _L1_ffn_in['b2']}

def reference(x, ctx_512, L0_xattn_Wk, L0_xattn_bk, L0_xattn_Wq, L0_xattn_bq, L0_xattn_Wv, L0_xattn_bv, L0_xattn_Wck, L0_xattn_bck, L0_xattn_Wcq, L0_xattn_bcq, L0_xattn_Wcv, L0_xattn_bcv, L0_xattn_Wp, L0_xattn_bp, L0_ffn_wqkv, L0_ffn_q_scale, L0_ffn_k_scale, L0_ffn_wo, L0_ffn_ln_g, L0_ffn_ln_b, L0_ffn_w1, L0_ffn_b1, L0_ffn_w2, L0_ffn_b2, L1_xattn_Wq, L1_xattn_bq, L1_xattn_Wk, L1_xattn_bk, L1_xattn_Wv, L1_xattn_bv, L1_xattn_Wo, L1_xattn_bo, L1_ffn_Wr, L1_ffn_br, L1_ffn_W1, L1_ffn_b1, L1_ffn_W2, L1_ffn_b2):
    import jax
    import jax.numpy as jnp

    def _L0_xattn_ref(x, cross_input, Wk, bk, Wq, bq, Wv, bv, Wck, bck, Wcq, bcq, Wcv, bcv, Wp, bp):
        import jax, jax.numpy as jnp
        import numpy as np
        B, T, TC, C, CC, H = (2, 512, 128, 256, 128, 16)
        D = C // H

        def _heads(t):
            b, l, _ = t.shape
            return t.reshape(b, l, H, D).transpose(0, 2, 1, 3)
        scale = np.float32(1.0 / np.sqrt(D))
        q = _heads(x @ Wq + bq)
        k = _heads(x @ Wk + bk)
        v = _heads(x @ Wv + bv)
        att = jnp.einsum('bhqd,bhkd->bhqk', q, k) * scale
        causal = jnp.tril(jnp.ones((T, T), bool))
        att = jnp.where(causal[None, None], att, -jnp.inf)
        y = jnp.einsum('bhqk,bhkd->bhqd', jax.nn.softmax(att, axis=-1), v)
        qc = _heads(x @ Wcq + bcq)
        kc = _heads(cross_input @ Wck + bck)
        vc = _heads(cross_input @ Wcv + bcv)
        attc = jnp.einsum('bhqd,bhkd->bhqk', qc, kc) * scale
        y = y + jnp.einsum('bhqk,bhkd->bhqd', jax.nn.softmax(attc, axis=-1), vc)
        y = y.transpose(0, 2, 1, 3).reshape(x.shape[0], T, C)
        return y @ Wp + bp

    def _L0_ffn_ref(x, wqkv, q_scale, k_scale, wo, ln_g, ln_b, w1, b1, w2, b2):
        import jax, jax.numpy as jnp
        import numpy as np
        DIM = 256
        DEPTH = 2
        HEADS = 8
        DIM_HEAD = 64
        WINDOW = 128
        INNER = HEADS * DIM_HEAD
        HID = int(DIM * 4 * 2 / 3)
        B, N = (2, 2048)
        QK_SCALE = 8.0

        def shift_token(t):
            t1, t2 = jnp.split(t, 2, axis=-1)
            t2 = jnp.pad(t2, ((0, 0), (1, 0), (0, 0)))[:, :-1]
            return jnp.concatenate([t1, t2], axis=-1)

        def l2norm(t):
            return t / jnp.clip(jnp.linalg.norm(t, axis=-1, keepdims=True), 1e-12)

        def rotate_half(x):
            x1, x2 = jnp.split(x, 2, axis=-1)
            return jnp.concatenate([-x2, x1], axis=-1)

        def rotary_xpos(q, k):
            n = q.shape[-2]
            half_idx = jnp.arange(0, DIM_HEAD, 2, dtype=jnp.float32)
            inv_freq = 1.0 / 10000.0 ** (half_idx / DIM_HEAD)
            t = jnp.arange(n, dtype=jnp.float32)
            freqs = t[:, None] * inv_freq[None, :]
            freqs = jnp.concatenate([freqs, freqs], axis=-1)
            base = (half_idx + 0.4 * DIM_HEAD) / (1.4 * DIM_HEAD)
            power = (t - n // 2) / float(WINDOW // 2)
            scale = base[None, :] ** power[:, None]
            scale = jnp.concatenate([scale, scale], axis=-1)
            cos, sin = (jnp.cos(freqs), jnp.sin(freqs))
            q = q * cos * scale + rotate_half(q) * sin * scale
            k = k * cos / scale + rotate_half(k) * sin / scale
            return (q, k)

        def local_attention(q, k, v):
            b, h, n, d = q.shape
            w = n // WINDOW
            bq = q.reshape(b, h, w, WINDOW, d) * QK_SCALE
            bk = k.reshape(b, h, w, WINDOW, d)
            bv = v.reshape(b, h, w, WINDOW, d)

            def look_around(t):
                p = jnp.pad(t, ((0, 0), (0, 0), (1, 0), (0, 0), (0, 0)))
                return jnp.concatenate([p[:, :, :w], p[:, :, 1:]], axis=3)
            bk, bv = (look_around(bk), look_around(bv))
            bt = jnp.arange(n).reshape(w, WINDOW)
            btp = jnp.pad(bt, ((1, 0), (0, 0)), constant_values=-1)
            btk = jnp.concatenate([btp[:w], btp[1:]], axis=1)
            sim = jnp.einsum('bhwid,bhwjd->bhwij', bq, bk)
            i = bt[:, :, None]
            j = btk[:, None, :]
            mask = (i < j) | (i > j + WINDOW) | (j == -1)
            sim = jnp.where(mask, -jnp.finfo(sim.dtype).max, sim)
            attn = jax.nn.softmax(sim, axis=-1)
            out = jnp.einsum('bhwij,bhwjd->bhwid', attn, bv)
            return out.reshape(b, h, n, d)

        def _layer(x, wqkv, qs, ksc, wo, lg, lb, w1, b1, w2, b2):
            b, n, _ = x.shape
            h = shift_token(x)
            qkv = h @ wqkv
            q, k, v = jnp.split(qkv, 3, axis=-1)
            to_heads = lambda t: t.reshape(b, n, HEADS, DIM_HEAD).transpose(0, 2, 1, 3)
            q, k, v = (to_heads(q), to_heads(k), to_heads(v))
            q = l2norm(q) * qs
            k = l2norm(k) * ksc
            q, k = rotary_xpos(q, k)
            o = local_attention(q, k, v)
            o = o.transpose(0, 2, 1, 3).reshape(b, n, INNER)
            x = x + o @ wo
            h = shift_token(x)
            mu = h.mean(-1, keepdims=True)
            var = h.var(-1, keepdims=True)
            h = (h - mu) / jnp.sqrt(var + 1e-05) * lg + lb
            h = h @ w1 + b1
            a, g = jnp.split(h, 2, axis=-1)
            h = a * jax.nn.gelu(g, approximate=False)
            x = x + h @ w2 + b2
            return x
        for l in range(DEPTH):
            x = _layer(x, wqkv[l], q_scale[l], k_scale[l], wo[l], ln_g[l], ln_b[l], w1[l], b1[l], w2[l], b2[l])
        return x

    def _L1_xattn_ref(q, k, v, Wq, bq, Wk, bk, Wv, bv, Wo, bo):
        import jax, jax.numpy as jnp
        import numpy as np
        HEADS = 16
        D_MODEL = 256
        IMG_MODEL = 128
        D_K = D_MODEL // HEADS
        B, LQ, _ = q.shape
        LKV = k.shape[1]
        qh = (q @ Wq + bq).reshape(B, LQ, HEADS, D_K).transpose(0, 2, 1, 3)
        kh = (k @ Wk + bk).reshape(B, LKV, HEADS, D_K).transpose(0, 2, 1, 3)
        vh = (v @ Wv + bv).reshape(B, LKV, HEADS, D_K).transpose(0, 2, 1, 3)
        scale = 1.0 / np.sqrt(D_K)
        scores = jnp.einsum('bhqd,bhkd->bhqk', qh, kh) * scale
        attn = jax.nn.softmax(scores, axis=-1)
        out = jnp.einsum('bhqk,bhkd->bhqd', attn, vh)
        concat = out.transpose(0, 2, 1, 3).reshape(B, LQ, D_MODEL)
        return concat @ Wo + bo

    def _L1_ffn_ref(x, Wr, br, W1, b1, W2, b2):
        import jax, jax.numpy as jnp
        import numpy as np
        E = 8
        K = 2
        CAPACITY_FACTOR = 1.25
        B, T, C = x.shape
        cap = max(1, int(T / E * CAPACITY_FACTOR))
        probs = jax.nn.softmax(x @ Wr + br, axis=-1)
        topk_p, topk_e = jax.lax.top_k(probs, K)
        e_flat = topk_e.reshape(B, T * K)
        p_flat = topk_p.reshape(B, T * K)
        oh = jax.nn.one_hot(e_flat, E, dtype=jnp.int32)
        pos_all = jnp.cumsum(oh, axis=1) - oh
        pos = jnp.take_along_axis(pos_all, e_flat[:, :, None], axis=2)[:, :, 0]
        keep = pos < cap
        b_idx = jnp.arange(B)[:, None]
        flat_idx = (e_flat * B + b_idx) * cap + jnp.minimum(pos, cap - 1)
        x_rep = jnp.broadcast_to(x[:, :, None, :], (B, T, K, C)).reshape(B, T * K, C)
        buf = jnp.zeros((E * B * cap, C), x.dtype).at[flat_idx.reshape(-1)].add((x_rep * keep[:, :, None].astype(x.dtype)).reshape(-1, C))
        buf = buf.reshape(E, B * cap, C)
        h = jax.nn.relu(jnp.einsum('enc,ech->enh', buf, W1) + b1[:, None, :])
        y = jnp.einsum('enh,ehc->enc', h, W2) + b2[:, None, :]
        y_tok = y.reshape(E * B * cap, C)[flat_idx.reshape(-1)].reshape(B, T * K, C)
        y_tok = y_tok * (p_flat * keep.astype(x.dtype))[:, :, None]
        return y_tok.reshape(B, T, K, C).sum(axis=2)
    x = x + _L0_xattn_ref(_layernorm(x, axis=-1), ctx_512, L0_xattn_Wk, L0_xattn_bk, L0_xattn_Wq, L0_xattn_bq, L0_xattn_Wv, L0_xattn_bv, L0_xattn_Wck, L0_xattn_bck, L0_xattn_Wcq, L0_xattn_bcq, L0_xattn_Wcv, L0_xattn_bcv, L0_xattn_Wp, L0_xattn_bp)
    x = x + _L0_ffn_ref(_layernorm(x, axis=-1), L0_ffn_wqkv, L0_ffn_q_scale, L0_ffn_k_scale, L0_ffn_wo, L0_ffn_ln_g, L0_ffn_ln_b, L0_ffn_w1, L0_ffn_b1, L0_ffn_w2, L0_ffn_b2)
    x = x + _L1_xattn_ref(_layernorm(x, axis=-1), ctx_512, ctx_512, L1_xattn_Wq, L1_xattn_bq, L1_xattn_Wk, L1_xattn_bk, L1_xattn_Wv, L1_xattn_bv, L1_xattn_Wo, L1_xattn_bo)
    x = x + _L1_ffn_ref(_layernorm(x, axis=-1), L1_ffn_Wr, L1_ffn_br, L1_ffn_W1, L1_ffn_b1, L1_ffn_W2, L1_ffn_b2)
    return x

_drawn_inputs = setup_inputs


def setup_inputs(seed=0):
    import zlib

    import numpy as np

    out = dict(_drawn_inputs(seed))
    spreads = {'L0_xattn_bk': (0.0, 0.8),
     'L0_xattn_bq': (0.0, 0.637),
     'L0_xattn_bv': (0.0, 0.1),
     'L0_xattn_bck': (0.0, 0.8),
     'L0_xattn_bcq': (0.0, 0.429),
     'L0_xattn_bcv': (0.0, 0.1),
     'L0_xattn_bp': (0.0, 0.1),
     'L0_ffn_q_scale': (1.0, 0.6),
     'L0_ffn_k_scale': (1.0, 0.6),
     'L0_ffn_ln_g': (1.0, 0.6),
     'L0_ffn_ln_b': (0.0, 0.8),
     'L0_ffn_b1': (0.0, 0.8),
     'L0_ffn_b2': (0.0, 0.1),
     'L1_xattn_bq': (0.0, 0.8),
     'L1_xattn_bk': (0.0, 0.8),
     'L1_xattn_bv': (0.0, 0.1),
     'L1_xattn_bo': (0.0, 0.1),
     'L1_ffn_br': (0.0, 0.8),
     'L1_ffn_b1': (0.0, 0.8),
     'L1_ffn_b2': (0.0, 0.8)}
    factors = {'L1_ffn_Wr': 4.379, 'L1_ffn_W1': 5.738, 'L1_ffn_W2': 4.658}
    for name, (base, spread) in spreads.items():
        noise = np.random.default_rng([zlib.crc32(name.encode()), seed]).standard_normal(out[name].shape)
        drawn = base * np.exp(spread * noise) if base else spread * noise
        out[name] = jnp.asarray(drawn.astype(out[name].dtype))
    for name, factor in factors.items():
        out[name] = (out[name] * factor).astype(out[name].dtype)
    return out
```

```python
from contextlib import ExitStack

import numpy as np

import concourse.bass as bass
from concourse import mybir

F32 = mybir.dt.float32
BF16 = mybir.dt.bfloat16
ALU = mybir.AluOpType
ACT = mybir.ActivationFunctionType
AX_X = mybir.AxisListType.X

P = 128
B, T, C = 4, 512, 256
NT = T // P
CT = C // P
H, D = 16, 16
HG = 4
NG = H // HG
TC, CC = 1601, 128
NEG = -1e30
EPS = 1e-5
QPAIR = "aabbac"
KPAIR = "ababca"
RM = 16 * len(QPAIR)
KROWS = RM + 3
PACKED = 16 * len(QPAIR)


class Phase:

    def __init__(self, nc, name):
        self.nc, self.name, self.ctx, self.sems = nc, name, ExitStack(), []

    def __enter__(self):
        self.ctx.__enter__()
        return self

    def __exit__(self, *a):
        return self.ctx.__exit__(*a)

    def sb(self, name, shape, dt=F32):
        return self.ctx.enter_context(self.nc.sbuf_tensor(f"{self.name}_{name}", shape, dt))

    def ps(self, name, shape, dt=F32):
        return self.ctx.enter_context(self.nc.psum_tensor(f"{self.name}_{name}", shape, dt))

    def sem(self, name):
        s = self.ctx.enter_context(self.nc.semaphore(f"{self.name}_{name}"))
        self.sems.append(s)
        return s

    def clear(self):
        self.nc.all_engine_barrier()
        for n, s in enumerate(self.sems):
            (self.nc.sync, self.nc.gpsimd)[n % 2].sem_clear(s)
        self.nc.all_engine_barrier()


def chunks(n, size):
    return [(i, min(size, n - i)) for i in range(0, n, size)]


def setup_constants(nc, ph):
    k = {
        "ident": ph.sb("ident", [P, P]), "identb": ph.sb("identb", [P, P], BF16),
        "q_from_k": ph.sb("q_from_k", [P, P], BF16), "k_from_q": ph.sb("k_from_q", [P, 2 * P], BF16),
        "half": ph.sb("half", [P, NT * 16]),
    }
    made = ph.sem("made")
    with nc.Block() as block:
        @block.gpsimd
        def _(pool):
            nc.gpsimd.memset(k["ident"][:], 0.0).then_inc(made, 1)
            nc.gpsimd.memset(k["q_from_k"][:], 0.0).then_inc(made, 1)
            nc.gpsimd.memset(k["k_from_q"][:], 0.0).then_inc(made, 1)
            nc.gpsimd.memset(k["half"][:], -0.5).then_inc(made, 1)
            pool.wait_ge(made, 4)
            nc.gpsimd.affine_select(out=k["ident"][:], in_=k["ident"][:], compare_op=ALU.not_equal, fill=1.0,
                                    base=0, pattern=[[-1, P]], channel_multiplier=1).then_inc(made, 1)
            nc.gpsimd.affine_select(out=k["q_from_k"][:], in_=k["q_from_k"][:], compare_op=ALU.is_ge, fill=NEG,
                                    base=0, pattern=[[1, P]], channel_multiplier=-1).then_inc(made, 1)
            nc.gpsimd.affine_select(out=k["k_from_q"][:, 0:P], in_=k["k_from_q"][:, 0:P], compare_op=ALU.is_ge,
                                    fill=NEG, base=0, pattern=[[1, P]], channel_multiplier=-1).then_inc(made, 1)
            nc.gpsimd.affine_select(out=k["k_from_q"][:, P:2 * P], in_=k["k_from_q"][:, P:2 * P],
                                    compare_op=ALU.is_ge, fill=NEG, base=0, pattern=[[-1, P]],
                                    channel_multiplier=1).then_inc(made, 1)
            pool.wait_ge(made, 8)
            nc.gpsimd.tensor_copy(k["identb"][:], k["ident"][:]).then_inc(made, 1)
            pool.wait_ge(made, 9)
    ph.clear()
    return k


def layernorm_stats(nc, dve, src, stats, mv, counted, first):
    for t in range(NT):
        nc.vector.bn_stats(stats[:, t], src(t)).then_inc(counted, 1)
    for t in range(NT):
        dve.wait_ge(counted, first + t + 1)
        nc.vector.bn_aggr(mv[:, t], stats[:, t]).then_inc(counted, 1)


def wide_attention(nc, k, x_all, name, src_dram, ctx_dram, w, causal):
    nk = T if causal else TC
    ktiles = chunks(nk, P)
    KT = len(ktiles)
    kchunks = chunks(nk, T if causal else 401)
    kvc = CT if causal else 1
    n_s1 = HG * NT * len(kchunks)
    NCH = len(kchunks)

    with Phase(nc, name) as ph:
        wq, wo = ph.sb("wq", [P, CT, C]), ph.sb("wo", [P, NG, C])
        wk, wv = ph.sb("wk", [P, kvc, C]), ph.sb("wv", [P, kvc, C])
        bq, bk = ph.sb("bq", [P, CT]), ph.sb("bk", [P, CT])
        bv, bo = ph.sb("bv", [P, C]), ph.sb("bo", [P, C])
        prob = ph.sb("prob", [P, 4, 2, T])
        scratch = ph.sb("scratch", [P, 2, T])
        den, rden = scratch[:, 0], scratch[:, 1]
        xs = scratch[:].rearrange("p a (t c) -> p (a t) c", c=C)
        xn, xnT = ph.sb("xn", [P, NT, C]), ph.sb("xnT", [P, CT, T])
        stats, mv, rstd = ph.sb("stats", [P, NT, 6]), ph.sb("mv", [P, NT, 2]), ph.sb("rstd", [P, NT])
        veps = ph.sb("veps", [P, NT])
        qparts, kparts = ph.sb("qparts", [P, CT, 3, T], BF16), ph.sb("kparts", [P, CT, 3, nk], BF16)
        qspill = nc.dram_tensor(f"{name}_qspill", [CT, P, 3, T], BF16).ap()
        kspill = nc.dram_tensor(f"{name}_kspill", [CT, P, 3, nk], BF16).ap()
        whole, rest = ph.sb("whole", [P, 2, T]), ph.sb("rest", [P, 2, T])
        qpack, kpack = ph.sb("qpack", [P, H, T], BF16), ph.sb("kpack", [P, H, nk], BF16)
        vals = ph.sb("vals", [P, KT, H, 2 * D])
        y = ph.sb("y", [P, NG, T])
        mx, mxc, mrest = ph.sb("mx", [P, HG * NT, NCH]), ph.sb("mxc", [P, HG * NT]), ph.sb("mrest", [P, HG * NT])
        m3 = ph.sb("m3", [P, HG * NT, 3], BF16)
        if not causal:
            ctx_tok = prob[:].rearrange("p a b t -> p (a b t)")[:, 0:KT * CC].rearrange("p (k c) -> p k c", c=CC)
            ctxT = ph.sb("ctxT", [P, TC])
        ps = ph.ps("ps", [P, 8, 512])

        zeroed, loaded, biases = ph.sem("zeroed"), ph.sem("loaded"), ph.sem("biases")
        with nc.Block() as block:
            @block.gpsimd
            def _(pool):
                nc.gpsimd.memset(wo[:], 0.0).then_inc(zeroed, 1)

            @block.vector
            def _(dve):
                nc.vector.memset(kpack[RM:RM + 32, :, :], 1.0)
                nc.vector.memset(vals[:], 1.0)
                dve.wait_ge(biases, 32)
                nc.vector.tensor_scalar(bq[:], bq[:], 0.25, None, ALU.mult)

            @block.sync
            def _(sp):
                with nc.allow_non_contiguous_dma(reason="bias columns"):
                    sp.dma_start(bq[:], w["bq"].rearrange("(t p) -> p t", p=P)).then_inc(biases, 16)
                    sp.dma_start(bk[:], w["bk"].rearrange("(t p) -> p t", p=P)).then_inc(biases, 16)
                n = 0
                for dst, src in ((wq, w["wq"]), (wk, w["wk"]), (wv, w["wv"])):
                    sp.dma_start(dst[:], src.rearrange("(t p) c -> p t c", p=P)).then_inc(loaded, 16)
                    n += 1
                sp.dma_start(bv[:], w["bv"][None, :].to_broadcast([P, C])).then_inc(loaded, 16)
                n += 1
                if w["bo"] is not None:
                    sp.dma_start(bo[:], w["bo"][None, :].to_broadcast([P, C])).then_inc(loaded, 16)
                    n += 1
                sp.wait_ge(zeroed, 1)
                for g in range(NG):
                    for j in range(HG):
                        h = g * HG + j
                        sp.dma_start(wo[32 * j:32 * j + D, g, :], w["wo"][h * D:(h + 1) * D, :]).then_inc(loaded, 16)
                        n += 1
                sp.wait_ge(loaded, 16 * n)
        ph.clear()

        src_in, ctx_in = ph.sem("src_in"), ph.sem("ctx_in")
        ln_done, var_eps, rstd_done, xn_done = (ph.sem(s) for s in ("ln_done", "var_eps", "rstd_done", "xn_done"))
        tile_mm, tile_act, tile_dve = ph.sem("tile_mm"), ph.sem("tile_act"), ph.sem("tile_dve")
        part_a, part_r, part_b, part_c = (ph.sem(f"part_{s}") for s in "arbc")
        q_packed = [ph.sem(f"q_packed{i}") for i in range(CT)]
        k_packed = [ph.sem(f"k_packed{i}") for i in range(CT)]
        spilled = {(n, c): ph.sem(f"spilled_{n}{c}") for n in "qk" for c in range(CT)}
        s1_mm, s1_max, max_split = ph.sem("s1_mm"), ph.sem("s1_max"), ph.sem("max_split")
        maxT_mm, maxT_out = ph.sem("maxT_mm"), ph.sem("maxT_out")
        s2_mm, exp_done, av_mm, normed = ph.sem("s2_mm"), ph.sem("exp_done"), ph.sem("av_mm"), ph.sem("normed")
        out_mm, out_add, biased = ph.sem("out_mm"), ph.sem("out_add"), ph.sem("biased")

        RING = 6
        tiles = [("xT", c, "dve") for c in range(CT)]
        if not causal:
            tiles += [("cT", j, "act") for j in range((KT + 3) // 4)]
        tiles += [("q", c, "act") for c in range(CT)]
        v_tiles = [("v", j, "dve") for j in range((KT + 1) // 2)]
        k_tiles = [("k", (c, n), "act") for c in range(CT) for n in range(NCH)]
        while k_tiles or v_tiles:
            tiles += k_tiles[:1] + v_tiles[:1]
            k_tiles, v_tiles = k_tiles[1:], v_tiles[1:]
        taken = {"act": tile_act, "dve": tile_dve}

        def nth(i):
            return sum(t[2] == tiles[i][2] for t in tiles[:i + 1])

        where = {(t[0], t[1]): i for i, t in enumerate(tiles)}
        units = [(t[0], t[1]) for t in tiles if t[0] in "qk"]
        unit_no = {u: i for i, u in enumerate(units)}

        def unit_parts(u):
            if u[0] == "q":
                return qparts[:, u[1]], 0, T
            (c, n) = u[1]
            return kparts[:, c], *kchunks[n]

        group_s1 = [(h, qt, ch) for h in range(HG) for qt in range(NT) for ch in range(NCH)]

        def s1_cols(qt, ch):
            return (0, (qt + 1) * P) if causal else kchunks[ch]

        def src(b, t):
            return x_all[:, b, t, :] if src_dram is None else xs[:, t, :]

        with nc.Fori(0, B) as b:
            with nc.Block() as block:
                @block.sync
                def _(sp):
                    if src_dram is not None:
                        sp.dma_start(xs, src_dram[b].rearrange("(t p) c -> p t c", p=P)).then_inc(src_in, 16)
                    if not causal:
                        full = (KT - 1) * P
                        sp.dma_start(ctx_tok[:, 0:KT - 1, :],
                                     ctx_dram[b, 0:full, :].rearrange("(k p) c -> p k c", p=P)).then_inc(ctx_in, 16)
                        sp.dma_start(ctx_tok[0:TC - full, KT - 1, :], ctx_dram[b, full:TC, :]).then_inc(ctx_in, 16)
                    for c in range(CT):
                        for kind, parts, spill, pack, sems, pairs in (
                                ("q", qparts, qspill, qpack, q_packed, QPAIR),
                                ("k", kparts, kspill, kpack, k_packed, KPAIR)):
                            last = ("q", c) if kind == "q" else ("k", (c, NCH - 1))
                            sp.wait_ge(part_a, unit_no[last] + 1)
                            sp.wait_ge(part_c, unit_no[last] + 1)
                            sp.dma_start(spill[c], parts[:, c]).then_inc(spilled[kind, c], 16)
                            sp.wait_ge(spilled[kind, c], 16)
                            for row, part in enumerate(pairs):
                                sp.dma_start(pack[row * D:(row + 1) * D, 8 * c:8 * c + 8, :],
                                             spill[c, :, "abc".index(part), :].rearrange("(h d) n -> d h n", d=D)) \
                                  .then_inc(sems[c], 16)
                    for c in range(CT):
                        sp.wait_ge(q_packed[c], PACKED)
                        sp.wait_ge(k_packed[c], PACKED)

                @block.gpsimd
                def _(pool):
                    pool.wait_ge(ln_done, 2 * NT)
                    nc.gpsimd.tensor_scalar(veps[:], mv[:, :, 1], EPS, None, ALU.add).then_inc(var_eps, 1)
                    pool.wait_ge(var_eps, 1)
                    nc.gpsimd.tensor_tensor(rstd[:], veps[:], k["half"][:, 0:NT], ALU.pow).then_inc(rstd_done, 1)
                    if w["bo"] is not None:
                        pool.wait_ge(xn_done, NT)
                        xb = x_all[:, b, :, :]
                        nc.gpsimd.tensor_tensor(xb, xb, bo[:].unsqueeze(1).to_broadcast([P, NT, C]), ALU.add) \
                          .then_inc(biased, 1)
                    for u, unit in enumerate(units):
                        parts, at, n = unit_parts(unit)
                        pool.wait_ge(part_r, u + 1)
                        nc.gpsimd.tensor_copy(parts[:, 1, at:at + n], rest[:, u % 2, 0:n]).then_inc(part_b, 1)
                        pool.wait_ge(part_b, u + 1)
                        nc.gpsimd.tensor_tensor(parts[:, 2, at:at + n], rest[:, u % 2, 0:n], parts[:, 1, at:at + n],
                                                ALU.subtract).then_inc(part_c, 1)

                @block.scalar
                def _(act):
                    for i, (what, j, who) in enumerate(tiles):
                        if who != "act":
                            continue
                        act.wait_ge(tile_mm, i + 1)
                        bank = ps[:, i % RING, :]
                        if what == "cT":
                            at, n = j * 512, min(512, TC - j * 512)
                            nc.scalar.activation(ctxT[:, at:at + n], bank[:, 0:n], ACT.Copy).then_inc(tile_act, 1)
                            continue
                        u = unit_no[(what, j)]
                        _, _, n = unit_parts((what, j))
                        if u >= 2:
                            act.wait_ge(part_r, u - 1)
                        bias, scale = (bq[:, j:j + 1], 0.25) if what == "q" else (bk[:, j[0]:j[0] + 1], 1.0)
                        nc.scalar.activation(whole[:, u % 2, 0:n], bank[:, 0:n], ACT.Identity, bias=bias,
                                             scale=scale).then_inc(tile_act, 1)
                    for g in range(NG):
                        for j in range(HG):
                            act.wait_ge(maxT_mm, g * HG + j + 1)
                            nc.scalar.activation(qpack[RM:RM + 3, g * HG + j, :], ps[RM:RM + 3, 7, :],
                                                 ACT.Copy).then_inc(maxT_out, 1)
                        for kt, (at, n) in enumerate(ktiles):
                            q0 = at if causal else 0
                            for p in range(2):
                                i = (g * KT + kt) * 2 + p
                                act.wait_ge(s2_mm, i + 1)
                                if i >= 4:
                                    act.wait_ge(av_mm, (i - 4) // 2 + 1)
                                nc.scalar.activation(prob[0:n, i % 4, :, q0:T],
                                                     ps[0:n, 2 + 2 * (i % 2):4 + 2 * (i % 2), q0:T],
                                                     ACT.Exp).then_inc(exp_done, 1)

                @block.vector
                def _(dve):
                    if src_dram is not None:
                        dve.wait_ge(src_in, 16)
                    layernorm_stats(nc, dve, lambda t: src(b, t), stats, mv, ln_done, 0)
                    dve.wait_ge(rstd_done, 1)
                    for t in range(NT):
                        nc.vector.tensor_scalar(xn[:, t], src(b, t), mv[:, t, 0:1], rstd[:, t:t + 1], ALU.subtract,
                                                ALU.mult).then_inc(xn_done, 1)
                    for i, (what, j, who) in enumerate(tiles):
                        bank = ps[:, i % RING, :]
                        if what in "qk":
                            u = unit_no[(what, j)]
                            parts, at, n = unit_parts((what, j))
                            dve.wait_ge(tile_act, nth(i))
                            nc.vector.tensor_copy(parts[:, 0, at:at + n], whole[:, u % 2, 0:n]).then_inc(part_a, 1)
                            dve.wait_ge(part_a, u + 1)
                            if u >= 2:
                                dve.wait_ge(part_c, u - 1)
                            nc.vector.tensor_tensor(rest[:, u % 2, 0:n], whole[:, u % 2, 0:n],
                                                    parts[:, 0, at:at + n], ALU.subtract).then_inc(part_r, 1)
                        if who != "dve":
                            continue
                        dve.wait_ge(tile_mm, i + 1)
                        if what == "xT":
                            nc.vector.tensor_copy(xnT[:, j, :], bank).then_inc(tile_dve, 1)
                        else:
                            for n, kt in enumerate(range(2 * j, min(2 * j + 2, KT))):
                                rows = ktiles[kt][1]
                                ins = nc.vector.tensor_tensor(
                                    vals[0:rows, kt, :, 0:D],
                                    bank[0:rows, n * C:(n + 1) * C].rearrange("p (h d) -> p h d", d=D),
                                    bv[0:rows, :].rearrange("p (h d) -> p h d", d=D), ALU.add)
                            ins.then_inc(tile_dve, 1)

                    def maxima(g):
                        for i, (h, qt, ch) in enumerate(group_s1):
                            n = g * n_s1 + i
                            cols = s1_cols(qt, ch)[1]
                            dve.wait_ge(s1_mm, n + 1)
                            nc.vector.tensor_reduce(mx[:, h * NT + qt, ch:ch + 1], ps[:, n % 2, 0:cols], AX_X,
                                                    ALU.max).then_inc(s1_max, 1)
                        dve.wait_ge(s1_max, (g + 1) * n_s1)
                        nc.vector.tensor_reduce(mxc[:], mx[:], AX_X, ALU.max).then_inc(max_split, 1)
                        dve.wait_ge(max_split, 5 * g + 1)
                        if g:
                            dve.wait_ge(maxT_mm, g * HG)
                        nc.vector.tensor_scalar(m3[:, :, 0], mxc[:], -1.0, None, ALU.mult).then_inc(max_split, 1)
                        dve.wait_ge(max_split, 5 * g + 2)
                        nc.vector.scalar_tensor_tensor(out=mrest[:], in0=mxc[:], scalar=-1.0, in1=m3[:, :, 0],
                                                       op0=ALU.mult, op1=ALU.subtract).then_inc(max_split, 1)
                        dve.wait_ge(max_split, 5 * g + 3)
                        nc.vector.tensor_copy(m3[:, :, 1], mrest[:]).then_inc(max_split, 1)
                        dve.wait_ge(max_split, 5 * g + 4)
                        nc.vector.tensor_tensor(m3[:, :, 2], mrest[:], m3[:, :, 1], ALU.subtract) \
                          .then_inc(max_split, 1)

                    def normalise(g):
                        dve.wait_ge(av_mm, (g + 1) * KT)
                        nc.vector.stream_shuffle(den, ps[:, 6, :], [16 + i % 16 for i in range(32)]) \
                          .then_inc(normed, 1)
                        dve.wait_ge(normed, 3 * g + 1)
                        nc.vector.reciprocal(rden, den).then_inc(normed, 1)
                        dve.wait_ge(normed, 3 * g + 2)
                        nc.vector.tensor_tensor(y[:, g, :], ps[:, 6, :], rden, ALU.mult).then_inc(normed, 1)

                    maxima(0)
                    for g in range(NG):
                        if g + 1 < NG:
                            maxima(g + 1)
                        normalise(g)
                    if w["bo"] is not None:
                        dve.wait_ge(biased, 1)
                    for j in range(NT // 2):
                        dve.wait_ge(out_mm, j + 1)
                        xb = x_all[:, b, 2 * j:2 * j + 2, :]
                        nc.vector.tensor_tensor(xb, ps[:, j, :].rearrange("p (t c) -> p t c", c=C), xb, ALU.add) \
                          .then_inc(out_add, 1)

                @block.tensor
                def _(pe):
                    for i, (what, j, who) in enumerate(tiles):
                        bank = ps[:, i % RING, :]
                        if i >= RING:
                            pe.wait_ge(taken[tiles[i - RING][2]], nth(i - RING))
                        if what == "xT":
                            pe.wait_ge(xn_done, NT)
                            for t in range(NT):
                                ins = nc.tensor.transpose(bank[:, t * P:(t + 1) * P], xn[:, t, j * P:(j + 1) * P],
                                                          k["ident"][:])
                        elif what == "cT":
                            pe.wait_ge(ctx_in, 32)
                            for kt in range(4 * j, min(4 * j + 4, KT)):
                                n = ktiles[kt][1]
                                ins = nc.tensor.transpose(bank[:, (kt % 4) * P:(kt % 4) * P + n],
                                                          ctx_tok[0:n, kt, :], k["ident"][0:n, 0:n])
                        elif what == "q":
                            pe.wait_ge(tile_dve, nth(where[("xT", CT - 1)]))
                            for c in range(CT):
                                ins = nc.tensor.matmul(bank, wq[:, c, j * P:(j + 1) * P], xnT[:, c, :],
                                                       start=(c == 0), stop=(c == CT - 1))
                        else:
                            kv = xnT if causal else ctxT[:].unsqueeze(1)
                            if not causal:
                                pe.wait_ge(tile_act, nth(where[("cT", (KT + 3) // 4 - 1)]))
                            if what == "k":
                                half, (at, n) = j[0], kchunks[j[1]]
                                for c in range(kvc):
                                    ins = nc.tensor.matmul(bank[:, 0:n], wk[:, c, half * P:(half + 1) * P],
                                                           kv[:, c, at:at + n], start=(c == 0), stop=(c == kvc - 1))
                            else:
                                for m, kt in enumerate(range(2 * j, min(2 * j + 2, KT))):
                                    at, n = ktiles[kt]
                                    for c in range(kvc):
                                        ins = nc.tensor.matmul(bank[0:n, m * C:(m + 1) * C], kv[:, c, at:at + n],
                                                               wv[:, c, :], start=(c == 0), stop=(c == kvc - 1))
                        ins.then_inc(tile_mm, 1)

                    def score_max(g, i):
                        h, qt, ch = group_s1[i]
                        n = g * n_s1 + i
                        at, cols = s1_cols(qt, ch)
                        if n >= 2:
                            pe.wait_ge(s1_max, n - 1)
                        hh = g * HG + h
                        ins = nc.tensor.matmul(ps[:, n % 2, 0:cols], qpack[0:RM, hh, qt * P:(qt + 1) * P],
                                               kpack[0:RM, hh, at:at + cols], start=True, stop=not causal)
                        if causal:
                            ins = nc.tensor.matmul(ps[:, n % 2, cols - P:cols], k["identb"][:],
                                                   k["k_from_q"][:, P:2 * P], start=False, stop=True)
                        ins.then_inc(s1_mm, 1)

                    def turn_maxima(g):
                        pe.wait_ge(max_split, 5 * (g + 1))
                        for j in range(HG):
                            n = g * HG + j
                            if n:
                                pe.wait_ge(maxT_out, n)
                            for qt in range(NT):
                                ins = nc.tensor.matmul(ps[RM:RM + 3, 7, qt * P:(qt + 1) * P],
                                                       m3[:, j * NT + qt, :], k["identb"][:], start=True, stop=True)
                            ins.then_inc(maxT_mm, 1)

                    def score(g, kt, p):
                        i = (g * KT + kt) * 2 + p
                        at, n = ktiles[kt]
                        q0 = at if causal else 0
                        if i >= 2:
                            pe.wait_ge(exp_done, i - 1)
                        for m in range(2):
                            hh = g * HG + 2 * p + m
                            out = ps[0:n, 2 + 2 * (i % 2) + m, :]
                            ins = nc.tensor.matmul(out[:, q0:T], kpack[0:KROWS, hh, at:at + n],
                                                   qpack[0:KROWS, hh, q0:T], start=True, stop=not causal)
                            if causal:
                                ins = nc.tensor.matmul(out[:, q0:q0 + P], k["identb"][:], k["q_from_k"][:],
                                                       start=False, stop=True)
                        ins.then_inc(s2_mm, 1)

                    def weigh(g, kt):
                        at, n = ktiles[kt]
                        q0 = at if causal else 0
                        pe.wait_ge(exp_done, 2 * (g * KT + kt) + 2)
                        if kt == 0 and g:
                            pe.wait_ge(normed, 3 * g)
                        for j in range(HG):
                            i = (g * KT + kt) * 2 + j // 2
                            ins = nc.tensor.matmul(ps[32 * j:32 * j + 32, 6, q0:T], vals[0:n, kt, g * HG + j, :],
                                                   prob[0:n, i % 4, j % 2, q0:T], start=(kt == 0),
                                                   stop=(kt == KT - 1), skip_group_check=True)
                        ins.then_inc(av_mm, 1)

                    def packed(g):
                        pe.wait_ge(q_packed[g * HG // 8], PACKED)
                        pe.wait_ge(k_packed[g * HG // 8], PACKED)

                    last = tiles[-RING:]
                    for i in range(len(tiles) - RING, len(tiles)):
                        pe.wait_ge(taken[tiles[i][2]], nth(i))
                    packed(0)
                    for i in range(n_s1):
                        score_max(0, i)
                    for g in range(NG):
                        turn_maxima(g)
                        if g + 1 < NG:
                            packed(g + 1)
                        pe.wait_ge(maxT_out, HG * (g + 1))
                        for kt in range(KT):
                            score(g, kt, 0)
                            score(g, kt, 1)
                            if kt:
                                weigh(g, kt - 1)
                            if g + 1 < NG:
                                for i in range(kt * n_s1 // KT, (kt + 1) * n_s1 // KT):
                                    score_max(g + 1, i)
                        weigh(g, KT - 1)
                    pe.wait_ge(normed, 3 * NG)
                    pe.wait_ge(s1_max, NG * n_s1)
                    for t in range(NT):
                        for g in range(NG):
                            ins = nc.tensor.matmul(ps[:, t // 2, (t % 2) * C:(t % 2 + 1) * C],
                                                   y[:, g, t * P:(t + 1) * P], wo[:, g, :],
                                                   start=(g == 0), stop=(g == NG - 1))
                        if t % 2:
                            ins.then_inc(out_mm, 1)
            ph.clear()



L = 2
LH, LD = 8, 64
INNER = LH * LD
HP = LH // 2
HID = int(C * 4 * 2 / 3)
FT = -(-HID // P)
FR = HID - (FT - 1) * P
WINDOW = P
QK_SCALE = 8.0


def rotary_tables():
    half = np.arange(0, LD, 2, dtype=np.float32)
    inv_freq = (1.0 / np.float32(10000.0) ** (half / np.float32(LD))).astype(np.float32)
    t = np.arange(T, dtype=np.float32)
    freqs = t[:, None] * inv_freq[None, :]
    base = (half + np.float32(0.4 * LD)) / np.float32(1.4 * LD)
    power = (t - T // 2) / np.float32(WINDOW // 2)
    scale = base[None, :] ** power[:, None]
    out = np.empty((2, 2, T, LD), np.float32)
    for i, s in enumerate((scale * np.float32(QK_SCALE), np.float32(1) / scale)):
        cos, sin = np.cos(freqs) * s, np.sin(freqs) * s
        out[i, 0] = np.concatenate([cos, cos], -1)
        out[i, 1] = np.concatenate([-sin, sin], -1)
    return out


def constants():
    return {"rotary": rotary_tables()}


def local_layers(nc, k, x_all, a):
    with Phase(nc, "local") as ph:
        z_all = ph.sb("z_all", [P, B, NT, C])
        wqkv, wo = ph.sb("wqkv", [P, CT, 3 * INNER]), ph.sb("wo", [P, HP, C])
        w1, w2 = ph.sb("w1", [P, CT, 2 * HID]), ph.sb("w2", [P, FT, C])
        b1, b2 = ph.sb("b1", [P, 2, FT]), ph.sb("b2", [P, C])
        ln_g, ln_b = ph.sb("ln_g", [P, CT]), ph.sb("ln_b", [P, CT])
        raw, rot = ph.sb("raw", [P, 2, 2, NT, LD]), ph.sb("rot", [P, 2, 2, NT, LD])
        head_scale = ph.sb("head_scale", [P, 2, LD])
        zt, hT = ph.sb("zt", [P, NT, C]), ph.sb("hT", [P, CT, T])
        sq, by_cos, by_sin = ph.sb("sq", [P, 2, INNER]), ph.sb("by_cos", [P, 2, INNER]), ph.sb("by_sin", [P, 2, INNER])
        ss, ssc, rnorm = (ph.sb(n, [P, 2 * NT, LH]) for n in ("ss", "ssc", "rnorm"))
        qk = ph.sb("qk", [P, 2 * NT, INNER])
        qT, kz = ph.sb("qT", [P, HP, T]), ph.sb("kz", [P, LH, T])
        vt = ph.sb("vt", [P, NT, INNER])
        mxs, nmx = ph.sb("mxs", [P, 2, 4]), ph.sb("nmx", [P, 2, 4])
        sums, rsums = ph.sb("sums", [P, 2, 4]), ph.sb("rsums", [P, 2, 4])
        prob, probT = ph.sb("prob", [P, 2, 4, 2 * P]), ph.sb("probT", [P, 2, 4, 2 * P])
        oT = ph.sb("oT", [P, HP, T])
        shifted, hn, hnT = ph.sb("shifted", [P, NT, P]), ph.sb("hn", [P, NT, C]), ph.sb("hnT", [P, CT, T])
        stats, mv, rstd = ph.sb("stats", [P, NT, 2, 6]), ph.sb("mv", [P, NT, 2]), ph.sb("rstd", [P, NT])
        veps = ph.sb("veps", [P, NT])
        gel, hid = ph.sb("gel", [P, 2, T]), ph.sb("hid", [P, FT, T])
        ps = ph.ps("ps", [P, 8, 512])

        tables = ph.sem("tables")
        ln_done, var_eps, rstd_done = ph.sem("ln_done"), ph.sem("var_eps"), ph.sem("rstd_done")
        with nc.Block() as block:
            @block.gpsimd
            def _(pool):
                nc.gpsimd.memset(kz[:], 0.0)
                nc.gpsimd.memset(w2[:, FT - 1, :], 0.0)

            @block.vector
            def _(dve):
                nc.vector.memset(hid[:, FT - 1, :], 0.0)
                nc.vector.memset(hT[:, 1, 0:1], 0.0)
                nc.vector.memset(shifted[0:1, 0, :], 0.0)

            @block.sync
            def _(sp):
                sp.dma_start(raw[:].rearrange("p a b t d -> p (a b) t d"),
                             a["rotary"].rearrange("a b (t p) d -> p (a b) t d", p=P)).then_inc(tables, 16)
                sp.wait_ge(tables, 16)
        with nc.Fori(0, B) as b:
            with nc.Block() as block:
                @block.vector
                def _(dve):
                    for t in range(NT):
                        nc.vector.bn_stats(stats[:, t, 0], x_all[:, b, t, :]).then_inc(ln_done, 1)
                    for t in range(NT):
                        dve.wait_ge(ln_done, t + 1)
                        nc.vector.bn_aggr(mv[:, t], stats[:, t, 0]).then_inc(ln_done, 1)
                    dve.wait_ge(rstd_done, 1)
                    for t in range(NT):
                        nc.vector.tensor_scalar(z_all[:, b, t, :], x_all[:, b, t, :], mv[:, t, 0:1],
                                                rstd[:, t:t + 1], ALU.subtract, ALU.mult)

                @block.gpsimd
                def _(pool):
                    pool.wait_ge(ln_done, 2 * NT)
                    nc.gpsimd.tensor_scalar(veps[:], mv[:, :, 1], EPS, None, ALU.add).then_inc(var_eps, 1)
                    pool.wait_ge(var_eps, 1)
                    nc.gpsimd.tensor_tensor(rstd[:], veps[:], k["half"][:, 0:NT], ALU.pow).then_inc(rstd_done, 1)
            ph.clear()

        loaded, scales, scaled = ph.sem("loaded"), ph.sem("scales"), ph.sem("scaled")
        copied, tile_mm, tile_act, tile_dve = (ph.sem(n) for n in ("copied", "tile_mm", "tile_act", "tile_dve"))
        squared, ss_sum, ss_ok, rotated = (ph.sem(n) for n in ("squared", "ss_sum", "ss_ok", "rotated"))
        rot_sum, norm_ok, qk_ready = (ph.sem(n) for n in ("rot_sum", "norm_ok", "qk_ready"))
        s_mm, maxed, exp_done, summed = (ph.sem(n) for n in ("s_mm", "maxed", "exp_done", "summed"))
        p_ready, pT_mm, pT_act, pT_dve = (ph.sem(n) for n in ("p_ready", "pT_mm", "pT_act", "pT_dve"))
        o_mm, o_out, wo_mm, z_attn = (ph.sem(n) for n in ("o_mm", "o_out", "wo_mm", "z_attn"))
        shift_in, hn_done, hnT_mm, hnT_out = (ph.sem(n) for n in ("shift_in", "hn_done", "hnT_mm", "hnT_out"))
        up_mm, gel_done, hid_done, down_mm = (ph.sem(n) for n in ("up_mm", "gel_done", "hid_done", "down_mm"))
        biased = ph.sem("biased")

        RING = 8
        tiles = [("zT", c, "dve") for c in range(CT)]
        for t in range(NT + 1):
            if t < NT:
                tiles += [("q", t, "dve"), ("k", t, "dve"), ("v", t, "act")]
            if t:
                tiles += [("qT", t - 1, "act"), ("kT", t - 1, "act")]
        taken = {"act": tile_act, "dve": tile_dve}

        def nth(i):
            return sum(t[2] == tiles[i][2] for t in tiles[:i + 1])

        steps = [(w, hg) for w in range(NT) for hg in range(LH // 4)]

        with nc.Fori(0, L) as l:
            with nc.Block() as block:
                @block.sync
                def _(sp):
                    with nc.allow_non_contiguous_dma(reason="small columns"):
                        sp.dma_start(head_scale[:, 0, :], a["L0_ffn_q_scale"][l][None, :].to_broadcast([P, LD])) \
                          .then_inc(scales, 16)
                        sp.dma_start(head_scale[:, 1, :], a["L0_ffn_k_scale"][l][None, :].to_broadcast([P, LD])) \
                          .then_inc(scales, 16)
                        parts = [
                            (wqkv[:], a["L0_ffn_wqkv"][l].rearrange("(t p) n -> p t n", p=P)),
                            (wo[:], a["L0_ffn_wo"][l].rearrange("(t p) n -> p t n", p=P)),
                            (w1[:], a["L0_ffn_w1"][l].rearrange("(t p) n -> p t n", p=P)),
                            (w2[:, 0:FT - 1, :],
                             a["L0_ffn_w2"][l, 0:(FT - 1) * P, :].rearrange("(t p) n -> p t n", p=P)),
                            (w2[0:FR, FT - 1, :], a["L0_ffn_w2"][l, (FT - 1) * P:HID, :]),
                            (b2[:], a["L0_ffn_b2"][l][None, :].to_broadcast([P, C])),
                            (ln_g[:], a["L0_ffn_ln_g"][l].rearrange("(t p) -> p t", p=P)),
                            (ln_b[:], a["L0_ffn_ln_b"][l].rearrange("(t p) -> p t", p=P)),
                        ]
                        for i in range(2):
                            col = a["L0_ffn_b1"][l, i * HID:(i + 1) * HID]
                            parts += [(b1[:, i, 0:FT - 1], col[0:(FT - 1) * P].rearrange("(t p) -> p t", p=P)),
                                      (b1[0:FR, i, FT - 1:FT], col[(FT - 1) * P:HID][:, None])]
                        for dst, src in parts:
                            sp.dma_start(dst, src).then_inc(loaded, 16)
                        sp.wait_ge(loaded, 16 * len(parts))

                @block.vector
                def _(dve):
                    dve.wait_ge(scales, 32)
                    for i in range(2):
                        hs = head_scale[:, i, :]
                        nc.vector.tensor_tensor(rot[:, i, 0], raw[:, i, 0],
                                                hs.unsqueeze(1).to_broadcast([P, NT, LD]), ALU.mult)
                        for lo, other in ((0, LD // 2), (LD // 2, 0)):
                            nc.vector.tensor_tensor(
                                rot[:, i, 1, :, lo:lo + LD // 2], raw[:, i, 1, :, lo:lo + LD // 2],
                                hs[:, other:other + LD // 2].unsqueeze(1).to_broadcast([P, NT, LD // 2]), ALU.mult)
            ph.clear()
            with nc.Fori(0, B) as b:
                with nc.Block() as block:
                    @block.sync
                    def _(sp):
                        sp.wait_ge(z_attn, 2)
                        sp.dma_start(shifted[1:P, :, :], zt[0:P - 1, :, P:C]).then_inc(shift_in, 16)
                        sp.dma_start(shifted[0:1, 1:NT, :], zt[P - 1:P, 0:NT - 1, P:C]).then_inc(shift_in, 16)
                        sp.wait_ge(shift_in, 32)

                    @block.gpsimd
                    def _(pool):
                        for u in range(2 * NT):
                            pool.wait_ge(rotated, u + 1)
                            nc.gpsimd.tensor_tensor(by_cos[:, u % 2], by_cos[:, u % 2], by_sin[:, u % 2], ALU.add) \
                              .then_inc(rot_sum, 1)
                            pool.wait_ge(ss_ok, u + 1)
                            nc.gpsimd.tensor_tensor(rnorm[:, u], ssc[:, u], k["half"][:, 0:LH], ALU.pow) \
                              .then_inc(norm_ok, 1)
                            pool.wait_ge(rot_sum, u + 1)
                            pool.wait_ge(norm_ok, u + 1)
                            nc.gpsimd.tensor_tensor(
                                qk[:, u].rearrange("p (h d) -> p h d", d=LD),
                                by_cos[:, u % 2].rearrange("p (h d) -> p h d", d=LD),
                                rnorm[:, u].unsqueeze(2).to_broadcast([P, LH, LD]), ALU.mult).then_inc(qk_ready, 1)
                        for s, (w, hg) in enumerate(steps):
                            c0 = 0 if w else P
                            pool.wait_ge(summed, s + 1)
                            pr = prob[:, s % 2, :, c0:2 * P]
                            nc.gpsimd.tensor_tensor(pr, pr, rsums[:, s % 2].unsqueeze(2).to_broadcast(
                                [P, 4, 2 * P - c0]), ALU.mult).then_inc(p_ready, 1)
                        pool.wait_ge(ln_done, 3 * NT)
                        nc.gpsimd.tensor_scalar(veps[:], mv[:, :, 1], EPS, None, ALU.add).then_inc(var_eps, 1)
                        pool.wait_ge(var_eps, 1)
                        nc.gpsimd.tensor_tensor(rstd[:], veps[:], k["half"][:, 0:NT], ALU.pow).then_inc(rstd_done, 1)
                        pool.wait_ge(hn_done, 1)
                        pool.wait_ge(shift_in, 32)
                        nc.gpsimd.tensor_tensor(zt[:], zt[:], b2[:].unsqueeze(1).to_broadcast([P, NT, C]), ALU.add) \
                          .then_inc(biased, 1)

                    @block.scalar
                    def _(act):
                        u = 0
                        for i, (what, t, who) in enumerate(tiles):
                            bank = ps[:, i % RING, :]
                            if what in ("q", "k"):
                                act.wait_ge(tile_mm, i + 1)
                                if u >= 2:
                                    act.wait_ge(ss_sum, u - 1)
                                nc.scalar.activation(sq[:, u % 2], bank, ACT.Square).then_inc(squared, 1)
                                u += 1
                            if who != "act":
                                continue
                            act.wait_ge(tile_mm, i + 1)
                            cols = slice(t * P, (t + 1) * P)
                            heads = bank.rearrange("p (h q) -> p h q", q=P)
                            if what == "v":
                                ins = nc.scalar.activation(vt[:, t], bank, ACT.Copy)
                            elif what == "qT":
                                ins = nc.scalar.activation(qT[:, :, cols], heads, ACT.Copy)
                            else:
                                kzp = kz[:].rearrange("p (h two) t -> p h two t", two=2)
                                nc.scalar.activation(kzp[0:LD, :, 0, cols], heads[0:LD], ACT.Copy)
                                ins = nc.scalar.activation(kzp[LD:P, :, 1, cols], heads[LD:P], ACT.Copy)
                            ins.then_inc(tile_act, 1)

                        def exps(s):
                            c0 = 0 if steps[s][0] else P
                            act.wait_ge(maxed, 2 * s + 2)
                            if s >= 2:
                                act.wait_ge(pT_mm, s - 1)
                            for m in range(4):
                                bank = ps[:, 2 * (s % 2) + m // 2, (m % 2) * 2 * P + c0:(m % 2 + 1) * 2 * P]
                                ins = nc.scalar.activation(prob[:, s % 2, m, c0:2 * P], bank, ACT.Exp,
                                                           bias=nmx[:, s % 2, m:m + 1],
                                                           accum_out=sums[:, s % 2, m:m + 1])
                            ins.then_inc(exp_done, 1)

                        def take_probT(s):
                            c0 = 0 if steps[s][0] else P
                            act.wait_ge(pT_mm, s + 1)
                            if s >= 2:
                                act.wait_ge(o_mm, s - 1)
                            nc.scalar.activation(
                                probT[:, s % 2, 0:2, c0:2 * P],
                                ps[:, 4, :].rearrange("p (m c) -> p m c", c=2 * P)[:, :, c0:2 * P],
                                ACT.Copy).then_inc(pT_act, 1)

                        exps(0)
                        for s in range(len(steps)):
                            if s + 1 < len(steps):
                                exps(s + 1)
                            take_probT(s)
                        for f in range(FT):
                            rows = P if f < FT - 1 else FR
                            act.wait_ge(up_mm, 2 * f + 1)
                            if f >= 2:
                                act.wait_ge(hid_done, f - 1)
                            nc.scalar.activation(gel[0:rows, f % 2, :], ps[0:rows, 4 + (2 * f) % 4, :], ACT.Gelu,
                                                 bias=b1[0:rows, 1, f:f + 1]).then_inc(gel_done, 1)

                    @block.vector
                    def _(dve):
                        nc.vector.tensor_copy(zt[:], z_all[:, b]).then_inc(copied, 1)
                        u = 0
                        for i, (what, t, who) in enumerate(tiles):
                            if who != "dve":
                                continue
                            bank = ps[:, i % RING, :]
                            dve.wait_ge(tile_mm, i + 1)
                            if what == "zT":
                                if t == 0:
                                    ins = nc.vector.tensor_copy(hT[:, 0, :], bank)
                                else:
                                    ins = nc.vector.tensor_copy(hT[:, 1, 1:T], bank[:, 0:T - 1])
                                ins.then_inc(tile_dve, 1)
                                continue
                            i2 = 0 if what == "q" else 1
                            dve.wait_ge(squared, u + 1)
                            nc.vector.tensor_reduce(ss[:, u], sq[:, u % 2].rearrange("p (h d) -> p h d", d=LD), AX_X,
                                                    ALU.add).then_inc(ss_sum, 1)
                            if u >= 2:
                                dve.wait_ge(qk_ready, u - 1)
                            heads = bank.rearrange("p (h d) -> p h d", d=LD)
                            bc = by_cos[:, u % 2].rearrange("p (h d) -> p h d", d=LD)
                            bs = by_sin[:, u % 2].rearrange("p (h d) -> p h d", d=LD)
                            cos, sin = rot[:, i2, 0, t, :], rot[:, i2, 1, t, :]
                            nc.vector.tensor_tensor(bc, heads, cos.unsqueeze(1).to_broadcast([P, LH, LD]), ALU.mult)
                            for lo, other in ((0, LD // 2), (LD // 2, 0)):
                                ins = nc.vector.tensor_tensor(
                                    bs[:, :, lo:lo + LD // 2], heads[:, :, other:other + LD // 2],
                                    sin[:, lo:lo + LD // 2].unsqueeze(1).to_broadcast([P, LH, LD // 2]), ALU.mult)
                            ins.then_inc(rotated, 1)
                            dve.wait_ge(ss_sum, u + 1)
                            nc.vector.tensor_scalar(ssc[:, u], ss[:, u], 1e-24, None, ALU.max).then_inc(ss_ok, 1)
                            u += 1

                        def maxima(s):
                            c0 = 0 if steps[s][0] else P
                            dve.wait_ge(s_mm, s + 1)
                            nc.vector.tensor_reduce(
                                mxs[:, s % 2], ps[:, 2 * (s % 2):2 * (s % 2) + 2, :].rearrange(
                                    "p a (m c) -> p (a m) c", c=2 * P)[:, :, c0:2 * P], AX_X, ALU.max) \
                              .then_inc(maxed, 1)
                            dve.wait_ge(maxed, 2 * s + 1)
                            if s >= 2:
                                dve.wait_ge(exp_done, s - 1)
                            nc.vector.tensor_scalar(nmx[:, s % 2], mxs[:, s % 2], -1.0, None, ALU.mult) \
                              .then_inc(maxed, 1)

                        maxima(0)
                        for s, (w, hg) in enumerate(steps):
                            c0 = 0 if w else P
                            dve.wait_ge(exp_done, s + 1)
                            if s >= 2:
                                dve.wait_ge(p_ready, s - 1)
                            nc.vector.reciprocal(rsums[:, s % 2], sums[:, s % 2]).then_inc(summed, 1)
                            if s + 1 < len(steps):
                                maxima(s + 1)
                            dve.wait_ge(pT_mm, s + 1)
                            if s >= 2:
                                dve.wait_ge(o_mm, s - 1)
                            nc.vector.tensor_copy(
                                probT[:, s % 2, 2:4, c0:2 * P],
                                ps[:, 5, :].rearrange("p (m c) -> p m c", c=2 * P)[:, :, c0:2 * P]) \
                              .then_inc(pT_dve, 1)
                            dve.wait_ge(o_mm, s + 1)
                            nc.vector.tensor_copy(oT[:, 2 * hg:2 * hg + 2, w * P:(w + 1) * P],
                                                  ps[:, 6 + s % 2, 0:2 * P].rearrange("p (h q) -> p h q", q=P)) \
                              .then_inc(o_out, 1)
                        for j in range(NT // 2):
                            dve.wait_ge(wo_mm, j + 1)
                            zz = zt[:, 2 * j:2 * j + 2, :]
                            nc.vector.tensor_tensor(zz, ps[:, j, :].rearrange("p (t c) -> p t c", c=C), zz, ALU.add) \
                              .then_inc(z_attn, 1)
                        dve.wait_ge(z_attn, 2)
                        for t in range(NT):
                            nc.vector.bn_stats(stats[:, t, 0], zt[:, t, 0:P]).then_inc(ln_done, 1)
                        dve.wait_ge(shift_in, 32)
                        for t in range(NT):
                            nc.vector.bn_stats(stats[:, t, 1], shifted[:, t]).then_inc(ln_done, 1)
                        for t in range(NT):
                            dve.wait_ge(ln_done, NT + t + 1)
                            nc.vector.bn_aggr(mv[:, t], stats[:, t]).then_inc(ln_done, 1)
                        dve.wait_ge(rstd_done, 1)
                        for t in range(NT):
                            for dst, src in ((hn[:, t, 0:P], zt[:, t, 0:P]), (hn[:, t, P:C], shifted[:, t])):
                                ins = nc.vector.tensor_scalar(dst, src, mv[:, t, 0:1], rstd[:, t:t + 1],
                                                              ALU.subtract, ALU.mult)
                        ins.then_inc(hn_done, 1)
                        for c in range(CT):
                            dve.wait_ge(hnT_mm, c + 1)
                            nc.vector.tensor_scalar(hnT[:, c, :], ps[:, 2 + c, :], ln_g[:, c:c + 1], ln_b[:, c:c + 1],
                                                    ALU.mult, ALU.add).then_inc(hnT_out, 1)
                        for f in range(FT):
                            rows = P if f < FT - 1 else FR
                            dve.wait_ge(up_mm, 2 * f + 2)
                            dve.wait_ge(gel_done, f + 1)
                            nc.vector.scalar_tensor_tensor(
                                out=hid[0:rows, f, :], in0=ps[0:rows, 4 + (2 * f + 1) % 4, :],
                                scalar=b1[0:rows, 0, f:f + 1], in1=gel[0:rows, f % 2, :], op0=ALU.add, op1=ALU.mult) \
                              .then_inc(hid_done, 1)
                        dve.wait_ge(biased, 1)
                        for j in range(NT // 2):
                            dve.wait_ge(down_mm, j + 1)
                            nc.vector.tensor_tensor(z_all[:, b, 2 * j:2 * j + 2, :],
                                                    ps[:, j, :].rearrange("p (t c) -> p t c", c=C),
                                                    zt[:, 2 * j:2 * j + 2, :], ALU.add)

                    @block.tensor
                    def _(pe):
                        for i, (what, t, who) in enumerate(tiles):
                            bank = ps[:, i % RING, :]
                            if i >= RING:
                                last = tiles[i - RING]
                                if last[0] in ("q", "k"):
                                    pe.wait_ge(rotated, 2 * last[1] + (last[0] == "k") + 1)
                                else:
                                    pe.wait_ge(taken[last[2]], nth(i - RING) if last[2] == "act" else last[1] + 1)
                            if what == "zT":
                                pe.wait_ge(copied, 1)
                                for n in range(NT):
                                    ins = nc.tensor.transpose(bank[:, n * P:(n + 1) * P], zt[:, n, t * P:(t + 1) * P],
                                                              k["ident"][:])
                            elif what in ("qT", "kT"):
                                u = 2 * t + (what == "kT")
                                pe.wait_ge(qk_ready, u + 1)
                                for n in range(HP):
                                    ins = nc.tensor.transpose(bank[:, n * P:(n + 1) * P],
                                                              qk[:, u, n * P:(n + 1) * P], k["ident"][:])
                            else:
                                pe.wait_ge(tile_dve, CT)
                                part = "qkv".index(what)
                                for c in range(CT):
                                    ins = nc.tensor.matmul(bank, hT[:, c, t * P:(t + 1) * P],
                                                           wqkv[:, c, part * INNER:(part + 1) * INNER],
                                                           start=(c == 0), stop=(c == CT - 1))
                            ins.then_inc(tile_mm, 1)

                        def score(s):
                            w, hg = steps[s]
                            c0 = 0 if w else P
                            if s >= 2:
                                pe.wait_ge(exp_done, s - 1)
                            for m in range(4):
                                h = 4 * hg + m
                                out = ps[:, 2 * (s % 2) + m // 2, (m % 2) * 2 * P + c0:(m % 2 + 1) * 2 * P]
                                nc.tensor.matmul(out, qT[:, h // 2, w * P:(w + 1) * P],
                                                 kz[:, h, (w - 1) * P + c0:(w + 1) * P], start=True, stop=False)
                                ins = nc.tensor.matmul(out, k["identb"][:], k["k_from_q"][:, c0:2 * P],
                                                       start=False, stop=True)
                            ins.then_inc(s_mm, 1)

                        def turn(s):
                            pe.wait_ge(p_ready, s + 1)
                            if s:
                                pe.wait_ge(pT_act, s)
                                pe.wait_ge(pT_dve, s)
                            for m in range(4):
                                for kb in range(0 if steps[s][0] else 1, 2):
                                    ins = nc.tensor.transpose(
                                        ps[:, 4 + m // 2, (m % 2) * 2 * P + kb * P:(m % 2) * 2 * P + (kb + 1) * P],
                                        prob[:, s % 2, m, kb * P:(kb + 1) * P], k["ident"][:])
                            ins.then_inc(pT_mm, 1)

                        def weigh(s):
                            w, hg = steps[s]
                            pe.wait_ge(pT_act, s + 1)
                            pe.wait_ge(pT_dve, s + 1)
                            if s >= 2:
                                pe.wait_ge(o_out, s - 1)
                            first = 0 if w else 1
                            for pair in range(2):
                                for kb in range(first, 2):
                                    for m in (2 * pair, 2 * pair + 1):
                                        h = 4 * hg + m
                                        ins = nc.tensor.matmul(
                                            ps[LD * (m % 2):LD * (m % 2) + LD, 6 + s % 2, pair * P:(pair + 1) * P],
                                            vt[:, w - 1 + kb, h * LD:(h + 1) * LD],
                                            probT[:, s % 2, m, kb * P:(kb + 1) * P],
                                            start=(kb == first), stop=(kb == 1), skip_group_check=True)
                            ins.then_inc(o_mm, 1)

                        pe.wait_ge(tile_act, nth(len(tiles) - 1))
                        pe.wait_ge(rotated, 2 * NT)
                        score(0)
                        score(1)
                        for s in range(len(steps)):
                            turn(s)
                            if s + 2 < len(steps):
                                score(s + 2)
                            weigh(s)
                        pe.wait_ge(o_out, len(steps))
                        for t in range(NT):
                            for n in range(HP):
                                ins = nc.tensor.matmul(ps[:, t // 2, (t % 2) * C:(t % 2 + 1) * C],
                                                       oT[:, n, t * P:(t + 1) * P], wo[:, n, :],
                                                       start=(n == 0), stop=(n == HP - 1))
                            if t % 2:
                                ins.then_inc(wo_mm, 1)
                        pe.wait_ge(hn_done, 1)
                        for c in range(CT):
                            for n in range(NT):
                                ins = nc.tensor.transpose(ps[:, 2 + c, n * P:(n + 1) * P],
                                                          hn[:, n, c * P:(c + 1) * P], k["ident"][:])
                            ins.then_inc(hnT_mm, 1)
                        pe.wait_ge(hnT_out, CT)
                        for i in range(2 * FT):
                            f, part = i // 2, 1 - i % 2
                            rows = P if f < FT - 1 else FR
                            if f >= 2:
                                pe.wait_ge(hid_done, f - 1)
                            at = part * HID + f * P
                            for c in range(CT):
                                ins = nc.tensor.matmul(ps[0:rows, 4 + i % 4, :], w1[:, c, at:at + rows], hnT[:, c, :],
                                                       start=(c == 0), stop=(c == CT - 1))
                            ins.then_inc(up_mm, 1)
                        pe.wait_ge(hid_done, FT)
                        for t in range(NT):
                            for f in range(FT):
                                ins = nc.tensor.matmul(ps[:, t // 2, (t % 2) * C:(t % 2 + 1) * C],
                                                       hid[:, f, t * P:(t + 1) * P], w2[:, f, :],
                                                       start=(f == 0), stop=(f == FT - 1))
                            if t % 2:
                                ins.then_inc(down_mm, 1)
                ph.clear()
        with nc.Block() as block:
            @block.vector
            def _(dve):
                for b in range(B):
                    nc.vector.tensor_tensor(x_all[:, b], x_all[:, b], z_all[:, b], ALU.add)



E = 8
CAP = max(1, int(T / E * 1.25))
HE = 1024
ET = HE // P
EH = E // 2
OFF = 1000.0


def experts(nc, k, x_all, a, out):
    with Phase(nc, "moe") as ph:
        slot_in = ph.sb("slot_in", [P, CT, E, B, CAP])
        y_slot = ph.sb("y_slot", [P, E, B, C])
        place = ph.sb("place", [P, B, NT, E])
        gate = ph.sb("gate", [P, B, NT, E])
        slots, orders = ph.sb("slots", [P, E, CAP]), ph.sb("orders", [P, NT, E])
        before, ones = ph.sb("before", [P, P], BF16), ph.sb("ones", [P, P], BF16)
        b1, b2 = ph.sb("b1", [P, E, ET]), ph.sb("b2", [P, E, C])
        wr, br = ph.sb("wr", [P, CT, E]), ph.sb("br", [P, E])
        w1 = [ph.sb(f"w1_{i}", [P, CT, HE]) for i in range(2)]
        w2 = [ph.sb(f"w2_{i}", [P, ET, C]) for i in range(2)]
        ps = ph.ps("ps", [P, 8, 512])
        w1_in = [nc_sem for nc_sem in (ph.ctx.enter_context(nc.semaphore(f"moe_w1_in{i}")) for i in range(2))]
        w2_in = [nc_sem for nc_sem in (ph.ctx.enter_context(nc.semaphore(f"moe_w2_in{i}")) for i in range(2))]

        w1_pairs = a["L1_ffn_W1"].rearrange("(e i) c h -> e i c h", i=2)
        w2_pairs = a["L1_ffn_W2"].rearrange("(e i) h c -> e i h c", i=2)
        slot_pairs = slot_in[:].rearrange("p c (e i) b s -> p c e i (b s)", i=2)
        y_pairs = y_slot[:].rearrange("p (e i) b c -> p e i b c", i=2)
        b1_pairs = b1[:].rearrange("p (e i) h -> p e i h", i=2)
        b2_pairs = b2[:].rearrange("p (e i) c -> p e i c", i=2)

        def load_w1(sp, e, i):
            sp.dma_start(w1[i][:], w1_pairs[e, i].rearrange("(t p) h -> p t h", p=P)).then_inc(w1_in[i], 16)

        def load_w2(sp, e, i):
            sp.dma_start(w2[i][:], w2_pairs[e, i].rearrange("(t p) c -> p t c", p=P)).then_inc(w2_in[i], 16)

        made, small = ph.sem("made"), ph.sem("small")
        with nc.Block() as block:
            @block.gpsimd
            def _(pool):
                nc.gpsimd.iota(slots[:], pattern=[[0, E], [1, CAP]], base=0, channel_multiplier=0,
                               allow_small_or_imprecise_dtypes=True)
                nc.gpsimd.iota(orders[:], pattern=[[0, NT], [-1, E]], base=E, channel_multiplier=0,
                               allow_small_or_imprecise_dtypes=True)
                nc.gpsimd.memset(ones[:], 1.0).then_inc(made, 1)
                pool.wait_ge(made, 1)
                nc.gpsimd.affine_select(out=before[:], in_=ones[:], compare_op=ALU.is_gt, fill=0.0, base=0,
                                        pattern=[[1, P]], channel_multiplier=-1)

            @block.sync
            def _(sp):
                with nc.allow_non_contiguous_dma(reason="small columns"):
                    parts = [(wr[:], a["L1_ffn_Wr"].rearrange("(t p) e -> p t e", p=P)),
                             (br[:], a["L1_ffn_br"][None, :].to_broadcast([P, E])),
                             (b1[:], a["L1_ffn_b1"].rearrange("e (t p) -> p e t", p=P)),
                             (b2[:], a["L1_ffn_b2"][None, :, :].to_broadcast([P, E, C]))]
                    for dst, src in parts:
                        sp.dma_start(dst, src).then_inc(small, 16)
                for i in range(2):
                    load_w1(sp, 0, i)
                    load_w2(sp, 0, i)
                sp.wait_ge(small, 16 * len(parts))
        ph.clear()

        with ExitStack() as part:
            def sb(name, shape, dt=F32):
                return part.enter_context(nc.sbuf_tensor(f"route_{name}", shape, dt))

            stats, mv, rstd, veps = sb("stats", [P, NT, 6]), sb("mv", [P, NT, 2]), sb("rstd", [P, NT]), sb("veps", [P, NT])
            xn, xnT = sb("xn", [P, NT, C]), sb("xnT", [P, CT, T])
            logit, prob, rest = sb("logit", [P, NT, E]), sb("prob", [P, NT, E]), sb("rest", [P, NT, E])
            same, key, chosen = sb("same", [P, NT, E]), sb("key", [P, NT, E]), sb("chosen", [P, 2, NT, E])
            top, total = sb("top", [P, NT]), sb("total", [P, NT])
            taken, takenb = sb("taken", [P, NT, E]), sb("takenb", [P, NT, E], BF16)
            onehot = sb("onehot", [P, NT, E, CAP])
            ln_done, var_eps, rstd_done, xn_done = (ph.sem(s) for s in ("ln_done", "var_eps", "rstd_done", "xn_done"))
            xT_mm, xT_out, logit_mm, step, exp_done = (ph.sem(s) for s in ("xT_mm", "xT_out", "logit_mm", "step", "exp_done"))
            pos_mm, hot_done, disp_mm, disp_out = (ph.sem(s) for s in ("pos_mm", "hot_done", "disp_mm", "disp_out"))
            PREP = 3
            ROUTE = 17

            def wide(v):
                return v.unsqueeze(2).to_broadcast([P, NT, E])

            with nc.Fori(0, B) as b:
                with nc.Block() as block:
                    @block.gpsimd
                    def _(pool):
                        pool.wait_ge(ln_done, 2 * NT)
                        nc.gpsimd.tensor_scalar(veps[:], mv[:, :, 1], EPS, None, ALU.add).then_inc(var_eps, 1)
                        pool.wait_ge(var_eps, 1)
                        nc.gpsimd.tensor_tensor(rstd[:], veps[:], k["half"][:, 0:NT], ALU.pow).then_inc(rstd_done, 1)

                    @block.vector
                    def _(dve):
                        layernorm_stats(nc, dve, lambda t: x_all[:, b, t, :], stats, mv, ln_done, 0)
                        dve.wait_ge(rstd_done, 1)
                        for t in range(NT):
                            nc.vector.tensor_scalar(xn[:, t], x_all[:, b, t, :], mv[:, t, 0:1], rstd[:, t:t + 1],
                                                    ALU.subtract, ALU.mult).then_inc(xn_done, 1)
                        for c in range(CT):
                            dve.wait_ge(xT_mm, c + 1)
                            nc.vector.tensor_copy(xnT[:, c, :], ps[:, c, :]).then_inc(xT_out, 1)
                        dve.wait_ge(logit_mm, 1)
                        count = [0]

                        def then(ins):
                            count[0] += 1
                            ins.then_inc(step, 1)
                            dve.wait_ge(step, count[0])

                        then(nc.vector.tensor_tensor(logit[:], ps[:, 2, 0:NT * E].rearrange("p (t e) -> p t e", e=E),
                                                     br[:].unsqueeze(1).to_broadcast([P, NT, E]), ALU.add))
                        then(nc.vector.tensor_reduce(top[:], logit[:], AX_X, ALU.max))
                        then(nc.vector.tensor_tensor(logit[:], logit[:], wide(top[:]), ALU.subtract))
                        assert count[0] == PREP
                        dve.wait_ge(exp_done, 1)
                        then(nc.vector.tensor_reduce(total[:], prob[:], AX_X, ALU.add))
                        then(nc.vector.reciprocal(total[:], total[:]))
                        then(nc.vector.tensor_tensor(prob[:], prob[:], wide(total[:]), ALU.mult))
                        for n in range(2):
                            p = prob if n == 0 else rest
                            then(nc.vector.tensor_reduce(top[:], p[:], AX_X, ALU.max))
                            then(nc.vector.tensor_tensor(same[:], p[:], wide(top[:]), ALU.is_equal))
                            then(nc.vector.tensor_tensor(key[:], same[:], orders[:], ALU.mult))
                            then(nc.vector.tensor_reduce(top[:], key[:], AX_X, ALU.max))
                            then(nc.vector.tensor_tensor(chosen[:, n], key[:], wide(top[:]), ALU.is_equal))
                            if n == 0:
                                then(nc.vector.scalar_tensor_tensor(out=rest[:], in0=chosen[:, 0], scalar=-2.0,
                                                                    in1=prob[:], op0=ALU.mult, op1=ALU.add))
                        then(nc.vector.tensor_tensor(taken[:], chosen[:, 0], chosen[:, 1], ALU.add))
                        nc.vector.tensor_tensor(gate[:, b], prob[:], taken[:], ALU.mult)
                        then(nc.vector.tensor_copy(takenb[:], taken[:]))
                        then(nc.vector.tensor_scalar(taken[:], taken[:], -OFF, OFF, ALU.mult, ALU.add))
                        assert count[0] == ROUTE + 3
                        dve.wait_ge(pos_mm, 1)
                        then(nc.vector.tensor_tensor(place[:, b], ps[:, 3, 0:NT * E].rearrange("p (t e) -> p t e", e=E),
                                                     taken[:], ALU.add))
                        for t in range(NT):
                            ins = nc.vector.tensor_tensor(onehot[:, t], slots[:], place[:, b, t, :].unsqueeze(2)
                                                          .to_broadcast([P, E, CAP]), ALU.is_equal)
                        ins.then_inc(hot_done, 1)

                    @block.scalar
                    def _(act):
                        act.wait_ge(step, PREP)
                        nc.scalar.activation(prob[:], logit[:], ACT.Exp).then_inc(exp_done, 1)
                        for i in range(2 * CT):
                            c, half = i // 2, i % 2
                            act.wait_ge(disp_mm, i + 1)
                            nc.scalar.activation(slot_in[:, c, half * EH:(half + 1) * EH, b, :],
                                                 ps[:, 4 + i, 0:EH * CAP].rearrange("p (e s) -> p e s", s=CAP),
                                                 ACT.Copy).then_inc(disp_out, 1)

                    @block.tensor
                    def _(pe):
                        pe.wait_ge(xn_done, NT)
                        for c in range(CT):
                            for t in range(NT):
                                ins = nc.tensor.transpose(ps[:, c, t * P:(t + 1) * P], xn[:, t, c * P:(c + 1) * P],
                                                          k["ident"][:])
                            ins.then_inc(xT_mm, 1)
                        pe.wait_ge(xT_out, CT)
                        for t in range(NT):
                            for c in range(CT):
                                ins = nc.tensor.matmul(ps[:, 2, t * E:(t + 1) * E], xnT[:, c, t * P:(t + 1) * P],
                                                       wr[:, c, :], start=(c == 0), stop=(c == CT - 1))
                        ins.then_inc(logit_mm, 1)
                        pe.wait_ge(step, ROUTE + 2)
                        for t in range(NT):
                            for n in range(t + 1):
                                ins = nc.tensor.matmul(ps[:, 3, t * E:(t + 1) * E], before[:] if n == t else ones[:],
                                                       takenb[:, n, :], start=(n == 0), stop=(n == t))
                        ins.then_inc(pos_mm, 1)
                        pe.wait_ge(hot_done, 1)
                        for i in range(2 * CT):
                            c, half = i // 2, i % 2
                            for t in range(NT):
                                ins = nc.tensor.matmul(ps[:, 4 + i, 0:EH * CAP], xn[:, t, c * P:(c + 1) * P],
                                                       onehot[:, t, half * EH:(half + 1) * EH, :],
                                                       start=(t == 0), stop=(t == NT - 1))
                            ins.then_inc(disp_mm, 1)
                ph.clear()

        with ExitStack() as part:
            hid = [part.enter_context(nc.sbuf_tensor(f"moe_hid{i}", [P, ET, B * CAP], F32)) for i in range(2)]
            up_mm, up_out, down_mm, down_out = (ph.sem(s) for s in ("up_mm", "up_out", "down_mm", "down_out"))
            with nc.Fori(0, E // 2) as e:
                with nc.Block() as block:
                    @block.sync
                    def _(sp):
                        for i in range(2):
                            sp.wait_ge(up_mm, ET * (i + 1))
                            load_w1(sp, (e + 1) % (E // 2), i)
                            sp.wait_ge(down_mm, B * (i + 1))
                            load_w2(sp, (e + 1) % (E // 2), i)

                    @block.tensor
                    def _(pe):
                        for i in range(2):
                            pe.wait_ge(w1_in[i], e * 16 + 16)
                            for n in range(ET):
                                m = i * ET + n
                                if m >= 4:
                                    pe.wait_ge(up_out, m - 3)
                                for c in range(CT):
                                    ins = nc.tensor.matmul(ps[:, m % 4, 0:B * CAP], w1[i][:, c, n * P:(n + 1) * P],
                                                           slot_pairs[:, c, e, i, :],
                                                           start=(c == 0), stop=(c == CT - 1))
                                ins.then_inc(up_mm, 1)
                            pe.wait_ge(w2_in[i], e * 16 + 16)
                            pe.wait_ge(up_out, ET * (i + 1))
                            for b in range(B):
                                m = i * B + b
                                if m >= 4:
                                    pe.wait_ge(down_out, m - 3)
                                for n in range(ET):
                                    ins = nc.tensor.matmul(ps[0:CAP, 4 + m % 4, 0:C], hid[i][:, n, b * CAP:(b + 1) * CAP],
                                                           w2[i][:, n, :], start=(n == 0), stop=(n == ET - 1))
                                ins.then_inc(down_mm, 1)

                    @block.scalar
                    def _(act):
                        for m in range(2 * ET):
                            i, n = m // ET, m % ET
                            act.wait_ge(up_mm, m + 1)
                            nc.scalar.activation(hid[i][:, n, :], ps[:, m % 4, 0:B * CAP], ACT.Relu,
                                                 bias=b1_pairs[:, e, i, n:n + 1]).then_inc(up_out, 1)

                    @block.vector
                    def _(dve):
                        for m in range(2 * B):
                            i, b = m // B, m % B
                            dve.wait_ge(down_mm, m + 1)
                            nc.vector.tensor_tensor(y_pairs[0:CAP, e, i, b, :], ps[0:CAP, 4 + m % 4, 0:C],
                                                    b2_pairs[0:CAP, e, i, :], ALU.add).then_inc(down_out, 1)
                ph.clear()

        with nc.Block() as block:
            @block.sync
            def _(sp):
                for i in range(2):
                    sp.wait_ge(w1_in[i], 16 * (E // 2 + 1))
                    sp.wait_ge(w2_in[i], 16 * (E // 2 + 1))

        with ExitStack() as part:
            hot, pick = (part.enter_context(nc.sbuf_tensor(f"moe_{n}", [P, 2, E, CAP], F32)) for n in ("hot", "pick"))
            pickT = part.enter_context(nc.sbuf_tensor("moe_pickT", [P, 2, E, P], F32))
            fin = part.enter_context(nc.sbuf_tensor("moe_fin", [P, NT, C], F32))
            hot_ok, pick_ok, turn_mm, turn_act, turn_dve, sum_mm, fin_ok, stored = (
                ph.sem(s) for s in ("hot_ok", "pick_ok", "turn_mm", "turn_act", "turn_dve", "sum_mm", "fin_ok", "stored"))
            with nc.Fori(0, B) as b:
                with nc.Block() as block:
                    @block.vector
                    def _(dve):
                        def choose(t):
                            if t >= 2:
                                dve.wait_ge(turn_mm, t - 1)
                            nc.vector.tensor_tensor(hot[:, t % 2], slots[:], place[:, b, t, :].unsqueeze(2)
                                                    .to_broadcast([P, E, CAP]), ALU.is_equal).then_inc(hot_ok, 1)
                            dve.wait_ge(hot_ok, t + 1)
                            nc.vector.tensor_tensor(pick[:, t % 2], hot[:, t % 2], gate[:, b, t, :].unsqueeze(2)
                                                    .to_broadcast([P, E, CAP]), ALU.mult).then_inc(pick_ok, 1)

                        choose(0)
                        for t in range(NT):
                            if t + 1 < NT:
                                choose(t + 1)
                            dve.wait_ge(turn_mm, t + 1)
                            if t >= 2:
                                dve.wait_ge(sum_mm, t - 1)
                            nc.vector.tensor_copy(pickT[0:CAP, t % 2, EH:E, :], ps[0:CAP, 2 * (t % 2) + 1, :]
                                                  .rearrange("p (e t) -> p e t", t=P)).then_inc(turn_dve, 1)
                            dve.wait_ge(sum_mm, t + 1)
                            nc.vector.tensor_tensor(fin[:, t, :], ps[:, 4 + t % 2, 0:C], x_all[:, b, t, :], ALU.add) \
                              .then_inc(fin_ok, 1)

                    @block.scalar
                    def _(act):
                        for t in range(NT):
                            act.wait_ge(turn_mm, t + 1)
                            if t >= 2:
                                act.wait_ge(sum_mm, t - 1)
                            nc.scalar.activation(pickT[0:CAP, t % 2, 0:EH, :], ps[0:CAP, 2 * (t % 2), :]
                                                 .rearrange("p (e t) -> p e t", t=P), ACT.Copy).then_inc(turn_act, 1)

                    @block.tensor
                    def _(pe):
                        def turn(t):
                            pe.wait_ge(pick_ok, t + 1)
                            if t >= 2:
                                pe.wait_ge(turn_act, t - 1)
                                pe.wait_ge(turn_dve, t - 1)
                            for n in range(E):
                                ins = nc.tensor.transpose(ps[0:CAP, 2 * (t % 2) + n // EH, (n % EH) * P:(n % EH + 1) * P],
                                                          pick[:, t % 2, n, :], k["ident"][:])
                            ins.then_inc(turn_mm, 1)

                        turn(0)
                        for t in range(NT):
                            if t + 1 < NT:
                                turn(t + 1)
                            pe.wait_ge(turn_act, t + 1)
                            pe.wait_ge(turn_dve, t + 1)
                            if t >= 2:
                                pe.wait_ge(fin_ok, t - 1)
                            for n in range(E):
                                ins = nc.tensor.matmul(ps[:, 4 + t % 2, 0:C], pickT[0:CAP, t % 2, n, :],
                                                       y_slot[0:CAP, n, b, :], start=(n == 0), stop=(n == E - 1))
                            ins.then_inc(sum_mm, 1)

                    @block.sync
                    def _(sp):
                        sp.wait_ge(fin_ok, NT)
                        sp.dma_start(out[b].rearrange("(t p) c -> p t c", p=P), fin[:]).then_inc(stored, 16)
                        sp.wait_ge(stored, 16)
                ph.clear()


def load_stream(nc, ph, x_all, x):
    loaded = ph.sem("x_loaded")
    with nc.Block() as block:
        @block.sync
        def _(sp):
            sp.dma_start(x_all[:], x.rearrange("b (t p) c -> p b t c", p=P)).then_inc(loaded, 16)
            sp.wait_ge(loaded, 16)
    ph.clear()


def program(nc, a, out):
    with Phase(nc, "all") as ph:
        x_all = ph.sb("x_all", [P, B, NT, C])
        k = setup_constants(nc, ph)
        load_stream(nc, ph, x_all, a["x"])
        def wide(l, q, kk, v, o, bo, bq, bk, bv):
            g = lambda n: a[f"L{l}_xattn_{n}"]
            return dict(wq=g(q), wk=g(kk), wv=g(v), wo=g(o), bq=g(bq), bk=g(bk), bv=g(bv), bo=g(bo) if bo else None)
        wide_attention(nc, k, x_all, "self", a["x"], None,
                       wide(0, "Wq", "Wk", "Wv", "Wp", None, "bq", "bk", "bv"), True)
        wide_attention(nc, k, x_all, "cross", a["x"], a["ctx_512"],
                       wide(0, "Wcq", "Wck", "Wcv", "Wp", "bp", "bcq", "bck", "bcv"), False)
        local_layers(nc, k, x_all, a)
        wide_attention(nc, k, x_all, "late", None, a["ctx_512"],
                       wide(1, "Wq", "Wk", "Wv", "Wo", "bo", "bq", "bk", "bv"), False)
        experts(nc, k, x_all, a, out)


_OUT = ((B, T, C), "float32")


def kernel(**inputs):
    import concourse.bacc as _bacc
    from concourse.bass_utils import run_bass_kernel_spmd as _run

    nc = _bacc.Bacc("TRN2", target_bir_lowering=False, num_devices=1)
    arrays, handles = {}, {}
    for name, value in {**inputs, **constants()}.items():
        value = np.ascontiguousarray(value)
        arrays[f"in_{name}_dram"] = value
        handles[name] = nc.dram_tensor(f"in_{name}_dram", value.shape, mybir.dt.from_np(value.dtype),
                                       kind="ExternalInput").ap()
    out = nc.dram_tensor("out_0_dram", _OUT[0], mybir.dt.from_np(np.dtype(_OUT[1])), kind="ExternalOutput").ap()
    program(nc, handles, out)
    return _run(nc, [arrays], core_ids=[0]).results[0]["out_0_dram"]
```

```python
from contextlib import ExitStack

import numpy as np

import concourse.bass as bass
from concourse import mybir

F32 = mybir.dt.float32
BF16 = mybir.dt.bfloat16
ALU = mybir.AluOpType
ACT = mybir.ActivationFunctionType
AX_X = mybir.AxisListType.X

P = 128
B, T, C = 4, 512, 256
NT = T // P
CT = C // P
H, D = 16, 16
HG = 4
NG = H // HG
TC, CC = 1601, 128
NEG = -1e30
EPS = 1e-5
QPAIR = "aabbac"
KPAIR = "ababca"
RM = 16 * len(QPAIR)
KROWS = RM + 3
S1_RING = 3
S2_RING = 3
AV_BANK = 6
AUX_BANK = 7
PROBS = 8
PIECES = 4
PACKED = 16 * len(QPAIR)


class Phase:

    def __init__(self, nc, name):
        self.nc, self.name, self.ctx, self.sems = nc, name, ExitStack(), []

    def __enter__(self):
        self.ctx.__enter__()
        return self

    def __exit__(self, *a):
        return self.ctx.__exit__(*a)

    def sb(self, name, shape, dt=F32):
        return self.ctx.enter_context(self.nc.sbuf_tensor(f"{self.name}_{name}", shape, dt))

    def ps(self, name, shape, dt=F32):
        return self.ctx.enter_context(self.nc.psum_tensor(f"{self.name}_{name}", shape, dt))

    def sem(self, name):
        s = self.ctx.enter_context(self.nc.semaphore(f"{self.name}_{name}"))
        self.sems.append(s)
        return s

    def clear(self):
        self.nc.all_engine_barrier()
        for n, s in enumerate(self.sems):
            (self.nc.sync, self.nc.gpsimd)[n % 2].sem_clear(s)
        self.nc.all_engine_barrier()


def chunks(n, size):
    return [(i, min(size, n - i)) for i in range(0, n, size)]


def setup_constants(nc, ph):
    k = {
        "ident": ph.sb("ident", [P, P]), "identb": ph.sb("identb", [P, P], BF16),
        "q_from_k": ph.sb("q_from_k", [P, P], BF16), "k_from_q": ph.sb("k_from_q", [P, 2 * P], BF16),
        "sum_rows": ph.sb("sum_rows", [P, P], BF16), "onesb": ph.sb("onesb", [P, P], BF16), "half": ph.sb("half", [P, NT * 16]),
    }
    made = ph.sem("made")
    with nc.Block() as block:
        @block.gpsimd
        def _(pool):
            nc.gpsimd.memset(k["ident"][:], 0.0).then_inc(made, 1)
            nc.gpsimd.memset(k["q_from_k"][:], 0.0).then_inc(made, 1)
            nc.gpsimd.memset(k["k_from_q"][:], 0.0).then_inc(made, 1)
            nc.gpsimd.memset(k["half"][:], -0.5).then_inc(made, 1)
            pool.wait_ge(made, 4)
            nc.gpsimd.affine_select(out=k["ident"][:], in_=k["ident"][:], compare_op=ALU.not_equal, fill=1.0,
                                    base=0, pattern=[[-1, P]], channel_multiplier=1).then_inc(made, 1)
            nc.gpsimd.affine_select(out=k["q_from_k"][:], in_=k["q_from_k"][:], compare_op=ALU.is_ge, fill=NEG,
                                    base=0, pattern=[[1, P]], channel_multiplier=-1).then_inc(made, 1)
            nc.gpsimd.affine_select(out=k["k_from_q"][:, 0:P], in_=k["k_from_q"][:, 0:P], compare_op=ALU.is_ge,
                                    fill=NEG, base=0, pattern=[[1, P]], channel_multiplier=-1).then_inc(made, 1)
            nc.gpsimd.affine_select(out=k["k_from_q"][:, P:2 * P], in_=k["k_from_q"][:, P:2 * P],
                                    compare_op=ALU.is_ge, fill=NEG, base=0, pattern=[[-1, P]],
                                    channel_multiplier=1).then_inc(made, 1)
            pool.wait_ge(made, 8)
            nc.gpsimd.memset(k["sum_rows"][:], 0.0).then_inc(made, 1)
            nc.gpsimd.memset(k["onesb"][:], 1.0)
            pool.wait_ge(made, 9)
            nc.gpsimd.memset(k["sum_rows"][:].rearrange("p (j r) -> p j r", r=32)[:, :, D:D + 1], 1.0 / P)
            nc.gpsimd.tensor_copy(k["identb"][:], k["ident"][:]).then_inc(made, 1)
            pool.wait_ge(made, 10)
    ph.clear()
    return k


def layernorm_stats(nc, dve, src, stats, mv, counted, first):
    for t in range(NT):
        nc.vector.bn_stats(stats[:, t], src(t)).then_inc(counted, 1)
    for t in range(NT):
        dve.wait_ge(counted, first + t + 1)
        nc.vector.bn_aggr(mv[:, t], stats[:, t]).then_inc(counted, 1)


def wide_attention(nc, k, x_all, name, src_dram, ctx_dram, w, causal):
    nk = T if causal else TC
    ktiles = chunks(nk, P)
    KT = len(ktiles)
    kchunks = chunks(nk, T if causal else 401)
    kvc = CT if causal else 1
    n_s1 = HG * NT * len(kchunks)
    NCH = len(kchunks)

    with Phase(nc, name) as ph:
        wq, wo = ph.sb("wq", [P, CT, C]), ph.sb("wo", [P, NG, C])
        wk, wv = ph.sb("wk", [P, kvc, C]), ph.sb("wv", [P, kvc, C])
        bq, bk = ph.sb("bq", [P, CT]), ph.sb("bk", [P, CT])
        bv, bo = ph.sb("bv", [P, C]), ph.sb("bo", [P, C])
        prob = ph.sb("prob", [P, 8, T])
        sums, den, rden = (ph.sb(n, [P, T]) for n in ("sums", "den", "rden"))
        xs = ph.sb("xs", [P, NT, C])
        xn, xnT = ph.sb("xn", [P, NT, C]), ph.sb("xnT", [P, CT, T])
        stats, mv, rstd = ph.sb("stats", [P, NT, 6]), ph.sb("mv", [P, NT, 2]), ph.sb("rstd", [P, NT])
        veps = ph.sb("veps", [P, NT])
        qparts, kparts = ph.sb("qparts", [P, CT, 3, T], BF16), ph.sb("kparts", [P, CT, 3, nk], BF16)
        qspill = nc.dram_tensor(f"{name}_qspill", [CT, P, 3, T], BF16).ap()
        kspill = nc.dram_tensor(f"{name}_kspill", [CT, P, 3, nk], BF16).ap()
        whole, rest = ph.sb("whole", [P, 2, T]), ph.sb("rest", [P, 2, T])
        qpack, kpack = ph.sb("qpack", [P, H, T], BF16), ph.sb("kpack", [P, H, nk], BF16)
        vals = ph.sb("vals", [P, KT, H, D + 1])
        y = ph.sb("y", [P, NG, T])
        mx, mxc, mrest = ph.sb("mx", [P, HG * NT, NCH]), ph.sb("mxc", [P, HG * NT]), ph.sb("mrest", [P, HG * NT])
        m3 = ph.sb("m3", [P, HG * NT, 3], BF16)
        if not causal:
            ctx_tok = ph.sb("ctx_tok", [P, KT, CC])
            ctxT = ph.sb("ctxT", [P, TC])
        ps = ph.ps("ps", [P, 8, 512])

        zeroed, loaded, biases, av_set = (ph.sem(s) for s in ("zeroed", "loaded", "biases", "av_set"))
        with nc.Block() as block:
            @block.gpsimd
            def _(pool):
                nc.gpsimd.memset(wo[:], 0.0).then_inc(zeroed, 1)

            @block.tensor
            def _(pe):
                for i in range(NT):
                    ins = nc.tensor.matmul(ps[:, AV_BANK, i * P:(i + 1) * P], k["sum_rows"][:], k["onesb"][:],
                                           start=True, stop=True)
                ins.then_inc(av_set, 1)

            @block.scalar
            def _(act):
                act.wait_ge(av_set, 1)
                nc.scalar.activation(sums[:], ps[:, AV_BANK, :], ACT.Copy)

            @block.vector
            def _(dve):
                nc.vector.memset(kpack[RM:RM + 32, :, :], 1.0)
                nc.vector.memset(vals[:], 1.0)
                nc.vector.memset(y[:], 0.0)
                dve.wait_ge(biases, 32)
                nc.vector.tensor_scalar(bq[:], bq[:], 0.25, None, ALU.mult)

            @block.sync
            def _(sp):
                with nc.allow_non_contiguous_dma(reason="bias columns"):
                    sp.dma_start(bq[:], w["bq"].rearrange("(t p) -> p t", p=P)).then_inc(biases, 16)
                    sp.dma_start(bk[:], w["bk"].rearrange("(t p) -> p t", p=P)).then_inc(biases, 16)
                n = 0
                for dst, src in ((wq, w["wq"]), (wk, w["wk"]), (wv, w["wv"])):
                    sp.dma_start(dst[:], src.rearrange("(t p) c -> p t c", p=P)).then_inc(loaded, 16)
                    n += 1
                sp.dma_start(bv[:], w["bv"][None, :].to_broadcast([P, C])).then_inc(loaded, 16)
                n += 1
                if w["bo"] is not None:
                    sp.dma_start(bo[:], w["bo"][None, :].to_broadcast([P, C])).then_inc(loaded, 16)
                    n += 1
                sp.wait_ge(zeroed, 1)
                for g in range(NG):
                    for j in range(HG):
                        h = g * HG + j
                        sp.dma_start(wo[32 * j:32 * j + D, g, :], w["wo"][h * D:(h + 1) * D, :]).then_inc(loaded, 16)
                        n += 1
                sp.wait_ge(loaded, 16 * n)
        ph.clear()

        src_in, ctx_in = ph.sem("src_in"), ph.sem("ctx_in")
        ln_done, var_eps, rstd_done, xn_done = (ph.sem(s) for s in ("ln_done", "var_eps", "rstd_done", "xn_done"))
        aux_mm, aux_act, aux_dve = ph.sem("aux_mm"), ph.sem("aux_act"), ph.sem("aux_dve")
        part_a, part_r, part_b, part_c = (ph.sem(f"part_{s}") for s in "arbc")
        packed = {(n, c): ph.sem(f"packed_{n}{c}") for n in "qk" for c in range(CT)}
        spilled = {(n, c): ph.sem(f"spilled_{n}{c}") for n in "qk" for c in range(CT)}
        s1_mm, s1_max, max_split = ph.sem("s1_mm"), ph.sem("s1_max"), ph.sem("max_split")
        s2_mm, exp_done, av_mm = ph.sem("s2_mm"), ph.sem("exp_done"), ph.sem("av_mm")
        sums_out, spread, inverted, normed = (ph.sem(s) for s in ("sums_out", "spread", "inverted", "normed"))

        def values_jobs(c):
            return [(("v", (c, j)), "dve") for j in range((KT + 3) // 4)]

        def parts_jobs(c):
            return [(("q", c), "act")] + [(("k", (c, n)), "act") for n in range(NCH)]

        turned_jobs = [(("xT", c), "act") for c in range(CT)]
        if not causal:
            turned_jobs += [(("cT", j), "act") for j in range((KT + 3) // 4)]
        kv_ready = turned_jobs[-1][0]

        def maxima_jobs(g):
            return [(("mx", g), "act")]

        out_jobs = [(("o", j), "dve") for j in range(NT // 2)]

        group_s1 = [(h, qt, ch) for h in range(HG) for qt in range(NT) for ch in range(NCH)]

        def s1_cols(qt, ch):
            return (0, (qt + 1) * P) if causal else kchunks[ch]

        def turn(b, prev, ahead, banks):
            attend = b is not None
            steps = NG * KT if attend else 0
            jobs = {s: [] for s in range(-1, steps + 1)}
            if attend:
                for n, job in enumerate(values_jobs(1)):
                    jobs[n * KT // 4].append(job)
                for g in range(1, NG):
                    jobs[g * KT - 2] += maxima_jobs(g)
            if ahead is not None:
                work = turned_jobs + parts_jobs(0) + parts_jobs(1)
                if attend:
                    first, last = KT, 2 * KT + max(KT - 4, 1)
                    for n, job in enumerate(work):
                        jobs[first + n * (last - first) // len(work)].append(job)
                    for n, job in enumerate(values_jobs(0)):
                        jobs[3 * KT - 2 + n * KT // 5].append(job)
                    jobs[steps - 2] += maxima_jobs(0)
                else:
                    jobs[-1] = work + values_jobs(0)
                    jobs[0] = jobs.get(0, []) + maxima_jobs(0)
            if attend:
                for n, job in enumerate(out_jobs):
                    jobs[(3 if KT > 4 else 1) + 2 * n].append(job)
            elif prev is not None:
                jobs[-1] += out_jobs
            order = [j for s in range(-1, steps + 1) for j in jobs[s]]
            number = {job: i for i, (job, _) in enumerate(order)}
            units = [job for job, _ in order if job[0] in "qk"]
            unit_no = {u: i for i, u in enumerate(units)}
            unit_step = {job: s for s in jobs for job, _ in jobs[s]}
            taken = {"act": aux_act, "dve": aux_dve}

            def out_of(job):
                i = number[job]
                return taken[order[i][1]], sum(who == order[i][1] for _, who in order[:i + 1])

            def bank_of(job):
                return ps[:, banks[number[job] % len(banks)], :]

            def unit_parts(u):
                if u[0] == "q":
                    return qparts[:, u[1]], 0, T
                (c, n) = u[1]
                return kparts[:, c], *kchunks[n]

            targets = ([*range(1, NG)] if attend else []) + ([0] if ahead is not None else [])
            if attend:
                lo, hi = 0, KT - 2
                s1_at = {(g, kt): range((kt - lo) * n_s1 // (hi - lo), (kt - lo + 1) * n_s1 // (hi - lo))
                         for g in range(len(targets)) for kt in range(lo, hi)}

            def src(t):
                return x_all[:, ahead, t, :] if src_dram is None else xs[:, t, :]

            with nc.Block() as block:
                @block.sync
                def _(sp):
                    def pack(c, fresh):
                        for kind, parts, spill, dst, pairs in (("q", qparts, qspill, qpack, QPAIR),
                                                               ("k", kparts, kspill, kpack, KPAIR)):
                            if fresh:
                                last = ("q", c) if kind == "q" else ("k", (c, NCH - 1))
                                sp.wait_ge(part_a, unit_no[last] + 1)
                                sp.wait_ge(part_b, unit_no[last] + 1)
                                sp.wait_ge(part_c, unit_no[last] + 1)
                            sp.dma_start(spill[c], parts[:, c]).then_inc(spilled[kind, c], 16)
                            sp.wait_ge(spilled[kind, c], 16)
                            if fresh and attend and kind == "q":
                                sp.wait_ge(s2_mm, 2 * KT * HG)
                            for row, part in enumerate(pairs):
                                sp.dma_start(dst[row * D:(row + 1) * D, 8 * c:8 * c + 8, :],
                                             spill[c, :, "abc".index(part), :].rearrange("(h d) n -> d h n", d=D)) \
                                  .then_inc(packed[kind, c], 16)

                    if ahead is not None and src_dram is not None:
                        sp.dma_start(xs[:], src_dram[ahead].rearrange("(t p) c -> p t c", p=P)).then_inc(src_in, 16)
                    if ahead is not None and not causal:
                        full = (KT - 1) * P
                        sp.dma_start(ctx_tok[:, 0:KT - 1, :], ctx_dram[ahead, 0:full, :]
                                     .rearrange("(k p) c -> p k c", p=P)).then_inc(ctx_in, 16)
                        sp.dma_start(ctx_tok[0:TC - full, KT - 1, :], ctx_dram[ahead, full:TC, :]).then_inc(ctx_in, 16)
                    if attend:
                        pack(1, False)
                    if ahead is not None:
                        pack(0, True)
                        for kind in "qk":
                            sp.wait_ge(packed[kind, 0], PACKED)

                @block.gpsimd
                def _(pool):
                    def divide(slot):
                        pool.wait_ge(inverted, PIECES * (slot + 1))
                        nc.gpsimd.tensor_tensor(y[:, (slot - 1) % NG, :], sums[:], rden[:], ALU.mult).then_inc(normed, 1)

                    if attend and w["bo"] is not None:
                        xb = x_all[:, b, :, :]
                        nc.gpsimd.tensor_tensor(xb, xb, bo[:].unsqueeze(1).to_broadcast([P, NT, C]), ALU.add)
                    if prev is not None:
                        divide(0)
                    divided = 1
                    if ahead is not None:
                        pool.wait_ge(ln_done, 2 * NT)
                        nc.gpsimd.tensor_scalar(veps[:], mv[:, :, 1], EPS, None, ALU.add).then_inc(var_eps, 1)
                        pool.wait_ge(var_eps, 1)
                        nc.gpsimd.tensor_tensor(rstd[:], veps[:], k["half"][:, 0:NT], ALU.pow).then_inc(rstd_done, 1)
                        for u, unit in enumerate(units):
                            while attend and divided < NG and unit_step[unit] > divided * KT + 1:
                                divide(divided)
                                divided += 1
                            parts, at, n = unit_parts(unit)
                            pool.wait_ge(part_b, u + 1)
                            nc.gpsimd.tensor_tensor(parts[:, 2, at:at + n], rest[:, u % 2, 0:n],
                                                    parts[:, 1, at:at + n], ALU.subtract).then_inc(part_c, 1)
                    while attend and divided < NG:
                        divide(divided)
                        divided += 1

                @block.scalar
                def _(act):
                    def second_part(u):
                        parts, at, n = unit_parts(units[u])
                        act.wait_ge(part_r, u + 1)
                        nc.scalar.activation(parts[:, 1, at:at + n], rest[:, u % 2, 0:n], ACT.Copy) \
                          .then_inc(part_b, 1)

                    def take(job):
                        what, j = job
                        act.wait_ge(aux_mm, number[job] + 1)
                        bank = bank_of(job)
                        if what == "xT":
                            nc.scalar.activation(xnT[:, j, :], bank, ACT.Copy).then_inc(aux_act, 1)
                        elif what == "cT":
                            at, n = j * 512, min(512, TC - j * 512)
                            nc.scalar.activation(ctxT[:, at:at + n], bank[:, 0:n], ACT.Copy).then_inc(aux_act, 1)
                        elif what == "mx":
                            for h in range(HG):
                                ins = nc.scalar.activation(qpack[RM:RM + 3, j * HG + h, :],
                                                           bank[32 * h:32 * h + 3, :], ACT.Copy)
                            ins.then_inc(aux_act, 1)
                        else:
                            u = unit_no[job]
                            parts, at, n = unit_parts(job)
                            if u >= 2:
                                act.wait_ge(part_r, u - 1)
                            if what == "k" and attend and j[0] == 1:
                                act.wait_ge(spilled["k", 1], 16)
                            if what == "q" and attend and j == 1:
                                act.wait_ge(spilled["q", 1], 16)
                            bias, scale = (bq[:, j:j + 1], 0.25) if what == "q" else (bk[:, j[0]:j[0] + 1], 1.0)
                            nc.scalar.activation(parts[:, 0, at:at + n], bank[:, 0:n], ACT.Identity, bias=bias,
                                                 scale=scale).then_inc(part_a, 1)
                            nc.scalar.activation(whole[:, u % 2, 0:n], bank[:, 0:n], ACT.Identity, bias=bias,
                                                 scale=scale).then_inc(aux_act, 1)
                            if u:
                                second_part(u - 1)
                            if u == len(units) - 1:
                                second_part(u)

                    def take_sums(g):
                        act.wait_ge(av_mm, (g + 1) * KT)
                        if g or prev is not None:
                            act.wait_ge(normed, g + 1)
                        nc.scalar.activation(sums[:], ps[:, AV_BANK, :], ACT.Copy).then_inc(sums_out, 1)

                    def take_all(s):
                        for job, who in jobs[s]:
                            if who == "act":
                                take(job)

                    take_all(-1)
                    if not attend:
                        take_all(0)
                    for s in range(steps):
                        g, kt = divmod(s, KT)
                        at, n = ktiles[kt]
                        q0 = at if causal else 0
                        for m in range(HG):
                            i = HG * s + m
                            act.wait_ge(s2_mm, i + 1)
                            if i >= PROBS:
                                act.wait_ge(av_mm, (i - PROBS) // HG + 1)
                            nc.scalar.activation(prob[0:n, i % PROBS, q0:T],
                                                 ps[0:n, S1_RING + i % S2_RING, q0:T], ACT.Exp) \
                              .then_inc(exp_done, 1)
                        if kt == 0 and g:
                            take_sums(g - 1)
                        take_all(s)
                    if attend:
                        take_sums(NG - 1)

                @block.vector
                def _(dve):
                    def norm():
                        if src_dram is not None:
                            dve.wait_ge(src_in, 16)
                        layernorm_stats(nc, dve, src, stats, mv, ln_done, 0)
                        dve.wait_ge(rstd_done, 1)
                        for t in range(NT):
                            nc.vector.tensor_scalar(xn[:, t], src(t), mv[:, t, 0:1], rstd[:, t:t + 1], ALU.subtract,
                                                    ALU.mult).then_inc(xn_done, 1)

                    def take(job):
                        what, j = job
                        if what in "qk":
                            u = unit_no[job]
                            parts, at, n = unit_parts(job)
                            dve.wait_ge(*out_of(job))
                            if u >= 2:
                                dve.wait_ge(part_c, u - 1)
                            nc.vector.tensor_tensor(rest[:, u % 2, 0:n], whole[:, u % 2, 0:n],
                                                    parts[:, 0, at:at + n], ALU.subtract).then_inc(part_r, 1)
                        if what == "o":
                            dve.wait_ge(aux_mm, number[job] + 1)
                            xb = x_all[:, prev, 2 * j:2 * j + 2, :]
                            nc.vector.tensor_tensor(xb, bank_of(job).rearrange("p (t c) -> p t c", c=C), xb,
                                                    ALU.add).then_inc(aux_dve, 1)
                        if what != "v":
                            return
                        dve.wait_ge(aux_mm, number[job] + 1)
                        c, j = j
                        if c == 0 and attend:
                            dve.wait_ge(av_mm, 2 * KT)
                        for n, kt in enumerate(range(4 * j, min(4 * j + 4, KT))):
                            rows = ktiles[kt][1]
                            ins = nc.vector.tensor_tensor(
                                vals[0:rows, kt, 8 * c:8 * c + 8, 0:D],
                                bank_of(job)[0:rows, n * P:(n + 1) * P].rearrange("p (h d) -> p h d", d=D),
                                bv[0:rows, c * P:(c + 1) * P].rearrange("p (h d) -> p h d", d=D), ALU.add)
                        ins.then_inc(aux_dve, 1)

                    def maximum(slot, i):
                        h, qt, ch = group_s1[i]
                        n = slot * n_s1 + i
                        cols = s1_cols(qt, ch)[1]
                        dve.wait_ge(s1_mm, n + 1)
                        nc.vector.tensor_reduce(mx[:, h * NT + qt, ch:ch + 1], ps[:, n % S1_RING, 0:cols], AX_X,
                                                ALU.max).then_inc(s1_max, 1)

                    def split(slot):
                        dve.wait_ge(s1_max, (slot + 1) * n_s1)
                        nc.vector.tensor_reduce(mxc[:], mx[:], AX_X, ALU.max).then_inc(max_split, 1)
                        dve.wait_ge(max_split, 5 * slot + 1)
                        if slot:
                            last = ("mx", targets[slot - 1])
                            dve.wait_ge(aux_mm, number[last] + 1)
                        nc.vector.tensor_scalar(m3[:, :, 0], mxc[:], -1.0, None, ALU.mult).then_inc(max_split, 1)
                        dve.wait_ge(max_split, 5 * slot + 2)
                        nc.vector.scalar_tensor_tensor(out=mrest[:], in0=mxc[:], scalar=-1.0, in1=m3[:, :, 0],
                                                       op0=ALU.mult, op1=ALU.subtract).then_inc(max_split, 1)
                        dve.wait_ge(max_split, 5 * slot + 3)
                        nc.vector.tensor_copy(m3[:, :, 1], mrest[:]).then_inc(max_split, 1)
                        dve.wait_ge(max_split, 5 * slot + 4)
                        nc.vector.tensor_tensor(m3[:, :, 2], mrest[:], m3[:, :, 1], ALU.subtract) \
                          .then_inc(max_split, 1)

                    def invert(slot):
                        def spread_sums():
                            if slot:
                                dve.wait_ge(sums_out, slot)
                                dve.wait_ge(inverted, PIECES * slot)
                            nc.vector.stream_shuffle(den[:], sums[:], [D] * 32).then_inc(spread, 1)

                        def piece(n):
                            cols = slice(n * T // PIECES, (n + 1) * T // PIECES)
                            dve.wait_ge(spread, slot + 1)
                            if slot:
                                dve.wait_ge(normed, slot)
                            nc.vector.reciprocal(rden[:, cols], den[:, cols]).then_inc(inverted, 1)

                        return [spread_sums] + [lambda n=n: piece(n) for n in range(PIECES)]

                    norm_step = max(KT - 4, 2)
                    if not attend and ahead is not None:
                        norm()
                        for job, _ in jobs[-1]:
                            take(job)
                        for i in range(n_s1):
                            maximum(0, i)
                        split(0)
                    pending = []
                    if prev is not None:
                        for piece in invert(0):
                            if attend:
                                pending.append(piece)
                            else:
                                piece()
                    if not attend and prev is not None:
                        for job, _ in jobs[-1]:
                            take(job)
                    for s in range(steps):
                        g, kt = divmod(s, KT)
                        if kt == 0:
                            for piece in pending[:]:
                                if g:
                                    piece()
                                    pending.remove(piece)
                        if kt == 1 and g:
                            pending += invert(g)
                        if s == norm_step and ahead is not None:
                            norm()
                        for i in (s1_at.get((g, kt), ()) if g < len(targets) else ()):
                            maximum(g, i)
                            if pending and (KT == 4 or i % 2):
                                pending.pop(0)()
                        if g < len(targets) and kt == KT - 3:
                            split(g)
                        for job, _ in jobs[s]:
                            take(job)
                    for piece in pending:
                        piece()

                @block.tensor
                def _(pe):
                    kv = xnT if causal else ctxT[:].unsqueeze(1) if not causal else None

                    def make(job):
                        what, j = job
                        i = number[job]
                        bank = bank_of(job)
                        if i >= len(banks):
                            pe.wait_ge(*out_of(order[i - len(banks)][0]))
                        if what == "xT":
                            pe.wait_ge(xn_done, NT)
                            for t in range(NT):
                                ins = nc.tensor.transpose(bank[:, t * P:(t + 1) * P], xn[:, t, j * P:(j + 1) * P],
                                                          k["ident"][:])
                        elif what == "cT":
                            pe.wait_ge(ctx_in, 32)
                            for kt in range(4 * j, min(4 * j + 4, KT)):
                                n = ktiles[kt][1]
                                ins = nc.tensor.transpose(bank[:, (kt % 4) * P:(kt % 4) * P + n],
                                                          ctx_tok[0:n, kt, :], k["ident"][0:n, 0:n])
                        elif what == "mx":
                            pe.wait_ge(max_split, 5 * (targets.index(j) + 1))
                            for qt in range(NT):
                                for h in range(HG):
                                    ins = nc.tensor.matmul(bank[32 * h:32 * h + 3, qt * P:(qt + 1) * P],
                                                           m3[:, h * NT + qt, :], k["identb"][:], start=True,
                                                           stop=True, skip_group_check=True)
                        elif what == "o":
                            pe.wait_ge(normed, 1)
                            for t in range(2):
                                for g in range(NG):
                                    ins = nc.tensor.matmul(bank[:, t * C:(t + 1) * C],
                                                           y[:, g, (2 * j + t) * P:(2 * j + t + 1) * P], wo[:, g, :],
                                                           start=(g == 0), stop=(g == NG - 1))
                        elif what == "q":
                            pe.wait_ge(*out_of(("xT", CT - 1)))
                            for c in range(CT):
                                ins = nc.tensor.matmul(bank, wq[:, c, j * P:(j + 1) * P], xnT[:, c, :],
                                                       start=(c == 0), stop=(c == CT - 1))
                        elif what == "k":
                            pe.wait_ge(*out_of(kv_ready))
                            half, (at, n) = j[0], kchunks[j[1]]
                            for c in range(kvc):
                                ins = nc.tensor.matmul(bank[:, 0:n], wk[:, c, half * P:(half + 1) * P],
                                                       kv[:, c, at:at + n], start=(c == 0), stop=(c == kvc - 1))
                        else:
                            half, j = j
                            if half == 0:
                                pe.wait_ge(*out_of(kv_ready))
                            for m, kt in enumerate(range(4 * j, min(4 * j + 4, KT))):
                                at, n = ktiles[kt]
                                for c in range(kvc):
                                    ins = nc.tensor.matmul(bank[0:n, m * P:(m + 1) * P], kv[:, c, at:at + n],
                                                           wv[:, c, half * P:(half + 1) * P], start=(c == 0),
                                                           stop=(c == kvc - 1))
                        ins.then_inc(aux_mm, 1)

                    def score_max(slot, i):
                        h, qt, ch = group_s1[i]
                        n = slot * n_s1 + i
                        at, cols = s1_cols(qt, ch)
                        if i == 0 and targets[slot] in (0, NG // 2):
                            for kind in "qk":
                                pe.wait_ge(packed[kind, targets[slot] // 2], PACKED)
                        if n >= S1_RING:
                            pe.wait_ge(s1_max, n - S1_RING + 1)
                        hh = targets[slot] * HG + h
                        ins = nc.tensor.matmul(ps[:, n % S1_RING, 0:cols], qpack[0:RM, hh, qt * P:(qt + 1) * P],
                                               kpack[0:RM, hh, at:at + cols], start=True, stop=not causal)
                        if causal:
                            ins = nc.tensor.matmul(ps[:, n % S1_RING, cols - P:cols], k["identb"][:],
                                                   k["k_from_q"][:, P:2 * P], start=False, stop=True)
                        ins.then_inc(s1_mm, 1)

                    def score(s, m):
                        g, kt = divmod(s, KT)
                        i = HG * s + m
                        at, n = ktiles[kt]
                        q0 = at if causal else 0
                        if i >= S2_RING:
                            pe.wait_ge(exp_done, i - S2_RING + 1)
                        out = ps[0:n, S1_RING + i % S2_RING, :]
                        ins = nc.tensor.matmul(out[:, q0:T], kpack[0:KROWS, g * HG + m, at:at + n],
                                               qpack[0:KROWS, g * HG + m, q0:T], start=True, stop=not causal)
                        if causal:
                            ins = nc.tensor.matmul(out[:, q0:q0 + P], k["identb"][:], k["q_from_k"][:],
                                                   start=False, stop=True)
                        ins.then_inc(s2_mm, 1)

                    def weigh(s):
                        g, kt = divmod(s, KT)
                        at, n = ktiles[kt]
                        q0 = at if causal else 0
                        pe.wait_ge(exp_done, HG * (s + 1))
                        if kt == 0 and g:
                            pe.wait_ge(sums_out, g)
                        if kt == 0 and g == NG // 2:
                            pe.wait_ge(*out_of(values_jobs(1)[-1][0]))
                        for j in range(HG):
                            ins = nc.tensor.matmul(ps[32 * j:32 * j + D + 1, AV_BANK, q0:T],
                                                   vals[0:n, kt, g * HG + j, :], prob[0:n, (HG * s + j) % PROBS, q0:T],
                                                   start=(kt == 0), stop=(kt == KT - 1), skip_group_check=True)
                        ins.then_inc(av_mm, 1)

                    for job, _ in jobs[-1]:
                        make(job)
                    if not attend and ahead is not None:
                        last = order[len(jobs[-1]) - len(banks):len(jobs[-1])]
                        for job, _ in last:
                            pe.wait_ge(*out_of(job))
                        for i in range(n_s1):
                            score_max(0, i)
                        for job, _ in jobs[0]:
                            make(job)
                    for s in range(steps):
                        g, kt = divmod(s, KT)
                        todo = list(s1_at.get((g, kt), ())) if g < len(targets) else []
                        if kt == 0 and g:
                            pe.wait_ge(*out_of(("mx", g)))
                        for m in range(HG):
                            score(s, m)
                            for i in todo[m:m + 1]:
                                score_max(g, i)
                        if s:
                            weigh(s - 1)
                        for i in todo[HG:HG + 1]:
                            score_max(g, i)
                        for job, _ in jobs[s][:1]:
                            make(job)
                        for i in todo[HG + 1:]:
                            score_max(g, i)
                        for job, _ in jobs[s][1:]:
                            make(job)
                    if attend:
                        weigh(steps - 1)
            ph.clear()

        turn(None, None, 0, [0, 1, 2, 3, 4, 5, AUX_BANK])
        with nc.Fori(0, B - 1) as b:
            turn(b, (b + B - 1) % B, b + 1, [AUX_BANK])
        turn(B - 1, B - 2, None, [AUX_BANK])
        turn(None, B - 1, None, [0, 1])


L = 2
LH, LD = 8, 64
INNER = LH * LD
HP = LH // 2
HID = int(C * 4 * 2 / 3)
FT = -(-HID // P)
FR = HID - (FT - 1) * P
WINDOW = P
QK_SCALE = 8.0


def rotary_tables():
    half = np.arange(0, LD, 2, dtype=np.float32)
    inv_freq = (1.0 / np.float32(10000.0) ** (half / np.float32(LD))).astype(np.float32)
    t = np.arange(T, dtype=np.float32)
    freqs = t[:, None] * inv_freq[None, :]
    base = (half + np.float32(0.4 * LD)) / np.float32(1.4 * LD)
    power = (t - T // 2) / np.float32(WINDOW // 2)
    scale = base[None, :] ** power[:, None]
    out = np.empty((2, 2, T, LD), np.float32)
    for i, s in enumerate((scale * np.float32(QK_SCALE), np.float32(1) / scale)):
        cos, sin = np.cos(freqs) * s, np.sin(freqs) * s
        out[i, 0] = np.concatenate([cos, cos], -1)
        out[i, 1] = np.concatenate([-sin, sin], -1)
    return out


def constants():
    return {"rotary": rotary_tables()}


def local_layers(nc, k, x_all, a):
    with Phase(nc, "local") as ph:
        z_all = ph.sb("z_all", [P, B, NT, C])
        wqkv, wo = ph.sb("wqkv", [P, CT, 3 * INNER]), ph.sb("wo", [P, HP, C])
        w1, w2 = ph.sb("w1", [P, CT, 2 * HID]), ph.sb("w2", [P, FT, C])
        b1, b2 = ph.sb("b1", [P, 2, FT]), ph.sb("b2", [P, C])
        ln_g, ln_b = ph.sb("ln_g", [P, CT]), ph.sb("ln_b", [P, CT])
        raw, rot = ph.sb("raw", [P, 2, 2, NT, LD]), ph.sb("rot", [P, 2, 2, NT, LD])
        head_scale = ph.sb("head_scale", [P, 2, LD])
        zt, hT = ph.sb("zt", [P, NT, C]), ph.sb("hT", [P, CT, T])
        sq, by_cos, by_sin = ph.sb("sq", [P, 2, INNER]), ph.sb("by_cos", [P, 2, INNER]), ph.sb("by_sin", [P, 2, INNER])
        ss, ssc, rnorm = (ph.sb(n, [P, 2 * NT, LH]) for n in ("ss", "ssc", "rnorm"))
        qk = ph.sb("qk", [P, 2 * NT, INNER])
        qT, kz = ph.sb("qT", [P, HP, T]), ph.sb("kz", [P, LH, T])
        vt = ph.sb("vt", [P, NT, INNER])
        mxs, nmx = ph.sb("mxs", [P, 2, 4]), ph.sb("nmx", [P, 2, 4])
        sums, rsums = ph.sb("sums", [P, 2, 4]), ph.sb("rsums", [P, 2, 4])
        prob, probT = ph.sb("prob", [P, 2, 4, 2 * P]), ph.sb("probT", [P, 2, 4, 2 * P])
        oT = ph.sb("oT", [P, HP, T])
        shifted, hn, hnT = ph.sb("shifted", [P, NT, P]), ph.sb("hn", [P, NT, C]), ph.sb("hnT", [P, CT, T])
        stats, mv, rstd = ph.sb("stats", [P, NT, 2, 6]), ph.sb("mv", [P, NT, 2]), ph.sb("rstd", [P, NT])
        veps = ph.sb("veps", [P, NT])
        gel, hid = ph.sb("gel", [P, 2, T]), ph.sb("hid", [P, FT, T])
        ps = ph.ps("ps", [P, 8, 512])

        tables = ph.sem("tables")
        ln_done, var_eps, rstd_done = ph.sem("ln_done"), ph.sem("var_eps"), ph.sem("rstd_done")
        with nc.Block() as block:
            @block.gpsimd
            def _(pool):
                nc.gpsimd.memset(kz[:], 0.0)
                nc.gpsimd.memset(w2[:, FT - 1, :], 0.0)

            @block.vector
            def _(dve):
                nc.vector.memset(hid[:, FT - 1, :], 0.0)
                nc.vector.memset(hT[:, 1, 0:1], 0.0)
                nc.vector.memset(shifted[0:1, 0, :], 0.0)

            @block.sync
            def _(sp):
                sp.dma_start(raw[:].rearrange("p a b t d -> p (a b) t d"),
                             a["rotary"].rearrange("a b (t p) d -> p (a b) t d", p=P)).then_inc(tables, 16)
                sp.wait_ge(tables, 16)
        with nc.Fori(0, B) as b:
            with nc.Block() as block:
                @block.vector
                def _(dve):
                    for t in range(NT):
                        nc.vector.bn_stats(stats[:, t, 0], x_all[:, b, t, :]).then_inc(ln_done, 1)
                    for t in range(NT):
                        dve.wait_ge(ln_done, t + 1)
                        nc.vector.bn_aggr(mv[:, t], stats[:, t, 0]).then_inc(ln_done, 1)
                    dve.wait_ge(rstd_done, 1)
                    for t in range(NT):
                        nc.vector.tensor_scalar(z_all[:, b, t, :], x_all[:, b, t, :], mv[:, t, 0:1],
                                                rstd[:, t:t + 1], ALU.subtract, ALU.mult)

                @block.gpsimd
                def _(pool):
                    pool.wait_ge(ln_done, 2 * NT)
                    nc.gpsimd.tensor_scalar(veps[:], mv[:, :, 1], EPS, None, ALU.add).then_inc(var_eps, 1)
                    pool.wait_ge(var_eps, 1)
                    nc.gpsimd.tensor_tensor(rstd[:], veps[:], k["half"][:, 0:NT], ALU.pow).then_inc(rstd_done, 1)
            ph.clear()

        loaded, scales, scaled = ph.sem("loaded"), ph.sem("scales"), ph.sem("scaled")
        copied, tile_mm, tile_act, tile_dve = (ph.sem(n) for n in ("copied", "tile_mm", "tile_act", "tile_dve"))
        squared, ss_sum, ss_ok, rotated = (ph.sem(n) for n in ("squared", "ss_sum", "ss_ok", "rotated"))
        rot_sum, norm_ok, qk_ready = (ph.sem(n) for n in ("rot_sum", "norm_ok", "qk_ready"))
        s_mm, maxed, exp_done, summed = (ph.sem(n) for n in ("s_mm", "maxed", "exp_done", "summed"))
        p_ready, pT_mm, pT_act, pT_dve = (ph.sem(n) for n in ("p_ready", "pT_mm", "pT_act", "pT_dve"))
        o_mm, o_out, wo_mm, z_attn = (ph.sem(n) for n in ("o_mm", "o_out", "wo_mm", "z_attn"))
        shift_in, hn_done, hnT_mm, hnT_out = (ph.sem(n) for n in ("shift_in", "hn_done", "hnT_mm", "hnT_out"))
        up_mm, gel_done, hid_done, down_mm = (ph.sem(n) for n in ("up_mm", "gel_done", "hid_done", "down_mm"))
        biased = ph.sem("biased")

        RING = 8
        tiles = [("zT", c, "dve") for c in range(CT)]
        for t in range(NT + 1):
            if t < NT:
                tiles += [("q", t, "dve"), ("k", t, "dve"), ("v", t, "act")]
            if t:
                tiles += [("qT", t - 1, "act"), ("kT", t - 1, "act")]
        taken = {"act": tile_act, "dve": tile_dve}

        def nth(i):
            return sum(t[2] == tiles[i][2] for t in tiles[:i + 1])

        steps = [(w, hg) for w in range(NT) for hg in range(LH // 4)]

        with nc.Fori(0, L) as l:
            with nc.Block() as block:
                @block.sync
                def _(sp):
                    with nc.allow_non_contiguous_dma(reason="small columns"):
                        sp.dma_start(head_scale[:, 0, :], a["L0_ffn_q_scale"][l][None, :].to_broadcast([P, LD])) \
                          .then_inc(scales, 16)
                        sp.dma_start(head_scale[:, 1, :], a["L0_ffn_k_scale"][l][None, :].to_broadcast([P, LD])) \
                          .then_inc(scales, 16)
                        parts = [
                            (wqkv[:], a["L0_ffn_wqkv"][l].rearrange("(t p) n -> p t n", p=P)),
                            (wo[:], a["L0_ffn_wo"][l].rearrange("(t p) n -> p t n", p=P)),
                            (w1[:], a["L0_ffn_w1"][l].rearrange("(t p) n -> p t n", p=P)),
                            (w2[:, 0:FT - 1, :],
                             a["L0_ffn_w2"][l, 0:(FT - 1) * P, :].rearrange("(t p) n -> p t n", p=P)),
                            (w2[0:FR, FT - 1, :], a["L0_ffn_w2"][l, (FT - 1) * P:HID, :]),
                            (b2[:], a["L0_ffn_b2"][l][None, :].to_broadcast([P, C])),
                            (ln_g[:], a["L0_ffn_ln_g"][l].rearrange("(t p) -> p t", p=P)),
                            (ln_b[:], a["L0_ffn_ln_b"][l].rearrange("(t p) -> p t", p=P)),
                        ]
                        for i in range(2):
                            col = a["L0_ffn_b1"][l, i * HID:(i + 1) * HID]
                            parts += [(b1[:, i, 0:FT - 1], col[0:(FT - 1) * P].rearrange("(t p) -> p t", p=P)),
                                      (b1[0:FR, i, FT - 1:FT], col[(FT - 1) * P:HID][:, None])]
                        for dst, src in parts:
                            sp.dma_start(dst, src).then_inc(loaded, 16)
                        sp.wait_ge(loaded, 16 * len(parts))

                @block.vector
                def _(dve):
                    dve.wait_ge(scales, 32)
                    for i in range(2):
                        hs = head_scale[:, i, :]
                        nc.vector.tensor_tensor(rot[:, i, 0], raw[:, i, 0],
                                                hs.unsqueeze(1).to_broadcast([P, NT, LD]), ALU.mult)
                        for lo, other in ((0, LD // 2), (LD // 2, 0)):
                            nc.vector.tensor_tensor(
                                rot[:, i, 1, :, lo:lo + LD // 2], raw[:, i, 1, :, lo:lo + LD // 2],
                                hs[:, other:other + LD // 2].unsqueeze(1).to_broadcast([P, NT, LD // 2]), ALU.mult)
            ph.clear()
            with nc.Fori(0, B) as b:
                with nc.Block() as block:
                    @block.sync
                    def _(sp):
                        sp.wait_ge(z_attn, 2)
                        sp.dma_start(shifted[1:P, :, :], zt[0:P - 1, :, P:C]).then_inc(shift_in, 16)
                        sp.dma_start(shifted[0:1, 1:NT, :], zt[P - 1:P, 0:NT - 1, P:C]).then_inc(shift_in, 16)
                        sp.wait_ge(shift_in, 32)

                    @block.gpsimd
                    def _(pool):
                        for u in range(2 * NT):
                            pool.wait_ge(rotated, u + 1)
                            nc.gpsimd.tensor_tensor(by_cos[:, u % 2], by_cos[:, u % 2], by_sin[:, u % 2], ALU.add) \
                              .then_inc(rot_sum, 1)
                            pool.wait_ge(ss_ok, u + 1)
                            nc.gpsimd.tensor_tensor(rnorm[:, u], ssc[:, u], k["half"][:, 0:LH], ALU.pow) \
                              .then_inc(norm_ok, 1)
                            pool.wait_ge(rot_sum, u + 1)
                            pool.wait_ge(norm_ok, u + 1)
                            nc.gpsimd.tensor_tensor(
                                qk[:, u].rearrange("p (h d) -> p h d", d=LD),
                                by_cos[:, u % 2].rearrange("p (h d) -> p h d", d=LD),
                                rnorm[:, u].unsqueeze(2).to_broadcast([P, LH, LD]), ALU.mult).then_inc(qk_ready, 1)
                        for s, (w, hg) in enumerate(steps):
                            c0 = 0 if w else P
                            pool.wait_ge(summed, s + 1)
                            pr = prob[:, s % 2, :, c0:2 * P]
                            nc.gpsimd.tensor_tensor(pr, pr, rsums[:, s % 2].unsqueeze(2).to_broadcast(
                                [P, 4, 2 * P - c0]), ALU.mult).then_inc(p_ready, 1)
                        pool.wait_ge(ln_done, 3 * NT)
                        nc.gpsimd.tensor_scalar(veps[:], mv[:, :, 1], EPS, None, ALU.add).then_inc(var_eps, 1)
                        pool.wait_ge(var_eps, 1)
                        nc.gpsimd.tensor_tensor(rstd[:], veps[:], k["half"][:, 0:NT], ALU.pow).then_inc(rstd_done, 1)
                        pool.wait_ge(hn_done, 1)
                        pool.wait_ge(shift_in, 32)
                        nc.gpsimd.tensor_tensor(zt[:], zt[:], b2[:].unsqueeze(1).to_broadcast([P, NT, C]), ALU.add) \
                          .then_inc(biased, 1)

                    @block.scalar
                    def _(act):
                        u = 0
                        for i, (what, t, who) in enumerate(tiles):
                            bank = ps[:, i % RING, :]
                            if what in ("q", "k"):
                                act.wait_ge(tile_mm, i + 1)
                                if u >= 2:
                                    act.wait_ge(ss_sum, u - 1)
                                nc.scalar.activation(sq[:, u % 2], bank, ACT.Square).then_inc(squared, 1)
                                u += 1
                            if who != "act":
                                continue
                            act.wait_ge(tile_mm, i + 1)
                            cols = slice(t * P, (t + 1) * P)
                            heads = bank.rearrange("p (h q) -> p h q", q=P)
                            if what == "v":
                                ins = nc.scalar.activation(vt[:, t], bank, ACT.Copy)
                            elif what == "qT":
                                ins = nc.scalar.activation(qT[:, :, cols], heads, ACT.Copy)
                            else:
                                kzp = kz[:].rearrange("p (h two) t -> p h two t", two=2)
                                nc.scalar.activation(kzp[0:LD, :, 0, cols], heads[0:LD], ACT.Copy)
                                ins = nc.scalar.activation(kzp[LD:P, :, 1, cols], heads[LD:P], ACT.Copy)
                            ins.then_inc(tile_act, 1)

                        def exps(s):
                            c0 = 0 if steps[s][0] else P
                            act.wait_ge(maxed, 2 * s + 2)
                            if s >= 2:
                                act.wait_ge(pT_mm, s - 1)
                            for m in range(4):
                                bank = ps[:, 2 * (s % 2) + m // 2, (m % 2) * 2 * P + c0:(m % 2 + 1) * 2 * P]
                                ins = nc.scalar.activation(prob[:, s % 2, m, c0:2 * P], bank, ACT.Exp,
                                                           bias=nmx[:, s % 2, m:m + 1],
                                                           accum_out=sums[:, s % 2, m:m + 1])
                            ins.then_inc(exp_done, 1)

                        def take_probT(s):
                            c0 = 0 if steps[s][0] else P
                            act.wait_ge(pT_mm, s + 1)
                            if s >= 2:
                                act.wait_ge(o_mm, s - 1)
                            nc.scalar.activation(
                                probT[:, s % 2, 0:2, c0:2 * P],
                                ps[:, 4, :].rearrange("p (m c) -> p m c", c=2 * P)[:, :, c0:2 * P],
                                ACT.Copy).then_inc(pT_act, 1)

                        exps(0)
                        for s in range(len(steps)):
                            if s + 1 < len(steps):
                                exps(s + 1)
                            take_probT(s)
                        for f in range(FT):
                            rows = P if f < FT - 1 else FR
                            act.wait_ge(up_mm, 2 * f + 1)
                            if f >= 2:
                                act.wait_ge(hid_done, f - 1)
                            nc.scalar.activation(gel[0:rows, f % 2, :], ps[0:rows, 4 + (2 * f) % 4, :], ACT.Gelu,
                                                 bias=b1[0:rows, 1, f:f + 1]).then_inc(gel_done, 1)

                    @block.vector
                    def _(dve):
                        nc.vector.tensor_copy(zt[:], z_all[:, b]).then_inc(copied, 1)
                        u = 0
                        for i, (what, t, who) in enumerate(tiles):
                            if who != "dve":
                                continue
                            bank = ps[:, i % RING, :]
                            dve.wait_ge(tile_mm, i + 1)
                            if what == "zT":
                                if t == 0:
                                    ins = nc.vector.tensor_copy(hT[:, 0, :], bank)
                                else:
                                    ins = nc.vector.tensor_copy(hT[:, 1, 1:T], bank[:, 0:T - 1])
                                ins.then_inc(tile_dve, 1)
                                continue
                            i2 = 0 if what == "q" else 1
                            dve.wait_ge(squared, u + 1)
                            nc.vector.tensor_reduce(ss[:, u], sq[:, u % 2].rearrange("p (h d) -> p h d", d=LD), AX_X,
                                                    ALU.add).then_inc(ss_sum, 1)
                            if u >= 2:
                                dve.wait_ge(qk_ready, u - 1)
                            heads = bank.rearrange("p (h d) -> p h d", d=LD)
                            bc = by_cos[:, u % 2].rearrange("p (h d) -> p h d", d=LD)
                            bs = by_sin[:, u % 2].rearrange("p (h d) -> p h d", d=LD)
                            cos, sin = rot[:, i2, 0, t, :], rot[:, i2, 1, t, :]
                            nc.vector.tensor_tensor(bc, heads, cos.unsqueeze(1).to_broadcast([P, LH, LD]), ALU.mult)
                            for lo, other in ((0, LD // 2), (LD // 2, 0)):
                                ins = nc.vector.tensor_tensor(
                                    bs[:, :, lo:lo + LD // 2], heads[:, :, other:other + LD // 2],
                                    sin[:, lo:lo + LD // 2].unsqueeze(1).to_broadcast([P, LH, LD // 2]), ALU.mult)
                            ins.then_inc(rotated, 1)
                            dve.wait_ge(ss_sum, u + 1)
                            nc.vector.tensor_scalar(ssc[:, u], ss[:, u], 1e-24, None, ALU.max).then_inc(ss_ok, 1)
                            u += 1

                        def maxima(s):
                            c0 = 0 if steps[s][0] else P
                            dve.wait_ge(s_mm, s + 1)
                            nc.vector.tensor_reduce(
                                mxs[:, s % 2], ps[:, 2 * (s % 2):2 * (s % 2) + 2, :].rearrange(
                                    "p a (m c) -> p (a m) c", c=2 * P)[:, :, c0:2 * P], AX_X, ALU.max) \
                              .then_inc(maxed, 1)
                            dve.wait_ge(maxed, 2 * s + 1)
                            if s >= 2:
                                dve.wait_ge(exp_done, s - 1)
                            nc.vector.tensor_scalar(nmx[:, s % 2], mxs[:, s % 2], -1.0, None, ALU.mult) \
                              .then_inc(maxed, 1)

                        maxima(0)
                        for s, (w, hg) in enumerate(steps):
                            c0 = 0 if w else P
                            dve.wait_ge(exp_done, s + 1)
                            if s >= 2:
                                dve.wait_ge(p_ready, s - 1)
                            nc.vector.reciprocal(rsums[:, s % 2], sums[:, s % 2]).then_inc(summed, 1)
                            if s + 1 < len(steps):
                                maxima(s + 1)
                            dve.wait_ge(pT_mm, s + 1)
                            if s >= 2:
                                dve.wait_ge(o_mm, s - 1)
                            nc.vector.tensor_copy(
                                probT[:, s % 2, 2:4, c0:2 * P],
                                ps[:, 5, :].rearrange("p (m c) -> p m c", c=2 * P)[:, :, c0:2 * P]) \
                              .then_inc(pT_dve, 1)
                            dve.wait_ge(o_mm, s + 1)
                            nc.vector.tensor_copy(oT[:, 2 * hg:2 * hg + 2, w * P:(w + 1) * P],
                                                  ps[:, 6 + s % 2, 0:2 * P].rearrange("p (h q) -> p h q", q=P)) \
                              .then_inc(o_out, 1)
                        for j in range(NT // 2):
                            dve.wait_ge(wo_mm, j + 1)
                            zz = zt[:, 2 * j:2 * j + 2, :]
                            nc.vector.tensor_tensor(zz, ps[:, j, :].rearrange("p (t c) -> p t c", c=C), zz, ALU.add) \
                              .then_inc(z_attn, 1)
                        dve.wait_ge(z_attn, 2)
                        for t in range(NT):
                            nc.vector.bn_stats(stats[:, t, 0], zt[:, t, 0:P]).then_inc(ln_done, 1)
                        dve.wait_ge(shift_in, 32)
                        for t in range(NT):
                            nc.vector.bn_stats(stats[:, t, 1], shifted[:, t]).then_inc(ln_done, 1)
                        for t in range(NT):
                            dve.wait_ge(ln_done, NT + t + 1)
                            nc.vector.bn_aggr(mv[:, t], stats[:, t]).then_inc(ln_done, 1)
                        dve.wait_ge(rstd_done, 1)
                        for t in range(NT):
                            for dst, src in ((hn[:, t, 0:P], zt[:, t, 0:P]), (hn[:, t, P:C], shifted[:, t])):
                                ins = nc.vector.tensor_scalar(dst, src, mv[:, t, 0:1], rstd[:, t:t + 1],
                                                              ALU.subtract, ALU.mult)
                        ins.then_inc(hn_done, 1)
                        for c in range(CT):
                            dve.wait_ge(hnT_mm, c + 1)
                            nc.vector.tensor_scalar(hnT[:, c, :], ps[:, 2 + c, :], ln_g[:, c:c + 1], ln_b[:, c:c + 1],
                                                    ALU.mult, ALU.add).then_inc(hnT_out, 1)
                        for f in range(FT):
                            rows = P if f < FT - 1 else FR
                            dve.wait_ge(up_mm, 2 * f + 2)
                            dve.wait_ge(gel_done, f + 1)
                            nc.vector.scalar_tensor_tensor(
                                out=hid[0:rows, f, :], in0=ps[0:rows, 4 + (2 * f + 1) % 4, :],
                                scalar=b1[0:rows, 0, f:f + 1], in1=gel[0:rows, f % 2, :], op0=ALU.add, op1=ALU.mult) \
                              .then_inc(hid_done, 1)
                        dve.wait_ge(biased, 1)
                        for j in range(NT // 2):
                            dve.wait_ge(down_mm, j + 1)
                            nc.vector.tensor_tensor(z_all[:, b, 2 * j:2 * j + 2, :],
                                                    ps[:, j, :].rearrange("p (t c) -> p t c", c=C),
                                                    zt[:, 2 * j:2 * j + 2, :], ALU.add)

                    @block.tensor
                    def _(pe):
                        for i, (what, t, who) in enumerate(tiles):
                            bank = ps[:, i % RING, :]
                            if i >= RING:
                                last = tiles[i - RING]
                                if last[0] in ("q", "k"):
                                    pe.wait_ge(rotated, 2 * last[1] + (last[0] == "k") + 1)
                                else:
                                    pe.wait_ge(taken[last[2]], nth(i - RING) if last[2] == "act" else last[1] + 1)
                            if what == "zT":
                                pe.wait_ge(copied, 1)
                                for n in range(NT):
                                    ins = nc.tensor.transpose(bank[:, n * P:(n + 1) * P], zt[:, n, t * P:(t + 1) * P],
                                                              k["ident"][:])
                            elif what in ("qT", "kT"):
                                u = 2 * t + (what == "kT")
                                pe.wait_ge(qk_ready, u + 1)
                                for n in range(HP):
                                    ins = nc.tensor.transpose(bank[:, n * P:(n + 1) * P],
                                                              qk[:, u, n * P:(n + 1) * P], k["ident"][:])
                            else:
                                pe.wait_ge(tile_dve, CT)
                                part = "qkv".index(what)
                                for c in range(CT):
                                    ins = nc.tensor.matmul(bank, hT[:, c, t * P:(t + 1) * P],
                                                           wqkv[:, c, part * INNER:(part + 1) * INNER],
                                                           start=(c == 0), stop=(c == CT - 1))
                            ins.then_inc(tile_mm, 1)

                        def score(s):
                            w, hg = steps[s]
                            c0 = 0 if w else P
                            if s >= 2:
                                pe.wait_ge(exp_done, s - 1)
                            for m in range(4):
                                h = 4 * hg + m
                                out = ps[:, 2 * (s % 2) + m // 2, (m % 2) * 2 * P + c0:(m % 2 + 1) * 2 * P]
                                nc.tensor.matmul(out, qT[:, h // 2, w * P:(w + 1) * P],
                                                 kz[:, h, (w - 1) * P + c0:(w + 1) * P], start=True, stop=False)
                                ins = nc.tensor.matmul(out, k["identb"][:], k["k_from_q"][:, c0:2 * P],
                                                       start=False, stop=True)
                            ins.then_inc(s_mm, 1)

                        def turn(s):
                            pe.wait_ge(p_ready, s + 1)
                            if s:
                                pe.wait_ge(pT_act, s)
                                pe.wait_ge(pT_dve, s)
                            for m in range(4):
                                for kb in range(0 if steps[s][0] else 1, 2):
                                    ins = nc.tensor.transpose(
                                        ps[:, 4 + m // 2, (m % 2) * 2 * P + kb * P:(m % 2) * 2 * P + (kb + 1) * P],
                                        prob[:, s % 2, m, kb * P:(kb + 1) * P], k["ident"][:])
                            ins.then_inc(pT_mm, 1)

                        def weigh(s):
                            w, hg = steps[s]
                            pe.wait_ge(pT_act, s + 1)
                            pe.wait_ge(pT_dve, s + 1)
                            if s >= 2:
                                pe.wait_ge(o_out, s - 1)
                            first = 0 if w else 1
                            for pair in range(2):
                                for kb in range(first, 2):
                                    for m in (2 * pair, 2 * pair + 1):
                                        h = 4 * hg + m
                                        ins = nc.tensor.matmul(
                                            ps[LD * (m % 2):LD * (m % 2) + LD, 6 + s % 2, pair * P:(pair + 1) * P],
                                            vt[:, w - 1 + kb, h * LD:(h + 1) * LD],
                                            probT[:, s % 2, m, kb * P:(kb + 1) * P],
                                            start=(kb == first), stop=(kb == 1), skip_group_check=True)
                            ins.then_inc(o_mm, 1)

                        pe.wait_ge(tile_act, nth(len(tiles) - 1))
                        pe.wait_ge(rotated, 2 * NT)
                        score(0)
                        score(1)
                        for s in range(len(steps)):
                            turn(s)
                            if s + 2 < len(steps):
                                score(s + 2)
                            weigh(s)
                        pe.wait_ge(o_out, len(steps))
                        for t in range(NT):
                            for n in range(HP):
                                ins = nc.tensor.matmul(ps[:, t // 2, (t % 2) * C:(t % 2 + 1) * C],
                                                       oT[:, n, t * P:(t + 1) * P], wo[:, n, :],
                                                       start=(n == 0), stop=(n == HP - 1))
                            if t % 2:
                                ins.then_inc(wo_mm, 1)
                        pe.wait_ge(hn_done, 1)
                        for c in range(CT):
                            for n in range(NT):
                                ins = nc.tensor.transpose(ps[:, 2 + c, n * P:(n + 1) * P],
                                                          hn[:, n, c * P:(c + 1) * P], k["ident"][:])
                            ins.then_inc(hnT_mm, 1)
                        pe.wait_ge(hnT_out, CT)
                        for i in range(2 * FT):
                            f, part = i // 2, 1 - i % 2
                            rows = P if f < FT - 1 else FR
                            if f >= 2:
                                pe.wait_ge(hid_done, f - 1)
                            at = part * HID + f * P
                            for c in range(CT):
                                ins = nc.tensor.matmul(ps[0:rows, 4 + i % 4, :], w1[:, c, at:at + rows], hnT[:, c, :],
                                                       start=(c == 0), stop=(c == CT - 1))
                            ins.then_inc(up_mm, 1)
                        pe.wait_ge(hid_done, FT)
                        for t in range(NT):
                            for f in range(FT):
                                ins = nc.tensor.matmul(ps[:, t // 2, (t % 2) * C:(t % 2 + 1) * C],
                                                       hid[:, f, t * P:(t + 1) * P], w2[:, f, :],
                                                       start=(f == 0), stop=(f == FT - 1))
                            if t % 2:
                                ins.then_inc(down_mm, 1)
                ph.clear()
        with nc.Block() as block:
            @block.vector
            def _(dve):
                for b in range(B):
                    nc.vector.tensor_tensor(x_all[:, b], x_all[:, b], z_all[:, b], ALU.add)



E = 8
CAP = max(1, int(T / E * 1.25))
HE = 1024
ET = HE // P
EH = E // 2
OFF = 1000.0


def experts(nc, k, x_all, a, out):
    with Phase(nc, "moe") as ph:
        slot_in = ph.sb("slot_in", [P, CT, E, B, CAP])
        y_slot = ph.sb("y_slot", [P, E, B, C])
        place = ph.sb("place", [P, B, NT, E])
        gate = ph.sb("gate", [P, B, NT, E])
        slots, orders = ph.sb("slots", [P, E, CAP]), ph.sb("orders", [P, NT, E])
        before, ones = ph.sb("before", [P, P], BF16), ph.sb("ones", [P, P], BF16)
        b1, b2 = ph.sb("b1", [P, E, ET]), ph.sb("b2", [P, E, C])
        wr, br = ph.sb("wr", [P, CT, E]), ph.sb("br", [P, E])
        w1 = [ph.sb(f"w1_{i}", [P, CT, HE]) for i in range(2)]
        w2 = [ph.sb(f"w2_{i}", [P, ET, C]) for i in range(2)]
        ps = ph.ps("ps", [P, 8, 512])
        w1_in = [nc_sem for nc_sem in (ph.ctx.enter_context(nc.semaphore(f"moe_w1_in{i}")) for i in range(2))]
        w2_in = [nc_sem for nc_sem in (ph.ctx.enter_context(nc.semaphore(f"moe_w2_in{i}")) for i in range(2))]

        w1_pairs = a["L1_ffn_W1"].rearrange("(e i) c h -> e i c h", i=2)
        w2_pairs = a["L1_ffn_W2"].rearrange("(e i) h c -> e i h c", i=2)
        slot_pairs = slot_in[:].rearrange("p c (e i) b s -> p c e i (b s)", i=2)
        y_pairs = y_slot[:].rearrange("p (e i) b c -> p e i b c", i=2)
        b1_pairs = b1[:].rearrange("p (e i) h -> p e i h", i=2)
        b2_pairs = b2[:].rearrange("p (e i) c -> p e i c", i=2)

        def load_w1(sp, e, i):
            sp.dma_start(w1[i][:], w1_pairs[e, i].rearrange("(t p) h -> p t h", p=P)).then_inc(w1_in[i], 16)

        def load_w2(sp, e, i):
            sp.dma_start(w2[i][:], w2_pairs[e, i].rearrange("(t p) c -> p t c", p=P)).then_inc(w2_in[i], 16)

        made, small = ph.sem("made"), ph.sem("small")
        with nc.Block() as block:
            @block.gpsimd
            def _(pool):
                nc.gpsimd.iota(slots[:], pattern=[[0, E], [1, CAP]], base=0, channel_multiplier=0,
                               allow_small_or_imprecise_dtypes=True)
                nc.gpsimd.iota(orders[:], pattern=[[0, NT], [-1, E]], base=E, channel_multiplier=0,
                               allow_small_or_imprecise_dtypes=True)
                nc.gpsimd.memset(ones[:], 1.0).then_inc(made, 1)
                pool.wait_ge(made, 1)
                nc.gpsimd.affine_select(out=before[:], in_=ones[:], compare_op=ALU.is_gt, fill=0.0, base=0,
                                        pattern=[[1, P]], channel_multiplier=-1)

            @block.sync
            def _(sp):
                with nc.allow_non_contiguous_dma(reason="small columns"):
                    parts = [(wr[:], a["L1_ffn_Wr"].rearrange("(t p) e -> p t e", p=P)),
                             (br[:], a["L1_ffn_br"][None, :].to_broadcast([P, E])),
                             (b1[:], a["L1_ffn_b1"].rearrange("e (t p) -> p e t", p=P)),
                             (b2[:], a["L1_ffn_b2"][None, :, :].to_broadcast([P, E, C]))]
                    for dst, src in parts:
                        sp.dma_start(dst, src).then_inc(small, 16)
                for i in range(2):
                    load_w1(sp, 0, i)
                    load_w2(sp, 0, i)
                sp.wait_ge(small, 16 * len(parts))
        ph.clear()

        with ExitStack() as part:
            def sb(name, shape, dt=F32):
                return part.enter_context(nc.sbuf_tensor(f"route_{name}", shape, dt))

            stats, mv, rstd, veps = sb("stats", [P, NT, 6]), sb("mv", [P, NT, 2]), sb("rstd", [P, NT]), sb("veps", [P, NT])
            xn, xnT = sb("xn", [P, NT, C]), sb("xnT", [P, CT, T])
            logit, prob, rest = sb("logit", [P, NT, E]), sb("prob", [P, NT, E]), sb("rest", [P, NT, E])
            same, key, chosen = sb("same", [P, NT, E]), sb("key", [P, NT, E]), sb("chosen", [P, 2, NT, E])
            top, total = sb("top", [P, NT]), sb("total", [P, NT])
            taken, takenb = sb("taken", [P, NT, E]), sb("takenb", [P, NT, E], BF16)
            onehot = sb("onehot", [P, NT, E, CAP])
            ln_done, var_eps, rstd_done, xn_done = (ph.sem(s) for s in ("ln_done", "var_eps", "rstd_done", "xn_done"))
            xT_mm, xT_out, logit_mm, step, exp_done = (ph.sem(s) for s in ("xT_mm", "xT_out", "logit_mm", "step", "exp_done"))
            pos_mm, hot_done, disp_mm, disp_out = (ph.sem(s) for s in ("pos_mm", "hot_done", "disp_mm", "disp_out"))
            PREP = 3
            ROUTE = 17

            def wide(v):
                return v.unsqueeze(2).to_broadcast([P, NT, E])

            with nc.Fori(0, B) as b:
                with nc.Block() as block:
                    @block.gpsimd
                    def _(pool):
                        pool.wait_ge(ln_done, 2 * NT)
                        nc.gpsimd.tensor_scalar(veps[:], mv[:, :, 1], EPS, None, ALU.add).then_inc(var_eps, 1)
                        pool.wait_ge(var_eps, 1)
                        nc.gpsimd.tensor_tensor(rstd[:], veps[:], k["half"][:, 0:NT], ALU.pow).then_inc(rstd_done, 1)

                    @block.vector
                    def _(dve):
                        layernorm_stats(nc, dve, lambda t: x_all[:, b, t, :], stats, mv, ln_done, 0)
                        dve.wait_ge(rstd_done, 1)
                        for t in range(NT):
                            nc.vector.tensor_scalar(xn[:, t], x_all[:, b, t, :], mv[:, t, 0:1], rstd[:, t:t + 1],
                                                    ALU.subtract, ALU.mult).then_inc(xn_done, 1)
                        for c in range(CT):
                            dve.wait_ge(xT_mm, c + 1)
                            nc.vector.tensor_copy(xnT[:, c, :], ps[:, c, :]).then_inc(xT_out, 1)
                        dve.wait_ge(logit_mm, 1)
                        count = [0]

                        def then(ins):
                            count[0] += 1
                            ins.then_inc(step, 1)
                            dve.wait_ge(step, count[0])

                        then(nc.vector.tensor_tensor(logit[:], ps[:, 2, 0:NT * E].rearrange("p (t e) -> p t e", e=E),
                                                     br[:].unsqueeze(1).to_broadcast([P, NT, E]), ALU.add))
                        then(nc.vector.tensor_reduce(top[:], logit[:], AX_X, ALU.max))
                        then(nc.vector.tensor_tensor(logit[:], logit[:], wide(top[:]), ALU.subtract))
                        assert count[0] == PREP
                        dve.wait_ge(exp_done, 1)
                        then(nc.vector.tensor_reduce(total[:], prob[:], AX_X, ALU.add))
                        then(nc.vector.reciprocal(total[:], total[:]))
                        then(nc.vector.tensor_tensor(prob[:], prob[:], wide(total[:]), ALU.mult))
                        for n in range(2):
                            p = prob if n == 0 else rest
                            then(nc.vector.tensor_reduce(top[:], p[:], AX_X, ALU.max))
                            then(nc.vector.tensor_tensor(same[:], p[:], wide(top[:]), ALU.is_equal))
                            then(nc.vector.tensor_tensor(key[:], same[:], orders[:], ALU.mult))
                            then(nc.vector.tensor_reduce(top[:], key[:], AX_X, ALU.max))
                            then(nc.vector.tensor_tensor(chosen[:, n], key[:], wide(top[:]), ALU.is_equal))
                            if n == 0:
                                then(nc.vector.scalar_tensor_tensor(out=rest[:], in0=chosen[:, 0], scalar=-2.0,
                                                                    in1=prob[:], op0=ALU.mult, op1=ALU.add))
                        then(nc.vector.tensor_tensor(taken[:], chosen[:, 0], chosen[:, 1], ALU.add))
                        nc.vector.tensor_tensor(gate[:, b], prob[:], taken[:], ALU.mult)
                        then(nc.vector.tensor_copy(takenb[:], taken[:]))
                        then(nc.vector.tensor_scalar(taken[:], taken[:], -OFF, OFF, ALU.mult, ALU.add))
                        assert count[0] == ROUTE + 3
                        dve.wait_ge(pos_mm, 1)
                        then(nc.vector.tensor_tensor(place[:, b], ps[:, 3, 0:NT * E].rearrange("p (t e) -> p t e", e=E),
                                                     taken[:], ALU.add))
                        for t in range(NT):
                            ins = nc.vector.tensor_tensor(onehot[:, t], slots[:], place[:, b, t, :].unsqueeze(2)
                                                          .to_broadcast([P, E, CAP]), ALU.is_equal)
                        ins.then_inc(hot_done, 1)

                    @block.scalar
                    def _(act):
                        act.wait_ge(step, PREP)
                        nc.scalar.activation(prob[:], logit[:], ACT.Exp).then_inc(exp_done, 1)
                        for i in range(2 * CT):
                            c, half = i // 2, i % 2
                            act.wait_ge(disp_mm, i + 1)
                            nc.scalar.activation(slot_in[:, c, half * EH:(half + 1) * EH, b, :],
                                                 ps[:, 4 + i, 0:EH * CAP].rearrange("p (e s) -> p e s", s=CAP),
                                                 ACT.Copy).then_inc(disp_out, 1)

                    @block.tensor
                    def _(pe):
                        pe.wait_ge(xn_done, NT)
                        for c in range(CT):
                            for t in range(NT):
                                ins = nc.tensor.transpose(ps[:, c, t * P:(t + 1) * P], xn[:, t, c * P:(c + 1) * P],
                                                          k["ident"][:])
                            ins.then_inc(xT_mm, 1)
                        pe.wait_ge(xT_out, CT)
                        for t in range(NT):
                            for c in range(CT):
                                ins = nc.tensor.matmul(ps[:, 2, t * E:(t + 1) * E], xnT[:, c, t * P:(t + 1) * P],
                                                       wr[:, c, :], start=(c == 0), stop=(c == CT - 1))
                        ins.then_inc(logit_mm, 1)
                        pe.wait_ge(step, ROUTE + 2)
                        for t in range(NT):
                            for n in range(t + 1):
                                ins = nc.tensor.matmul(ps[:, 3, t * E:(t + 1) * E], before[:] if n == t else ones[:],
                                                       takenb[:, n, :], start=(n == 0), stop=(n == t))
                        ins.then_inc(pos_mm, 1)
                        pe.wait_ge(hot_done, 1)
                        for i in range(2 * CT):
                            c, half = i // 2, i % 2
                            for t in range(NT):
                                ins = nc.tensor.matmul(ps[:, 4 + i, 0:EH * CAP], xn[:, t, c * P:(c + 1) * P],
                                                       onehot[:, t, half * EH:(half + 1) * EH, :],
                                                       start=(t == 0), stop=(t == NT - 1))
                            ins.then_inc(disp_mm, 1)
                ph.clear()

        with ExitStack() as part:
            hid = [part.enter_context(nc.sbuf_tensor(f"moe_hid{i}", [P, ET, B * CAP], F32)) for i in range(2)]
            up_mm, up_out, down_mm, down_out = (ph.sem(s) for s in ("up_mm", "up_out", "down_mm", "down_out"))
            with nc.Fori(0, E // 2) as e:
                with nc.Block() as block:
                    @block.sync
                    def _(sp):
                        for i in range(2):
                            sp.wait_ge(up_mm, ET * (i + 1))
                            load_w1(sp, (e + 1) % (E // 2), i)
                            sp.wait_ge(down_mm, B * (i + 1))
                            load_w2(sp, (e + 1) % (E // 2), i)

                    @block.tensor
                    def _(pe):
                        for i in range(2):
                            pe.wait_ge(w1_in[i], e * 16 + 16)
                            for n in range(ET):
                                m = i * ET + n
                                if m >= 4:
                                    pe.wait_ge(up_out, m - 3)
                                for c in range(CT):
                                    ins = nc.tensor.matmul(ps[:, m % 4, 0:B * CAP], w1[i][:, c, n * P:(n + 1) * P],
                                                           slot_pairs[:, c, e, i, :],
                                                           start=(c == 0), stop=(c == CT - 1))
                                ins.then_inc(up_mm, 1)
                            pe.wait_ge(w2_in[i], e * 16 + 16)
                            pe.wait_ge(up_out, ET * (i + 1))
                            for b in range(B):
                                m = i * B + b
                                if m >= 4:
                                    pe.wait_ge(down_out, m - 3)
                                for n in range(ET):
                                    ins = nc.tensor.matmul(ps[0:CAP, 4 + m % 4, 0:C], hid[i][:, n, b * CAP:(b + 1) * CAP],
                                                           w2[i][:, n, :], start=(n == 0), stop=(n == ET - 1))
                                ins.then_inc(down_mm, 1)

                    @block.scalar
                    def _(act):
                        for m in range(2 * ET):
                            i, n = m // ET, m % ET
                            act.wait_ge(up_mm, m + 1)
                            nc.scalar.activation(hid[i][:, n, :], ps[:, m % 4, 0:B * CAP], ACT.Relu,
                                                 bias=b1_pairs[:, e, i, n:n + 1]).then_inc(up_out, 1)

                    @block.vector
                    def _(dve):
                        for m in range(2 * B):
                            i, b = m // B, m % B
                            dve.wait_ge(down_mm, m + 1)
                            nc.vector.tensor_tensor(y_pairs[0:CAP, e, i, b, :], ps[0:CAP, 4 + m % 4, 0:C],
                                                    b2_pairs[0:CAP, e, i, :], ALU.add).then_inc(down_out, 1)
                ph.clear()

        with nc.Block() as block:
            @block.sync
            def _(sp):
                for i in range(2):
                    sp.wait_ge(w1_in[i], 16 * (E // 2 + 1))
                    sp.wait_ge(w2_in[i], 16 * (E // 2 + 1))

        with ExitStack() as part:
            hot, pick = (part.enter_context(nc.sbuf_tensor(f"moe_{n}", [P, 2, E, CAP], F32)) for n in ("hot", "pick"))
            pickT = part.enter_context(nc.sbuf_tensor("moe_pickT", [P, 2, E, P], F32))
            fin = part.enter_context(nc.sbuf_tensor("moe_fin", [P, NT, C], F32))
            hot_ok, pick_ok, turn_mm, turn_act, turn_dve, sum_mm, fin_ok, stored = (
                ph.sem(s) for s in ("hot_ok", "pick_ok", "turn_mm", "turn_act", "turn_dve", "sum_mm", "fin_ok", "stored"))
            with nc.Fori(0, B) as b:
                with nc.Block() as block:
                    @block.vector
                    def _(dve):
                        def choose(t):
                            if t >= 2:
                                dve.wait_ge(turn_mm, t - 1)
                            nc.vector.tensor_tensor(hot[:, t % 2], slots[:], place[:, b, t, :].unsqueeze(2)
                                                    .to_broadcast([P, E, CAP]), ALU.is_equal).then_inc(hot_ok, 1)
                            dve.wait_ge(hot_ok, t + 1)
                            nc.vector.tensor_tensor(pick[:, t % 2], hot[:, t % 2], gate[:, b, t, :].unsqueeze(2)
                                                    .to_broadcast([P, E, CAP]), ALU.mult).then_inc(pick_ok, 1)

                        choose(0)
                        for t in range(NT):
                            if t + 1 < NT:
                                choose(t + 1)
                            dve.wait_ge(turn_mm, t + 1)
                            if t >= 2:
                                dve.wait_ge(sum_mm, t - 1)
                            nc.vector.tensor_copy(pickT[0:CAP, t % 2, EH:E, :], ps[0:CAP, 2 * (t % 2) + 1, :]
                                                  .rearrange("p (e t) -> p e t", t=P)).then_inc(turn_dve, 1)
                            dve.wait_ge(sum_mm, t + 1)
                            nc.vector.tensor_tensor(fin[:, t, :], ps[:, 4 + t % 2, 0:C], x_all[:, b, t, :], ALU.add) \
                              .then_inc(fin_ok, 1)

                    @block.scalar
                    def _(act):
                        for t in range(NT):
                            act.wait_ge(turn_mm, t + 1)
                            if t >= 2:
                                act.wait_ge(sum_mm, t - 1)
                            nc.scalar.activation(pickT[0:CAP, t % 2, 0:EH, :], ps[0:CAP, 2 * (t % 2), :]
                                                 .rearrange("p (e t) -> p e t", t=P), ACT.Copy).then_inc(turn_act, 1)

                    @block.tensor
                    def _(pe):
                        def turn(t):
                            pe.wait_ge(pick_ok, t + 1)
                            if t >= 2:
                                pe.wait_ge(turn_act, t - 1)
                                pe.wait_ge(turn_dve, t - 1)
                            for n in range(E):
                                ins = nc.tensor.transpose(ps[0:CAP, 2 * (t % 2) + n // EH, (n % EH) * P:(n % EH + 1) * P],
                                                          pick[:, t % 2, n, :], k["ident"][:])
                            ins.then_inc(turn_mm, 1)

                        turn(0)
                        for t in range(NT):
                            if t + 1 < NT:
                                turn(t + 1)
                            pe.wait_ge(turn_act, t + 1)
                            pe.wait_ge(turn_dve, t + 1)
                            if t >= 2:
                                pe.wait_ge(fin_ok, t - 1)
                            for n in range(E):
                                ins = nc.tensor.matmul(ps[:, 4 + t % 2, 0:C], pickT[0:CAP, t % 2, n, :],
                                                       y_slot[0:CAP, n, b, :], start=(n == 0), stop=(n == E - 1))
                            ins.then_inc(sum_mm, 1)

                    @block.sync
                    def _(sp):
                        sp.wait_ge(fin_ok, NT)
                        sp.dma_start(out[b].rearrange("(t p) c -> p t c", p=P), fin[:]).then_inc(stored, 16)
                        sp.wait_ge(stored, 16)
                ph.clear()


def load_stream(nc, ph, x_all, x):
    loaded = ph.sem("x_loaded")
    with nc.Block() as block:
        @block.sync
        def _(sp):
            sp.dma_start(x_all[:], x.rearrange("b (t p) c -> p b t c", p=P)).then_inc(loaded, 16)
            sp.wait_ge(loaded, 16)
    ph.clear()


def program(nc, a, out):
    with Phase(nc, "all") as ph:
        x_all = ph.sb("x_all", [P, B, NT, C])
        k = setup_constants(nc, ph)
        load_stream(nc, ph, x_all, a["x"])
        def wide(l, q, kk, v, o, bo, bq, bk, bv):
            g = lambda n: a[f"L{l}_xattn_{n}"]
            return dict(wq=g(q), wk=g(kk), wv=g(v), wo=g(o), bq=g(bq), bk=g(bk), bv=g(bv), bo=g(bo) if bo else None)
        wide_attention(nc, k, x_all, "self", a["x"], None,
                       wide(0, "Wq", "Wk", "Wv", "Wp", None, "bq", "bk", "bv"), True)
        wide_attention(nc, k, x_all, "cross", a["x"], a["ctx_512"],
                       wide(0, "Wcq", "Wck", "Wcv", "Wp", "bp", "bcq", "bck", "bcv"), False)
        local_layers(nc, k, x_all, a)
        wide_attention(nc, k, x_all, "late", None, a["ctx_512"],
                       wide(1, "Wq", "Wk", "Wv", "Wo", "bo", "bq", "bk", "bv"), False)
        experts(nc, k, x_all, a, out)


_OUT = ((B, T, C), "float32")


def kernel(**inputs):
    import concourse.bacc as _bacc
    from concourse.bass_utils import run_bass_kernel_spmd as _run

    nc = _bacc.Bacc("TRN2", target_bir_lowering=False, num_devices=1)
    arrays, handles = {}, {}
    for name, value in {**inputs, **constants()}.items():
        value = np.ascontiguousarray(value)
        arrays[f"in_{name}_dram"] = value
        handles[name] = nc.dram_tensor(f"in_{name}_dram", value.shape, mybir.dt.from_np(value.dtype),
                                       kind="ExternalInput").ap()
    out = nc.dram_tensor("out_0_dram", _OUT[0], mybir.dt.from_np(np.dtype(_OUT[1])), kind="ExternalOutput").ap()
    program(nc, handles, out)
    return _run(nc, [arrays], core_ids=[0]).results[0]["out_0_dram"]
```

```python
from contextlib import ExitStack

import numpy as np

import concourse.bass as bass
from concourse import mybir

F32 = mybir.dt.float32
BF16 = mybir.dt.bfloat16
ALU = mybir.AluOpType
ACT = mybir.ActivationFunctionType
AX_X = mybir.AxisListType.X

P = 128
B, T, C = 4, 512, 256
NT = T // P
CT = C // P
H, D = 16, 16
HG = 4
NG = H // HG
TC, CC = 1601, 128
NEG = -1e30
EPS = 1e-5
QPAIR = "aabbac"
KPAIR = "ababca"
RM = 16 * len(QPAIR)
KROWS = RM + 3
S1_RING = 3
S2_RING = 3
AV_BANK = 6
AUX_BANK = 7
OWN_BANKS = [0, 1, 2, AUX_BANK]
PROBS = 8
PIECES = 2
PACKED = 16 * len(QPAIR)


class Phase:

    def __init__(self, nc, name):
        self.nc, self.name, self.ctx, self.sems = nc, name, ExitStack(), []

    def __enter__(self):
        self.ctx.__enter__()
        return self

    def __exit__(self, *a):
        return self.ctx.__exit__(*a)

    def sb(self, name, shape, dt=F32):
        return self.ctx.enter_context(self.nc.sbuf_tensor(f"{self.name}_{name}", shape, dt))

    def ps(self, name, shape, dt=F32):
        return self.ctx.enter_context(self.nc.psum_tensor(f"{self.name}_{name}", shape, dt))

    def sem(self, name):
        s = self.ctx.enter_context(self.nc.semaphore(f"{self.name}_{name}"))
        self.sems.append(s)
        return s

    def clear(self):
        self.nc.all_engine_barrier()
        for n, s in enumerate(self.sems):
            (self.nc.sync, self.nc.gpsimd)[n % 2].sem_clear(s)
        self.nc.all_engine_barrier()


def chunks(n, size):
    return [(i, min(size, n - i)) for i in range(0, n, size)]


def setup_constants(nc, ph):
    k = {
        "ident": ph.sb("ident", [P, P]), "identb": ph.sb("identb", [P, P], BF16),
        "q_from_k": ph.sb("q_from_k", [P, P], BF16), "k_from_q": ph.sb("k_from_q", [P, 2 * P], BF16),
        "sum_rows": ph.sb("sum_rows", [P, P], BF16), "onesb": ph.sb("onesb", [P, P], BF16), "half": ph.sb("half", [P, NT * 16]),
    }
    made = ph.sem("made")
    with nc.Block() as block:
        @block.gpsimd
        def _(pool):
            nc.gpsimd.memset(k["ident"][:], 0.0).then_inc(made, 1)
            nc.gpsimd.memset(k["q_from_k"][:], 0.0).then_inc(made, 1)
            nc.gpsimd.memset(k["k_from_q"][:], 0.0).then_inc(made, 1)
            nc.gpsimd.memset(k["half"][:], -0.5).then_inc(made, 1)
            pool.wait_ge(made, 4)
            nc.gpsimd.affine_select(out=k["ident"][:], in_=k["ident"][:], compare_op=ALU.not_equal, fill=1.0,
                                    base=0, pattern=[[-1, P]], channel_multiplier=1).then_inc(made, 1)
            nc.gpsimd.affine_select(out=k["q_from_k"][:], in_=k["q_from_k"][:], compare_op=ALU.is_ge, fill=NEG,
                                    base=0, pattern=[[1, P]], channel_multiplier=-1).then_inc(made, 1)
            nc.gpsimd.affine_select(out=k["k_from_q"][:, 0:P], in_=k["k_from_q"][:, 0:P], compare_op=ALU.is_ge,
                                    fill=NEG, base=0, pattern=[[1, P]], channel_multiplier=-1).then_inc(made, 1)
            nc.gpsimd.affine_select(out=k["k_from_q"][:, P:2 * P], in_=k["k_from_q"][:, P:2 * P],
                                    compare_op=ALU.is_ge, fill=NEG, base=0, pattern=[[-1, P]],
                                    channel_multiplier=1).then_inc(made, 1)
            pool.wait_ge(made, 8)
            nc.gpsimd.memset(k["sum_rows"][:], 0.0).then_inc(made, 1)
            nc.gpsimd.memset(k["onesb"][:], 1.0)
            pool.wait_ge(made, 9)
            nc.gpsimd.memset(k["sum_rows"][:].rearrange("p (j r) -> p j r", r=32)[:, :, D:D + 1], 1.0 / P)
            nc.gpsimd.tensor_copy(k["identb"][:], k["ident"][:]).then_inc(made, 1)
            pool.wait_ge(made, 10)
    ph.clear()
    return k


def layernorm_stats(nc, dve, src, stats, mv, counted, first):
    for t in range(NT):
        nc.vector.bn_stats(stats[:, t], src(t)).then_inc(counted, 1)
    for t in range(NT):
        dve.wait_ge(counted, first + t + 1)
        nc.vector.bn_aggr(mv[:, t], stats[:, t]).then_inc(counted, 1)


def wide_attention(nc, k, x_all, name, src_dram, ctx_dram, w, causal):
    nk = T if causal else TC
    ktiles = chunks(nk, P)
    KT = len(ktiles)
    kchunks = chunks(nk, T if causal else 401)
    kvc = CT if causal else 1
    n_s1 = HG * NT * len(kchunks)
    NCH = len(kchunks)

    with Phase(nc, name) as ph:
        wq, wo = ph.sb("wq", [P, CT, C]), ph.sb("wo", [P, NG, C])
        wk, wv = ph.sb("wk", [P, kvc, C]), ph.sb("wv", [P, kvc, C])
        bq, bk = ph.sb("bq", [P, CT]), ph.sb("bk", [P, CT])
        bv, bo = ph.sb("bv", [P, C]), ph.sb("bo", [P, C])
        prob = ph.sb("prob", [P, 8, T])
        sums, den, rden = (ph.sb(n, [P, T]) for n in ("sums", "den", "rden"))
        xs = ph.sb("xs", [P, NT, C])
        xn, xnT = ph.sb("xn", [P, NT, C]), ph.sb("xnT", [P, CT, T])
        stats, mv, rstd = ph.sb("stats", [P, NT, 6]), ph.sb("mv", [P, NT, 2]), ph.sb("rstd", [P, NT])
        veps = ph.sb("veps", [P, NT])
        qparts, kparts = ph.sb("qparts", [P, CT, 3, T], BF16), ph.sb("kparts", [P, CT, 3, nk], BF16)
        qspill = nc.dram_tensor(f"{name}_qspill", [CT, P, 3, T], BF16).ap()
        kspill = nc.dram_tensor(f"{name}_kspill", [CT, P, 3, nk], BF16).ap()
        whole, rest = ph.sb("whole", [P, 2, T]), ph.sb("rest", [P, 2, T])
        qpack, kpack = ph.sb("qpack", [P, H, T], BF16), ph.sb("kpack", [P, H, nk], BF16)
        vals = ph.sb("vals", [P, KT, H, D + 1])
        y = ph.sb("y", [P, NG, T])
        mx, mxc, mrest = ph.sb("mx", [P, HG * NT, NCH]), ph.sb("mxc", [P, HG * NT]), ph.sb("mrest", [P, HG * NT])
        m3 = ph.sb("m3", [P, HG * NT, 3], BF16)
        if not causal:
            ctx_tok = ph.sb("ctx_tok", [P, KT, CC])
            ctxT = ph.sb("ctxT", [P, TC])
        ps = ph.ps("ps", [P, 8, 512])

        zeroed, loaded, qkv_in, biases, one_head = (
            ph.sem(s) for s in ("zeroed", "loaded", "qkv_in", "biases", "one_head"))
        av_set, scaled, set_up = (ph.sem(s) for s in ("av_set", "scaled", "set_up"))
        n_loads = HG + (w["bo"] is not None)

        def set_up_pool(pool):
            nc.gpsimd.memset(wo[:], 0.0).then_inc(zeroed, 1)
            nc.gpsimd.memset(y[:], 0.0).then_inc(set_up, 1)

        def set_up_pe(pe):
            for i in range(NT):
                ins = nc.tensor.matmul(ps[:, AV_BANK, i * P:(i + 1) * P], k["sum_rows"][:], k["onesb"][:],
                                       start=True, stop=True)
            ins.then_inc(av_set, 1)

        def set_up_act(act):
            act.wait_ge(av_set, 1)
            nc.scalar.activation(sums[:], ps[:, AV_BANK, :], ACT.Copy)
            act.wait_ge(scaled, 1)

        def set_up_dve(dve):
            nc.vector.memset(kpack[RM:RM + 32, 0, :], 1.0).then_inc(one_head, 1)
            dve.wait_ge(biases, 32)
            nc.vector.tensor_scalar(bq[:], bq[:], 0.25, None, ALU.mult).then_inc(scaled, 1)

        def set_up_values(dve):
            nc.vector.memset(vals[:], 1.0).then_inc(set_up, 1)

        def set_up_loads(sp):
            with nc.allow_non_contiguous_dma(reason="bias columns"):
                sp.dma_start(bq[:], w["bq"].rearrange("(t p) -> p t", p=P)).then_inc(biases, 16)
                sp.dma_start(bk[:], w["bk"].rearrange("(t p) -> p t", p=P)).then_inc(biases, 16)
            for dst, src in ((wq, w["wq"]), (wk, w["wk"]), (wv, w["wv"])):
                sp.dma_start(dst[:], src.rearrange("(t p) c -> p t c", p=P)).then_inc(qkv_in, 16)
            sp.dma_start(bv[:], w["bv"][None, :].to_broadcast([P, C])).then_inc(qkv_in, 16)
            if w["bo"] is not None:
                sp.dma_start(bo[:], w["bo"][None, :].to_broadcast([P, C])).then_inc(loaded, 16)
            sp.wait_ge(zeroed, 1)
            heads = w["wo"].rearrange("(g j d) c -> j d g c", j=HG, d=D)
            for j in range(HG):
                sp.dma_start(wo[32 * j:32 * j + D, :, :], heads[j]).then_inc(loaded, 16)
            sp.wait_ge(one_head, 1)
            sp.dma_start(kpack[RM:KROWS, 1:H, :], kpack[RM:KROWS, 0:1, :].to_broadcast([3, H - 1, nk])) \
              .then_inc(set_up, 16)

        src_in, ctx_in = ph.sem("src_in"), ph.sem("ctx_in")
        ln_done, var_eps, rstd_done, xn_done = (ph.sem(s) for s in ("ln_done", "var_eps", "rstd_done", "xn_done"))
        aux_mm, aux_act, aux_dve = ph.sem("aux_mm"), ph.sem("aux_act"), ph.sem("aux_dve")
        part_a, part_r, part_b, part_c = (ph.sem(f"part_{s}") for s in "arbc")
        packed = {(n, c): ph.sem(f"packed_{n}{c}") for n in "qk" for c in range(CT)}
        spilled = {(n, c): ph.sem(f"spilled_{n}{c}") for n in "qk" for c in range(CT)}
        s1_mm, s1_max, max_split = ph.sem("s1_mm"), ph.sem("s1_max"), ph.sem("max_split")
        s2_mm, exp_done, av_mm = ph.sem("s2_mm"), ph.sem("exp_done"), ph.sem("av_mm")
        sums_out, spread, inverted, normed = (ph.sem(s) for s in ("sums_out", "spread", "inverted", "normed"))

        def values_jobs(c):
            return [(("v", (c, j)), "dve") for j in range((KT + 3) // 4)]

        def parts_jobs(c):
            return [(("q", c), "act")] + [(("k", (c, n)), "act") for n in range(NCH)]

        turned_jobs = [(("xT", c), "act") for c in range(CT)]
        if not causal:
            turned_jobs += [(("cT", j), "act") for j in range((KT + 3) // 4)]
        kv_ready = turned_jobs[-1][0]

        def maxima_jobs(g):
            return [(("mx", g), "act")]

        out_jobs = [(("o", j), "dve") for j in range(NT // 2)]

        group_s1 = [(h, qt, ch) for h in range(HG) for qt in range(NT) for ch in range(NCH)]

        def s1_cols(qt, ch):
            return (0, (qt + 1) * P) if causal else kchunks[ch]

        def turn(b, prev, ahead, banks, opening=False, closing=False):
            attend = b is not None
            steps = NG * KT if attend else 0
            jobs = {s: [] for s in range(-1, steps + 1)}
            if attend:
                for n, job in enumerate(values_jobs(1)):
                    jobs[n * KT // 4].append(job)
                for g in range(1, NG):
                    jobs[g * KT - 2] += maxima_jobs(g)
            if ahead is not None:
                work = turned_jobs + parts_jobs(0) + parts_jobs(1)
                if attend:
                    first, last = KT, 2 * KT + max(KT - 4, 1)
                    for n, job in enumerate(work):
                        jobs[first + n * (last - first) // len(work)].append(job)
                    for n, job in enumerate(values_jobs(0)):
                        jobs[3 * KT - 2 + n * KT // 5].append(job)
                    jobs[steps - 2] += maxima_jobs(0)
                else:
                    jobs[-1] = work + values_jobs(0)
                    jobs[0] = jobs.get(0, []) + maxima_jobs(0)
            if attend:
                for n, job in enumerate(out_jobs):
                    jobs[KT + 1 + 2 * n].append(job)
            if closing:
                jobs[steps].append((("own", 0), "dve"))
            if attend and KT > 4:
                for s in range(steps - 1):
                    jobs[s].sort(key=lambda job: job[0][0] != "mx")
                    jobs[s + 1][0:0] = jobs[s][1:]
                    del jobs[s][1:]
            defer = KT > 4
            at_once = {s: jobs[s][:-1] if defer else jobs[s] for s in jobs}
            later = {s: jobs[s - 1][-1:] if s and defer else [] for s in range(0, steps + 1)}
            order = [j for s in range(-1, steps + 1) for j in jobs[s]]
            number = {job: i for i, (job, _) in enumerate(order)}
            units = [job for job, _ in order if job[0] in "qk"]
            unit_no = {u: i for i, u in enumerate(units)}
            unit_step = {job: s for s in jobs for job, _ in jobs[s]}
            taken = {"act": aux_act, "dve": aux_dve}

            def out_of(job):
                i = number[job]
                return taken[order[i][1]], sum(who == order[i][1] for _, who in order[:i + 1])

            def bank_of(job):
                return ps[:, banks[number[job] % len(banks)], :]

            def unit_parts(u):
                if u[0] == "q":
                    return qparts[:, u[1]], 0, T
                (c, n) = u[1]
                return kparts[:, c], *kchunks[n]

            targets = ([*range(1, NG)] if attend else []) + ([0] if ahead is not None else [])
            if attend:
                lo, hi = 0, KT - 2
                s1_at = {(g, kt): range((kt - lo) * n_s1 // (hi - lo), (kt - lo + 1) * n_s1 // (hi - lo))
                         for g in range(len(targets)) for kt in range(lo, hi)}

            def src(t):
                return x_all[:, ahead, t, :] if src_dram is None else xs[:, t, :]

            with nc.Block() as block:
                @block.sync
                def _(sp):
                    def pack(c, fresh):
                        for kind, parts, spill, dst, pairs in (("q", qparts, qspill, qpack, QPAIR),
                                                               ("k", kparts, kspill, kpack, KPAIR)):
                            if fresh:
                                last = ("q", c) if kind == "q" else ("k", (c, NCH - 1))
                                sp.wait_ge(part_a, unit_no[last] + 1)
                                sp.wait_ge(part_b, unit_no[last] + 1)
                                sp.wait_ge(part_c, unit_no[last] + 1)
                            sp.dma_start(spill[c], parts[:, c]).then_inc(spilled[kind, c], 16)
                            sp.wait_ge(spilled[kind, c], 16)
                            if fresh and attend and kind == "q":
                                sp.wait_ge(s2_mm, 2 * KT * HG)
                            for row, part in enumerate(pairs):
                                sp.dma_start(dst[row * D:(row + 1) * D, 8 * c:8 * c + 8, :],
                                             spill[c, :, "abc".index(part), :].rearrange("(h d) n -> d h n", d=D)) \
                                  .then_inc(packed[kind, c], 16)

                    if ahead is not None and src_dram is not None:
                        sp.dma_start(xs[:], src_dram[ahead].rearrange("(t p) c -> p t c", p=P)).then_inc(src_in, 16)
                    if ahead is not None and not causal:
                        full = (KT - 1) * P
                        sp.dma_start(ctx_tok[:, 0:KT - 1, :], ctx_dram[ahead, 0:full, :]
                                     .rearrange("(k p) c -> p k c", p=P)).then_inc(ctx_in, 16)
                        sp.dma_start(ctx_tok[0:TC - full, KT - 1, :], ctx_dram[ahead, full:TC, :]).then_inc(ctx_in, 16)
                    if opening:
                        set_up_loads(sp)
                    if attend:
                        pack(1, False)
                    if ahead is not None:
                        pack(0, True)
                        for kind in "qk":
                            sp.wait_ge(packed[kind, 0], PACKED)
                    if opening:
                        sp.wait_ge(loaded, 16 * n_loads)
                        sp.wait_ge(one_head, 1)
                        sp.wait_ge(set_up, 18)

                @block.gpsimd
                def _(pool):
                    def divide(slot):
                        pool.wait_ge(inverted, PIECES * (slot + 1))
                        nc.gpsimd.tensor_tensor(y[:, (slot - 1) % NG, :], sums[:], rden[:], ALU.mult).then_inc(normed, 1)

                    if opening:
                        set_up_pool(pool)
                    if attend and w["bo"] is not None:
                        xb = x_all[:, b, :, :]
                        nc.gpsimd.tensor_tensor(xb, xb, bo[:].unsqueeze(1).to_broadcast([P, NT, C]), ALU.add)
                    divided = 0
                    if ahead is not None:
                        pool.wait_ge(ln_done, 2 * NT)
                        nc.gpsimd.tensor_scalar(veps[:], mv[:, :, 1], EPS, None, ALU.add).then_inc(var_eps, 1)
                        pool.wait_ge(var_eps, 1)
                        nc.gpsimd.tensor_tensor(rstd[:], veps[:], k["half"][:, 0:NT], ALU.pow).then_inc(rstd_done, 1)
                        for u, unit in enumerate(units):
                            ready = unit_step[units[min(u + 1, len(units) - 1)]] + (1 if defer else 0)
                            while attend and divided < NG and ready >= (divided + 1) * KT:
                                divide(divided)
                                divided += 1
                            parts, at, n = unit_parts(unit)
                            pool.wait_ge(part_b, u + 1)
                            nc.gpsimd.tensor_tensor(parts[:, 2, at:at + n], rest[:, u % 2, 0:n],
                                                    parts[:, 1, at:at + n], ALU.subtract).then_inc(part_c, 1)
                    while attend and divided < NG:
                        divide(divided)
                        divided += 1
                    if closing:
                        divide(NG)

                @block.scalar
                def _(act):
                    def second_part(u):
                        parts, at, n = unit_parts(units[u])
                        act.wait_ge(part_r, u + 1)
                        nc.scalar.activation(parts[:, 1, at:at + n], rest[:, u % 2, 0:n], ACT.Copy) \
                          .then_inc(part_b, 1)

                    def take(job):
                        what, j = job
                        act.wait_ge(aux_mm, number[job] + 1)
                        bank = bank_of(job)
                        if what == "xT":
                            nc.scalar.activation(xnT[:, j, :], bank, ACT.Copy).then_inc(aux_act, 1)
                        elif what == "cT":
                            at, n = j * 512, min(512, TC - j * 512)
                            nc.scalar.activation(ctxT[:, at:at + n], bank[:, 0:n], ACT.Copy).then_inc(aux_act, 1)
                        elif what == "mx":
                            for h in range(HG):
                                ins = nc.scalar.activation(qpack[RM:RM + 3, j * HG + h, :],
                                                           bank[32 * h:32 * h + 3, :], ACT.Copy)
                            ins.then_inc(aux_act, 1)
                        else:
                            u = unit_no[job]
                            parts, at, n = unit_parts(job)
                            if u >= 2:
                                act.wait_ge(part_r, u - 1)
                            if what == "k" and attend and j[0] == 1:
                                act.wait_ge(spilled["k", 1], 16)
                            if what == "q" and attend and j == 1:
                                act.wait_ge(spilled["q", 1], 16)
                            bias, scale = (bq[:, j:j + 1], 0.25) if what == "q" else (bk[:, j[0]:j[0] + 1], 1.0)
                            nc.scalar.activation(parts[:, 0, at:at + n], bank[:, 0:n], ACT.Identity, bias=bias,
                                                 scale=scale).then_inc(part_a, 1)
                            nc.scalar.activation(whole[:, u % 2, 0:n], bank[:, 0:n], ACT.Identity, bias=bias,
                                                 scale=scale).then_inc(aux_act, 1)
                            if u:
                                second_part(u - 1)
                            if u == len(units) - 1:
                                second_part(u)

                    def take_sums(g):
                        act.wait_ge(av_mm, (g + 1) * KT)
                        if g or prev is not None:
                            act.wait_ge(normed, g + 1)
                        nc.scalar.activation(sums[:], ps[:, AV_BANK, :], ACT.Copy).then_inc(sums_out, 1)

                    def take_all(some):
                        for job, who in some:
                            if who == "act":
                                take(job)

                    if opening:
                        set_up_act(act)
                    take_all(jobs[-1])
                    if not attend:
                        take_all(jobs[0])
                    for s in range(steps):
                        g, kt = divmod(s, KT)
                        at, n = ktiles[kt]
                        q0 = at if causal else 0
                        for m in range(HG):
                            i = HG * s + m
                            act.wait_ge(s2_mm, i + 1)
                            if i >= PROBS:
                                act.wait_ge(av_mm, (i - PROBS) // HG + 1)
                            nc.scalar.activation(prob[0:n, i % PROBS, q0:T],
                                                 ps[0:n, S1_RING + i % S2_RING, q0:T], ACT.Exp) \
                              .then_inc(exp_done, 1)
                            if m == 1:
                                take_all(later[s])
                        if kt == 0 and g:
                            take_sums(g - 1)
                        take_all(at_once[s])
                    if attend:
                        take_all(later[steps])
                        take_sums(NG - 1)

                @block.vector
                def _(dve):
                    def norm():
                        if src_dram is not None:
                            dve.wait_ge(src_in, 16)
                        layernorm_stats(nc, dve, src, stats, mv, ln_done, 0)
                        dve.wait_ge(rstd_done, 1)
                        for t in range(NT):
                            nc.vector.tensor_scalar(xn[:, t], src(t), mv[:, t, 0:1], rstd[:, t:t + 1], ALU.subtract,
                                                    ALU.mult).then_inc(xn_done, 1)

                    def take(job):
                        what, j = job
                        if what in "qk":
                            u = unit_no[job]
                            parts, at, n = unit_parts(job)
                            dve.wait_ge(*out_of(job))
                            if u >= 2:
                                dve.wait_ge(part_c, u - 1)
                            nc.vector.tensor_tensor(rest[:, u % 2, 0:n], whole[:, u % 2, 0:n],
                                                    parts[:, 0, at:at + n], ALU.subtract).then_inc(part_r, 1)
                        if what == "own":
                            dve.wait_ge(aux_mm, number[job] + 1)
                            for t in range(NT):
                                xb = x_all[:, b, t, :]
                                nc.vector.tensor_tensor(xb, ps[:, OWN_BANKS[t], 0:C], xb, ALU.add)
                        if what == "o":
                            dve.wait_ge(aux_mm, number[job] + 1)
                            xb = x_all[:, prev, 2 * j:2 * j + 2, :]
                            nc.vector.tensor_tensor(xb, bank_of(job).rearrange("p (t c) -> p t c", c=C), xb,
                                                    ALU.add).then_inc(aux_dve, 1)
                        if what != "v":
                            return
                        dve.wait_ge(aux_mm, number[job] + 1)
                        c, j = j
                        if c == 0 and attend:
                            dve.wait_ge(av_mm, 2 * KT)
                        for n, kt in enumerate(range(4 * j, min(4 * j + 4, KT))):
                            rows = ktiles[kt][1]
                            ins = nc.vector.tensor_tensor(
                                vals[0:rows, kt, 8 * c:8 * c + 8, 0:D],
                                bank_of(job)[0:rows, n * P:(n + 1) * P].rearrange("p (h d) -> p h d", d=D),
                                bv[0:rows, c * P:(c + 1) * P].rearrange("p (h d) -> p h d", d=D), ALU.add)
                        ins.then_inc(aux_dve, 1)

                    def maximum(slot, i):
                        h, qt, ch = group_s1[i]
                        n = slot * n_s1 + i
                        cols = s1_cols(qt, ch)[1]
                        dve.wait_ge(s1_mm, n + 1)
                        nc.vector.tensor_reduce(mx[:, h * NT + qt, ch:ch + 1], ps[:, n % S1_RING, 0:cols], AX_X,
                                                ALU.max).then_inc(s1_max, 1)

                    def split(slot):
                        dve.wait_ge(s1_max, (slot + 1) * n_s1)
                        nc.vector.tensor_reduce(mxc[:], mx[:], AX_X, ALU.max).then_inc(max_split, 1)
                        dve.wait_ge(max_split, 5 * slot + 1)
                        if slot:
                            last = ("mx", targets[slot - 1])
                            dve.wait_ge(aux_mm, number[last] + 1)
                        nc.vector.tensor_scalar(m3[:, :, 0], mxc[:], -1.0, None, ALU.mult).then_inc(max_split, 1)
                        dve.wait_ge(max_split, 5 * slot + 2)
                        nc.vector.scalar_tensor_tensor(out=mrest[:], in0=mxc[:], scalar=-1.0, in1=m3[:, :, 0],
                                                       op0=ALU.mult, op1=ALU.subtract).then_inc(max_split, 1)
                        dve.wait_ge(max_split, 5 * slot + 3)
                        nc.vector.tensor_copy(m3[:, :, 1], mrest[:]).then_inc(max_split, 1)
                        dve.wait_ge(max_split, 5 * slot + 4)
                        nc.vector.tensor_tensor(m3[:, :, 2], mrest[:], m3[:, :, 1], ALU.subtract) \
                          .then_inc(max_split, 1)

                    def invert(slot, n):
                        if n == 0:
                            if slot:
                                dve.wait_ge(sums_out, slot)
                                dve.wait_ge(inverted, PIECES * slot)
                            nc.vector.stream_shuffle(den[:], sums[:], [D] * 32).then_inc(spread, 1)
                            return
                        cols = slice((n - 1) * T // PIECES, n * T // PIECES)
                        dve.wait_ge(spread, slot + 1)
                        if slot:
                            dve.wait_ge(normed, slot)
                        nc.vector.reciprocal(rden[:, cols], den[:, cols]).then_inc(inverted, 1)

                    norm_step = max(KT - 2, 2)
                    if opening:
                        set_up_dve(dve)
                    if not attend and ahead is not None:
                        norm()
                        set_up_values(dve)
                        for job, _ in jobs[-1]:
                            take(job)
                        for i in range(n_s1):
                            maximum(0, i)
                        split(0)
                    for s in range(steps):
                        g, kt = divmod(s, KT)
                        if s == norm_step and ahead is not None:
                            norm()
                        mine = s1_at.get((g, kt), ()) if g < len(targets) else ()
                        for n, i in enumerate(mine):
                            maximum(g, i)
                            if n == 1:
                                for job, _ in later[s]:
                                    if job[0] in "vo":
                                        take(job)
                        for job, _ in later[s]:
                            if job[0] not in "vo" or len(mine) < 2:
                                take(job)
                        if g < len(targets) and kt == KT - 3:
                            split(g)
                        for job, _ in at_once[s]:
                            take(job)
                        if kt >= KT - 2:
                            half = PIECES // 2 + 1
                            for n in (range(half) if kt == KT - 2 else range(half, PIECES + 1)):
                                invert(g, n)
                    for job, _ in (later[steps] if attend else ()):
                        take(job)
                    if closing:
                        for n in range(PIECES + 1):
                            invert(NG, n)
                        for job, _ in jobs[steps]:
                            take(job)

                @block.tensor
                def _(pe):
                    kv = xnT if causal else ctxT[:].unsqueeze(1) if not causal else None

                    def make(job, fill=lambda: None):
                        what, j = job
                        i = number[job]
                        bank = bank_of(job)
                        if i >= len(banks):
                            pe.wait_ge(*out_of(order[i - len(banks)][0]))
                        if what == "xT":
                            pe.wait_ge(xn_done, NT)
                            for t in range(NT):
                                ins = nc.tensor.transpose(bank[:, t * P:(t + 1) * P], xn[:, t, j * P:(j + 1) * P],
                                                          k["ident"][:])
                        elif what == "cT":
                            pe.wait_ge(ctx_in, 32)
                            for kt in range(4 * j, min(4 * j + 4, KT)):
                                n = ktiles[kt][1]
                                ins = nc.tensor.transpose(bank[:, (kt % 4) * P:(kt % 4) * P + n],
                                                          ctx_tok[0:n, kt, :], k["ident"][0:n, 0:n])
                        elif what == "mx":
                            pe.wait_ge(max_split, 5 * (targets.index(j) + 1))
                            for qt in range(NT):
                                for h in range(HG):
                                    ins = nc.tensor.matmul(bank[32 * h:32 * h + 3, qt * P:(qt + 1) * P],
                                                           m3[:, h * NT + qt, :], k["identb"][:], start=True,
                                                           stop=True, skip_group_check=True)
                        elif what == "own":
                            for first, last in ((0, NG - 1), (NG - 1, NG)):
                                pe.wait_ge(normed, last + 1)
                                for t in range(NT):
                                    for g in range(first, last):
                                        ins = nc.tensor.matmul(ps[:, OWN_BANKS[t], 0:C], y[:, g, t * P:(t + 1) * P],
                                                               wo[:, g, :], start=(g == 0), stop=(g == NG - 1))
                        elif what == "o":
                            pe.wait_ge(normed, 1)
                            for t in range(2):
                                for g in range(NG):
                                    ins = nc.tensor.matmul(bank[:, t * C:(t + 1) * C],
                                                           y[:, g, (2 * j + t) * P:(2 * j + t + 1) * P], wo[:, g, :],
                                                           start=(g == 0), stop=(g == NG - 1))
                                    if t == 0 and g % 2:
                                        fill()
                        elif what == "q":
                            pe.wait_ge(*out_of(("xT", CT - 1)))
                            for c in range(CT):
                                ins = nc.tensor.matmul(bank, wq[:, c, j * P:(j + 1) * P], xnT[:, c, :],
                                                       start=(c == 0), stop=(c == CT - 1))
                                if c == 0:
                                    fill()
                        elif what == "k":
                            pe.wait_ge(*out_of(kv_ready))
                            half, (at, n) = j[0], kchunks[j[1]]
                            for c in range(kvc):
                                ins = nc.tensor.matmul(bank[:, 0:n], wk[:, c, half * P:(half + 1) * P],
                                                       kv[:, c, at:at + n], start=(c == 0), stop=(c == kvc - 1))
                                if c < kvc - 1:
                                    fill()
                        else:
                            half, j = j
                            if half == 0:
                                pe.wait_ge(*out_of(kv_ready))
                            for m, kt in enumerate(range(4 * j, min(4 * j + 4, KT))):
                                at, n = ktiles[kt]
                                for c in range(kvc):
                                    ins = nc.tensor.matmul(bank[0:n, m * P:(m + 1) * P], kv[:, c, at:at + n],
                                                           wv[:, c, half * P:(half + 1) * P], start=(c == 0),
                                                           stop=(c == kvc - 1))
                        ins.then_inc(aux_mm, 1)

                    def score_max(slot, i):
                        h, qt, ch = group_s1[i]
                        n = slot * n_s1 + i
                        at, cols = s1_cols(qt, ch)
                        if i == 0 and targets[slot] in (0, NG // 2):
                            for kind in "qk":
                                pe.wait_ge(packed[kind, targets[slot] // 2], PACKED)
                        if n >= S1_RING:
                            pe.wait_ge(s1_max, n - S1_RING + 1)
                        hh = targets[slot] * HG + h
                        ins = nc.tensor.matmul(ps[:, n % S1_RING, 0:cols], qpack[0:RM, hh, qt * P:(qt + 1) * P],
                                               kpack[0:RM, hh, at:at + cols], start=True, stop=not causal)
                        if causal:
                            ins = nc.tensor.matmul(ps[:, n % S1_RING, cols - P:cols], k["identb"][:],
                                                   k["k_from_q"][:, P:2 * P], start=False, stop=True)
                        ins.then_inc(s1_mm, 1)

                    def score(s, m):
                        g, kt = divmod(s, KT)
                        i = HG * s + m
                        at, n = ktiles[kt]
                        q0 = at if causal else 0
                        if i >= S2_RING:
                            pe.wait_ge(exp_done, i - S2_RING + 1)
                        out = ps[0:n, S1_RING + i % S2_RING, :]
                        ins = nc.tensor.matmul(out[:, q0:T], kpack[0:KROWS, g * HG + m, at:at + n],
                                               qpack[0:KROWS, g * HG + m, q0:T], start=True, stop=not causal)
                        if causal:
                            ins = nc.tensor.matmul(out[:, q0:q0 + P], k["identb"][:], k["q_from_k"][:],
                                                   start=False, stop=True)
                        ins.then_inc(s2_mm, 1)

                    def weigh(s):
                        g, kt = divmod(s, KT)
                        at, n = ktiles[kt]
                        q0 = at if causal else 0
                        pe.wait_ge(exp_done, HG * (s + 1))
                        if kt == 0 and g:
                            pe.wait_ge(sums_out, g)
                        if kt == 0 and g == NG // 2:
                            pe.wait_ge(*out_of(values_jobs(1)[-1][0]))
                        for j in range(HG):
                            ins = nc.tensor.matmul(ps[32 * j:32 * j + D + 1, AV_BANK, q0:T],
                                                   vals[0:n, kt, g * HG + j, :], prob[0:n, (HG * s + j) % PROBS, q0:T],
                                                   start=(kt == 0), stop=(kt == KT - 1), skip_group_check=True)
                        ins.then_inc(av_mm, 1)

                    if opening:
                        set_up_pe(pe)
                        pe.wait_ge(qkv_in, 16 * 4)
                    for job, _ in jobs[-1]:
                        make(job)
                    if not attend and ahead is not None:
                        last = order[len(jobs[-1]) - len(banks):len(jobs[-1])]
                        for job, _ in last:
                            pe.wait_ge(*out_of(job))
                        for i in range(n_s1):
                            score_max(0, i)
                        for job, _ in jobs[0]:
                            make(job)
                    for s in range(steps):
                        g, kt = divmod(s, KT)
                        todo = list(s1_at.get((g, kt), ())) if g < len(targets) else []
                        if kt == 0 and g:
                            pe.wait_ge(*out_of(("mx", g)))
                        filled = 0

                        def fill(n=1):
                            nonlocal filled
                            for i in todo[filled:filled + n]:
                                score_max(g, i)
                            filled = min(filled + n, len(todo))

                        fill()
                        for m in range(HG):
                            score(s, m)
                            fill()
                            if m == 1 and s:
                                weigh(s - 1)
                                fill()
                        for job, _ in jobs[s][:1]:
                            make(job, fill)
                        fill(len(todo))
                        for job, _ in jobs[s][1:]:
                            make(job)
                    if attend:
                        weigh(steps - 1)
                    if closing:
                        for job, _ in jobs[steps]:
                            make(job)
            ph.clear()

        turn(None, None, 0, [0, 1, 2, 3, 4, 5, AUX_BANK], opening=True)
        with nc.Fori(0, B - 1) as b:
            turn(b, (b + B - 1) % B, b + 1, [AUX_BANK])
        turn(B - 1, B - 2, None, [AUX_BANK], closing=True)


L = 2
LH, LD = 8, 64
INNER = LH * LD
HP = LH // 2
HID = int(C * 4 * 2 / 3)
FT = -(-HID // P)
FR = HID - (FT - 1) * P
WINDOW = P
QK_SCALE = 8.0
PAIRS = NT * HP
S_RING = 3
PT_BANK, O_BANK = 3, 5
JOB_BANKS = [6, 7]
P_RING = 3
QK_RING = 4
BIAS_SLOT = 4


def rotary_tables():
    half = np.arange(0, LD, 2, dtype=np.float32)
    inv_freq = (1.0 / np.float32(10000.0) ** (half / np.float32(LD))).astype(np.float32)
    t = np.arange(T, dtype=np.float32)
    freqs = t[:, None] * inv_freq[None, :]
    base = (half + np.float32(0.4 * LD)) / np.float32(1.4 * LD)
    power = (t - T // 2) / np.float32(WINDOW // 2)
    scale = base[None, :] ** power[:, None]
    out = np.empty((2, 2, T, LD), np.float32)
    for i, s in enumerate((scale * np.float32(QK_SCALE), np.float32(1) / scale)):
        cos, sin = np.cos(freqs) * s, np.sin(freqs) * s
        out[i, 0] = np.concatenate([cos, cos], -1)
        out[i, 1] = np.concatenate([-sin, sin], -1)
    return out


def constants():
    return {"rotary": rotary_tables()}


def local_layers(nc, k, x_all, a):
    turns = L * B
    assert L == 2
    spill = nc.dram_tensor("local_spill", [P, B, NT, C], F32).ap()
    with Phase(nc, "local") as ph:
        wqkv, wo = ph.sb("wqkv", [P, L, CT, 3 * INNER]), ph.sb("wo", [P, L, HP, C])
        w1, w2 = ph.sb("w1", [P, L, CT, 2 * HID]), ph.sb("w2", [P, L, FT, C])
        b1, b2 = ph.sb("b1", [P, L, 2, FT]), ph.sb("b2", [P, L, C])
        ln_g, ln_b = ph.sb("ln_g", [P, L, CT]), ph.sb("ln_b", [P, L, CT])
        rot = ph.sb("rot", [P, L, 2, 2, NT, LD])
        zt, hT = ph.sb("zt", [P, NT, C]), ph.sb("hT", [P, CT, T])
        sq, by_cos, by_sin = ph.sb("sq", [P, 2, INNER]), ph.sb("by_cos", [P, 2, INNER]), ph.sb("by_sin", [P, 2, INNER])
        ss, ssc, rnorm = (ph.sb(n, [P, 2 * NT, LH]) for n in ("ss", "ssc", "rnorm"))
        qk = ph.sb("qk", [P, QK_RING, INNER])
        qT, kz, vt = ph.sb("qT", [P, HP, T]), ph.sb("kz", [P, LH, T]), ph.sb("vt", [P, NT, INNER])
        mxs, nmx, sums, rsums = (ph.sb(n, [P, PAIRS, 2]) for n in ("mxs", "nmx", "sums", "rsums"))
        prob, probT = ph.sb("prob", [P, P_RING, 2, 2 * P]), ph.sb("probT", [P, 2, 2, 2 * P])
        oT = ph.sb("oT", [P, HP, T])
        shifted, hn, hnT = ph.sb("shifted", [P, NT, P]), ph.sb("hn", [P, NT, C]), ph.sb("hnT", [P, CT, T])
        stats, mv, rstd = ph.sb("stats", [P, B * NT, 2, 6]), ph.sb("mv", [P, B * NT, 2]), ph.sb("rstd", [P, B * NT])
        veps = ph.sb("veps", [P, B * NT])
        gel, hid = ph.sb("gel", [P, 2, T]), ph.sb("hid", [P, FT, T])
        ps = ph.ps("ps", [P, 8, 512])

        tables, spilled = ph.sem("tables"), ph.sem("spilled")
        loaded = ph.ctx.enter_context(nc.semaphore("local_loaded"))
        n_loads = 0
        ln_done, var_eps, rstd_done = ph.sem("ln_done"), ph.sem("var_eps"), ph.sem("rstd_done")
        zeroed = ph.sem("zeroed")
        x_tiles = x_all[:].rearrange("p b t c -> p (b t) c")
        with ExitStack() as part:
            raw = part.enter_context(nc.sbuf_tensor("local_raw", [P, 2, 2, NT, LD], F32))
            head_scale = part.enter_context(nc.sbuf_tensor("local_head_scale", [P, L, 2, LD], F32))
            with nc.Block() as block:
                @block.gpsimd
                def _(pool):
                    nc.gpsimd.memset(kz[:], 0.0)
                    for l in range(L):
                        nc.gpsimd.memset(w2[:, l, FT - 1, :], 0.0).then_inc(zeroed, 1)
                    pool.wait_ge(ln_done, 2 * B * NT)
                    nc.gpsimd.tensor_scalar(veps[:], mv[:, :, 1], EPS, None, ALU.add).then_inc(var_eps, 1)
                    pool.wait_ge(var_eps, 1)
                    nc.gpsimd.tensor_tensor(rstd[:], veps[:], k["half"][:, 0:B * NT], ALU.pow).then_inc(rstd_done, 1)

                @block.vector
                def _(dve):
                    nc.vector.memset(hid[:, FT - 1, :], 0.0)
                    nc.vector.memset(hT[:, 1, 0:1], 0.0)
                    nc.vector.memset(shifted[0:1, 0, :], 0.0)
                    for t in range(B * NT):
                        nc.vector.bn_stats(stats[:, t, 0], x_tiles[:, t, :]).then_inc(ln_done, 1)
                    for t in range(B * NT):
                        dve.wait_ge(ln_done, t + 1)
                        nc.vector.bn_aggr(mv[:, t], stats[:, t, 0]).then_inc(ln_done, 1)
                    dve.wait_ge(spilled, 16)
                    dve.wait_ge(rstd_done, 1)
                    for t in range(B * NT):
                        nc.vector.tensor_scalar(x_tiles[:, t, :], x_tiles[:, t, :], mv[:, t, 0:1],
                                                rstd[:, t:t + 1], ALU.subtract, ALU.mult)
                    dve.wait_ge(tables, 16 * (2 + 2 * L))
                    for l in range(L):
                        for i in range(2):
                            hs = head_scale[:, l, i, :]
                            nc.vector.tensor_tensor(rot[:, l, i, 0], raw[:, i, 0],
                                                    hs.unsqueeze(1).to_broadcast([P, NT, LD]), ALU.mult)
                            for lo, other in ((0, LD // 2), (LD // 2, 0)):
                                nc.vector.tensor_tensor(
                                    rot[:, l, i, 1, :, lo:lo + LD // 2], raw[:, i, 1, :, lo:lo + LD // 2],
                                    hs[:, other:other + LD // 2].unsqueeze(1).to_broadcast([P, NT, LD // 2]), ALU.mult)

                @block.sync
                def _(sp):
                    nonlocal n_loads
                    sp.dma_start(spill, x_all[:]).then_inc(spilled, 16)
                    sp.dma_start(raw[:].rearrange("p a b t d -> p (a b) t d"),
                                 a["rotary"].rearrange("a b (t p) d -> p (a b) t d", p=P)).then_inc(tables, 16)
                    sp.dma_start(wqkv[:, 0], a["L0_ffn_wqkv"][0].rearrange("(t p) n -> p t n", p=P)).then_inc(tables, 16)
                    with nc.allow_non_contiguous_dma(reason="small columns"):
                        parts = []
                        for l in range(L):
                            for i, n in enumerate("qk"):
                                sp.dma_start(head_scale[:, l, i, :], a[f"L0_ffn_{n}_scale"][l][None, :]
                                             .to_broadcast([P, LD])).then_inc(tables, 16)
                            if l:
                                parts += [(wqkv[:, l], a["L0_ffn_wqkv"][l].rearrange("(t p) n -> p t n", p=P))]
                            parts += [
                                (wo[:, l], a["L0_ffn_wo"][l].rearrange("(t p) n -> p t n", p=P)),
                                (w1[:, l], a["L0_ffn_w1"][l].rearrange("(t p) n -> p t n", p=P)),
                                (w2[:, l, 0:FT - 1, :],
                                 a["L0_ffn_w2"][l, 0:(FT - 1) * P, :].rearrange("(t p) n -> p t n", p=P)),
                                (w2[0:FR, l, FT - 1, :], a["L0_ffn_w2"][l, (FT - 1) * P:HID, :]),
                                (b2[:, l], a["L0_ffn_b2"][l][None, :].to_broadcast([P, C])),
                                (ln_g[:, l], a["L0_ffn_ln_g"][l].rearrange("(t p) -> p t", p=P)),
                                (ln_b[:, l], a["L0_ffn_ln_b"][l].rearrange("(t p) -> p t", p=P)),
                            ]
                            for i in range(2):
                                col = a["L0_ffn_b1"][l, i * HID:(i + 1) * HID]
                                parts += [(b1[:, l, i, 0:FT - 1], col[0:(FT - 1) * P].rearrange("(t p) -> p t", p=P)),
                                          (b1[0:FR, l, i, FT - 1:FT], col[(FT - 1) * P:HID][:, None])]
                        sp.wait_ge(zeroed, L)
                        for dst, src in parts:
                            sp.dma_start(dst, src).then_inc(loaded, 16)
                            n_loads += 1
                    sp.wait_ge(tables, 16 * (2 + 2 * L))
        ph.clear()

        job_mm, job_act, job_dve = ph.sem("job_mm"), ph.sem("job_act"), ph.sem("job_dve")
        squared, ss_sum, ss_ok = (ph.sem(n) for n in ("squared", "ss_sum", "ss_ok"))
        rot_sum, norm_ok, qk_ready = (ph.sem(n) for n in ("rot_sum", "norm_ok", "qk_ready"))
        s_mm, maxed, exp_done, summed = (ph.sem(n) for n in ("s_mm", "maxed", "exp_done", "summed"))
        p_ready, pT_mm, pT_out, o_mm, o_out = (ph.sem(n) for n in ("p_ready", "pT_mm", "pT_out", "o_mm", "o_out"))
        stream = kz[:].rearrange("p (b h) t -> p b (h t)", b=B).rearrange("p b (t c) -> p b t c", c=C)
        stream_in = [ph.sem(f"stream_in{b}") for b in range(B)]
        copied, shift_in, hn_done, biased = (ph.sem(n) for n in ("copied", "shift_in", "hn_done", "biased"))

        def turn(cur, prev, ahead, ffn_layer=None):
            attend = cur is not None
            last = PAIRS + 1
            slots = range(-1, last + 1)
            jobs = {s: [] for s in slots}

            def at(slot, *some):
                jobs[slot if attend else -1] += some

            if ahead is not None:
                at(-1, ("zT", 0), ("zT", 1), ("q", 0))
                at(0, ("k", 0))
                at(1, ("q", 1))
                at(2, ("k", 1))
            if prev is not None:
                at(3, ("hT", 0), ("hT", 1))
                at(4, ("gate", 0), ("gate", 1))
                at(5, ("value", 0), ("value", 1))
                at(6, ("gate", 2), ("gate", 3))
                at(7, ("value", 2), ("value", 3))
                at(8, ("gate", 4), ("gate", 5))
            if ahead is not None:
                at(9, ("v", 0), ("qT", 0), ("kT", 0))
            if prev is not None:
                at(10, ("value", 4), ("value", 5))
                for t in range(NT):
                    at(11 + t, ("down", t))
            if ahead is not None:
                at(11, ("q", 2))
                at(12, ("k", 2))
                at(13, ("v", 1), ("qT", 1), ("kT", 1))
                at(15, ("q", 3))
                at(16, ("k", 3))
            if attend:
                for w in range(NT):
                    at(HP * (w + 1) + 1, ("wo", w))
            if ahead is not None:
                at(last, ("v", 2), ("qT", 2), ("kT", 2), ("v", 3), ("qT", 3), ("kT", 3))
            order = [job for s in sorted(jobs) for job in jobs[s]]
            number = {job: i for i, job in enumerate(order)}
            banks = JOB_BANKS if attend else list(range(8))
            by_act = ("v", "qT", "kT", "gate")

            def out_of(job):
                mine = job[0] in by_act
                return job_act if mine else job_dve, sum((j[0] in by_act) == mine for j in order[:number[job] + 1])

            def bank_of(job):
                return ps[:, banks[number[job] % len(banks)], :]

            def z(turn_no):
                return x_all[:, turn_no % B]

            def layer(turn_no):
                return turn_no // B

            def unit(job):
                return 2 * job[1] + (job[0][0] == "k")

            def first_col(u):
                return 0 if u >= HP else P

            def up_rows(f):
                return P if f < FT - 1 else FR

            with nc.Block() as block:
                if not attend and prev is None:
                    @block.sync
                    def _(sp):
                        sp.wait_ge(loaded, 16 * n_loads)
                if prev is not None:
                    @block.sync
                    def _(sp):
                        if not attend:
                            for b in range(B):
                                sp.dma_start(stream[:, b], spill[:, b]).then_inc(stream_in[b], 16)
                        zp = z(prev)
                        sp.dma_start(shifted[1:P, :, :], zp[0:P - 1, :, P:C]).then_inc(shift_in, 16)
                        sp.dma_start(shifted[0:1, 1:NT, :], zp[P - 1:P, 0:NT - 1, P:C]).then_inc(shift_in, 16)
                        sp.wait_ge(shift_in, 32)
                        if not attend:
                            for b in range(B):
                                sp.wait_ge(stream_in[b], 16)

                @block.gpsimd
                def _(pool):
                    def rotate(job):
                        u = unit(job)
                        if attend:
                            pool.wait_ge(*out_of(job))
                            nc.gpsimd.tensor_tensor(by_cos[:, u % 2], by_cos[:, u % 2], by_sin[:, u % 2], ALU.add) \
                              .then_inc(rot_sum, 1)
                        pool.wait_ge(ss_ok, u + 1)
                        nc.gpsimd.tensor_tensor(rnorm[:, u], ssc[:, u], k["half"][:, 0:LH], ALU.pow) \
                          .then_inc(norm_ok, 1)
                        if u >= QK_RING:
                            turned = ("kT" if u % 2 else "qT", (u - QK_RING) // 2)
                            pool.wait_ge(job_mm, number[turned] + 1)
                        pool.wait_ge(rot_sum, u + 1)
                        pool.wait_ge(norm_ok, u + 1)
                        nc.gpsimd.tensor_tensor(
                            qk[:, u % QK_RING].rearrange("p (h d) -> p h d", d=LD),
                            by_cos[:, u % 2].rearrange("p (h d) -> p h d", d=LD),
                            rnorm[:, u].unsqueeze(2).to_broadcast([P, LH, LD]), ALU.mult).then_inc(qk_ready, 1)

                    def norm():
                        pool.wait_ge(ln_done, 3 * NT)
                        nc.gpsimd.tensor_scalar(veps[:, 0:NT], mv[:, 0:NT, 1], EPS, None, ALU.add) \
                          .then_inc(var_eps, 1)
                        pool.wait_ge(var_eps, 1)
                        nc.gpsimd.tensor_tensor(rstd[:, 0:NT], veps[:, 0:NT], k["half"][:, 0:NT], ALU.pow) \
                          .then_inc(rstd_done, 1)

                    def bias():
                        pool.wait_ge(hn_done, 1)
                        pool.wait_ge(shift_in, 32)
                        zp = z(prev)
                        nc.gpsimd.tensor_tensor(zp, zp, b2[:, ffn_layer, :].unsqueeze(1).to_broadcast([P, NT, C]),
                                                ALU.add).then_inc(biased, 1)

                    for s in slots:
                        if s == (0 if attend else -1) and prev is not None:
                            norm()
                        if s == BIAS_SLOT and prev is not None and attend:
                            bias()
                        for job in jobs[s]:
                            if job[0] in "qk":
                                rotate(job)
                    if prev is not None and not attend:
                        bias()

                @block.scalar
                def _(act):
                    def exps(u):
                        act.wait_ge(maxed, 2 * u + 2)
                        if u >= P_RING:
                            act.wait_ge(pT_mm, u - P_RING + 1)
                        c0 = first_col(u)
                        for m in range(2):
                            ins = nc.scalar.activation(
                                prob[:, u % P_RING, m, c0:2 * P], ps[:, u % S_RING, m * 2 * P + c0:(m + 1) * 2 * P],
                                ACT.Exp, bias=nmx[:, u, m:m + 1], accum_out=sums[:, u, m:m + 1])
                        ins.then_inc(exp_done, 1)

                    def take_probT(u):
                        act.wait_ge(pT_mm, u + 1)
                        if u >= 2:
                            act.wait_ge(o_mm, u - 1)
                        c0 = first_col(u)
                        nc.scalar.activation(
                            probT[:, u % 2, :, c0:2 * P],
                            ps[:, PT_BANK + u % 2, :].rearrange("p (m c) -> p m c", c=2 * P)[:, :, c0:2 * P],
                            ACT.Copy).then_inc(pT_out, 1)

                    def take(job):
                        what, t = job
                        if what not in by_act and what not in "qk":
                            return
                        act.wait_ge(job_mm, number[job] + 1)
                        bank, cols = bank_of(job), slice(t * P, (t + 1) * P)
                        heads = bank.rearrange("p (h q) -> p h q", q=P)
                        if what in "qk":
                            u = unit(job)
                            if u >= 2:
                                act.wait_ge(ss_sum, u - 1)
                            nc.scalar.activation(sq[:, u % 2], bank, ACT.Square).then_inc(squared, 1)
                            return
                        if what == "v":
                            if attend:
                                act.wait_ge(o_mm, min(HP * (t + 2), PAIRS))
                            ins = nc.scalar.activation(vt[:, t], bank, ACT.Copy)
                        elif what == "qT":
                            if attend:
                                act.wait_ge(s_mm, HP * (t + 1))
                            ins = nc.scalar.activation(qT[:, :, cols], heads, ACT.Copy)
                        elif what == "kT":
                            if attend:
                                act.wait_ge(s_mm, min(HP * (t + 2), PAIRS))
                            kzp = kz[:].rearrange("p (h two) t -> p h two t", two=2)
                            nc.scalar.activation(kzp[0:LD, :, 0, cols], heads[0:LD], ACT.Copy)
                            ins = nc.scalar.activation(kzp[LD:P, :, 1, cols], heads[LD:P], ACT.Copy)
                        else:
                            rows = up_rows(t)
                            if t >= 2:
                                act.wait_ge(*out_of(("value", t - 2)))
                            ins = nc.scalar.activation(gel[0:rows, t % 2, :], bank[0:rows], ACT.Gelu,
                                                       bias=b1[0:rows, ffn_layer, 1, t:t + 1])
                        ins.then_inc(job_act, 1)

                    if ahead is not None:
                        nc.scalar.activation(zt[:], z(ahead), ACT.Copy).then_inc(copied, 1)
                    for s in slots:
                        if attend:
                            if s == -1:
                                exps(0)
                            if s + 2 < PAIRS:
                                exps(s + 2)
                            if 0 <= s < PAIRS:
                                take_probT(s)
                        for job in jobs[s]:
                            take(job)

                @block.vector
                def _(dve):
                    def maxima(u):
                        c0 = first_col(u)
                        dve.wait_ge(s_mm, u + 1)
                        nc.vector.tensor_reduce(
                            mxs[:, u], ps[:, u % S_RING, :].rearrange("p (m c) -> p m c", c=2 * P)[:, :, c0:2 * P],
                            AX_X, ALU.max).then_inc(maxed, 1)
                        dve.wait_ge(maxed, 2 * u + 1)
                        nc.vector.tensor_scalar(nmx[:, u], mxs[:, u], -1.0, None, ALU.mult).then_inc(maxed, 1)

                    def divide(u):
                        dve.wait_ge(exp_done, u + 1)
                        nc.vector.reciprocal(rsums[:, u], sums[:, u]).then_inc(summed, 1)
                        dve.wait_ge(summed, u + 1)
                        for m in range(2):
                            pr = prob[:, u % P_RING, m, first_col(u):2 * P]
                            ins = nc.vector.tensor_scalar(pr, pr, rsums[:, u, m:m + 1], None, ALU.mult)
                        ins.then_inc(p_ready, 1)

                    def take_outputs(u):
                        w, n = divmod(u, HP)
                        dve.wait_ge(o_mm, u + 1)
                        nc.vector.tensor_copy(oT[:, n, w * P:(w + 1) * P],
                                              ps[:, O_BANK, n * P:(n + 1) * P]).then_inc(o_out, 1)

                    def rotate(job):
                        u, i, t = unit(job), "qk".index(job[0]), job[1]
                        table = rot[:, layer(ahead)]
                        dve.wait_ge(squared, u + 1)
                        nc.vector.tensor_reduce(ss[:, u], sq[:, u % 2].rearrange("p (h d) -> p h d", d=LD), AX_X,
                                                ALU.add).then_inc(ss_sum, 1)
                        dve.wait_ge(ss_sum, u + 1)
                        nc.vector.tensor_scalar(ssc[:, u], ss[:, u], 1e-24, None, ALU.max).then_inc(ss_ok, 1)
                        if u >= 2:
                            dve.wait_ge(qk_ready, u - 1)
                        heads = bank_of(job).rearrange("p (h d) -> p h d", d=LD)
                        bc = by_cos[:, u % 2].rearrange("p (h d) -> p h d", d=LD)
                        bs = by_sin[:, u % 2].rearrange("p (h d) -> p h d", d=LD)
                        cos, sin = table[:, i, 0, t, :], table[:, i, 1, t, :]
                        for lo, other in ((0, LD // 2), (LD // 2, 0)):
                            nc.vector.tensor_tensor(
                                bs[:, :, lo:lo + LD // 2], heads[:, :, other:other + LD // 2],
                                sin[:, lo:lo + LD // 2].unsqueeze(1).to_broadcast([P, LH, LD // 2]), ALU.mult)
                        nc.vector.tensor_tensor(bc, heads, cos.unsqueeze(1).to_broadcast([P, LH, LD]), ALU.mult) \
                          .then_inc(job_dve, 1)
                        if not attend:
                            dve.wait_ge(*out_of(job))
                            nc.vector.tensor_tensor(by_cos[:, u % 2], by_cos[:, u % 2], by_sin[:, u % 2], ALU.add) \
                              .then_inc(rot_sum, 1)

                    def take(job):
                        what, t = job
                        if what in by_act:
                            return
                        dve.wait_ge(job_mm, number[job] + 1)
                        bank = bank_of(job)
                        if what in "qk":
                            rotate(job)
                            return
                        if what == "zT" and t == 0:
                            ins = nc.vector.tensor_copy(hT[:, 0, :], bank)
                        elif what == "zT":
                            ins = nc.vector.tensor_copy(hT[:, 1, 1:T], bank[:, 0:T - 1])
                        elif what == "hT":
                            l = ffn_layer
                            ins = nc.vector.tensor_scalar(hnT[:, t, :], bank, ln_g[:, l, t:t + 1],
                                                          ln_b[:, l, t:t + 1], ALU.mult, ALU.add)
                        elif what == "value":
                            rows = up_rows(t)
                            dve.wait_ge(*out_of(("gate", t)))
                            ins = nc.vector.scalar_tensor_tensor(
                                out=hid[0:rows, t, :], in0=bank[0:rows], scalar=b1[0:rows, ffn_layer, 0, t:t + 1],
                                in1=gel[0:rows, t % 2, :], op0=ALU.add, op1=ALU.mult)
                        else:
                            if what == "down":
                                dve.wait_ge(biased, 1)
                            zz = z(prev if what == "down" else cur)[:, t, :]
                            ins = nc.vector.tensor_tensor(zz, bank[:, 0:C], zz, ALU.add)
                        ins.then_inc(job_dve, 1)

                    def give_back(b):
                        dve.wait_ge(stream_in[b], 16)
                        nc.vector.tensor_tensor(x_all[:, b], x_all[:, b], stream[:, b], ALU.add)

                    def norm():
                        zp = z(prev)
                        for t in range(NT):
                            nc.vector.bn_stats(stats[:, t, 0], zp[:, t, 0:P]).then_inc(ln_done, 1)
                        dve.wait_ge(shift_in, 32)
                        for t in range(NT):
                            nc.vector.bn_stats(stats[:, t, 1], shifted[:, t]).then_inc(ln_done, 1)
                        for t in range(NT):
                            dve.wait_ge(ln_done, NT + t + 1)
                            nc.vector.bn_aggr(mv[:, t], stats[:, t]).then_inc(ln_done, 1)

                    def normed():
                        zp = z(prev)
                        dve.wait_ge(rstd_done, 1)
                        for t in range(NT):
                            for dst, src in ((hn[:, t, 0:P], zp[:, t, 0:P]), (hn[:, t, P:C], shifted[:, t])):
                                ins = nc.vector.tensor_scalar(dst, src, mv[:, t, 0:1], rstd[:, t:t + 1],
                                                              ALU.subtract, ALU.mult)
                        ins.then_inc(hn_done, 1)

                    for s in slots:
                        if attend:
                            if s == -1:
                                maxima(0)
                            if s + 2 < PAIRS:
                                maxima(s + 2)
                            if s + 1 < PAIRS:
                                divide(s + 1)
                            if s >= 2:
                                take_outputs(s - 2)
                        if s == (0 if attend else -1) and prev is not None:
                            norm()
                        if s == -1 and prev is not None and not attend:
                            for b in range(B - 1):
                                give_back(b)
                        if s == (2 if attend else -1) and prev is not None:
                            normed()
                        for job in jobs[s]:
                            take(job)
                    if prev is not None and not attend:
                        dve.wait_ge(*out_of(("down", NT - 1)))
                        give_back(B - 1)

                @block.tensor
                def _(pe):
                    def score(u):
                        w, n = divmod(u, HP)
                        c0 = first_col(u)
                        if u >= S_RING:
                            pe.wait_ge(exp_done, u - S_RING + 1)
                        out = ps[:, u % S_RING, :].rearrange("p (m c) -> p m c", c=2 * P)[:, :, c0:2 * P]
                        nc.tensor.matmul(out, qT[:, n, w * P:(w + 1) * P],
                                         kz[:, 2 * n:2 * n + 2, (w - 1) * P + c0:(w + 1) * P], start=True, stop=False)
                        nc.tensor.matmul(out, k["identb"][:], k["k_from_q"][:, c0:2 * P].unsqueeze(1)
                                         .to_broadcast([P, 2, 2 * P - c0]), start=False, stop=True).then_inc(s_mm, 1)

                    def turn_weights(u):
                        pe.wait_ge(p_ready, u + 1)
                        if u >= 2:
                            pe.wait_ge(pT_out, u - 1)
                        for m in range(2):
                            for kb in range(first_col(u) // P, 2):
                                ins = nc.tensor.transpose(
                                    ps[:, PT_BANK + u % 2, m * 2 * P + kb * P:m * 2 * P + (kb + 1) * P],
                                    prob[:, u % P_RING, m, kb * P:(kb + 1) * P], k["ident"][:])
                        ins.then_inc(pT_mm, 1)

                    def weigh(u):
                        w, n = divmod(u, HP)
                        pe.wait_ge(pT_out, u + 1)
                        if u:
                            pe.wait_ge(o_out, u)
                        first = first_col(u) // P
                        for kb in range(first, 2):
                            for m in range(2):
                                h = 2 * n + m
                                ins = nc.tensor.matmul(
                                    ps[LD * m:LD * m + LD, O_BANK, n * P:(n + 1) * P],
                                    vt[:, w - 1 + kb, h * LD:(h + 1) * LD], probT[:, u % 2, m, kb * P:(kb + 1) * P],
                                    start=(kb == first), stop=(kb == 1), skip_group_check=True)
                        ins.then_inc(o_mm, 1)

                    def make(job):
                        what, t = job
                        i, bank = number[job], bank_of(job)
                        if i >= len(banks):
                            pe.wait_ge(*out_of(order[i - len(banks)]))
                        if what == "zT":
                            pe.wait_ge(copied, 1)
                            for n in range(NT):
                                ins = nc.tensor.transpose(bank[:, n * P:(n + 1) * P],
                                                          zt[:, n, t * P:(t + 1) * P], k["ident"][:])
                        elif what in ("qT", "kT"):
                            u = unit(job)
                            pe.wait_ge(qk_ready, u + 1)
                            for n in range(HP):
                                ins = nc.tensor.transpose(bank[:, n * P:(n + 1) * P],
                                                          qk[:, u % QK_RING, n * P:(n + 1) * P], k["ident"][:])
                        elif what in "qkv":
                            pe.wait_ge(*out_of(("zT", CT - 1)))
                            part = "qkv".index(what)
                            for c in range(CT):
                                ins = nc.tensor.matmul(bank, hT[:, c, t * P:(t + 1) * P],
                                                       wqkv[:, layer(ahead), c, part * INNER:(part + 1) * INNER],
                                                       start=(c == 0), stop=(c == CT - 1))
                        elif what == "wo":
                            pe.wait_ge(o_out, HP * (t + 1))
                            for n in range(HP):
                                ins = nc.tensor.matmul(bank[:, 0:C], oT[:, n, t * P:(t + 1) * P],
                                                       wo[:, layer(cur), n, :], start=(n == 0), stop=(n == HP - 1))
                        elif what == "hT":
                            pe.wait_ge(hn_done, 1)
                            for n in range(NT):
                                ins = nc.tensor.transpose(bank[:, n * P:(n + 1) * P], hn[:, n, t * P:(t + 1) * P],
                                                          k["ident"][:])
                        elif what in ("gate", "value"):
                            pe.wait_ge(*out_of(("hT", CT - 1)))
                            rows = up_rows(t)
                            col = (HID if what == "gate" else 0) + t * P
                            for c in range(CT):
                                ins = nc.tensor.matmul(bank[0:rows], w1[:, ffn_layer, c, col:col + rows], hnT[:, c, :],
                                                       start=(c == 0), stop=(c == CT - 1))
                        else:
                            pe.wait_ge(*out_of(("value", FT - 1)))
                            for f in range(FT):
                                ins = nc.tensor.matmul(bank[:, 0:C], hid[:, f, t * P:(t + 1) * P],
                                                       w2[:, ffn_layer, f, :], start=(f == 0), stop=(f == FT - 1))
                        ins.then_inc(job_mm, 1)

                    for s in slots:
                        if attend:
                            if s == -1:
                                score(0)
                            if s + 2 < PAIRS:
                                score(s + 2)
                            if 0 <= s < PAIRS:
                                turn_weights(s)
                        for job in jobs[s]:
                            make(job)
                        if 0 <= s - 1 < PAIRS:
                            if attend:
                                weigh(s - 1)
            ph.clear()

        turn(None, None, 0)
        turn(0, None, 1)
        with nc.Fori(1, B + 1) as i:
            turn(i, i - 1, i + 1, 0)
        with nc.Fori(B + 1, turns - 1) as i:
            turn(i, i - 1, i + 1, L - 1)
        turn(turns - 1, turns - 2, None, L - 1)
        turn(None, turns - 1, None, L - 1)

E = 8
CAP = max(1, int(T / E * 1.25))
HE = 1024
ET = HE // P
BT = B * NT
EH = E // 2
OFF = 1000.0


def experts(nc, k, x_all, a, out):
    with Phase(nc, "moe") as ph:
        slot_in = ph.sb("slot_in", [P, CT, E, B, CAP])
        y_slot = ph.sb("y_slot", [P, E, B, C])
        place = ph.sb("place", [P, B, NT, E])
        gate = ph.sb("gate", [P, B, NT, E])
        slots, orders = ph.sb("slots", [P, E, CAP]), ph.sb("orders", [P, BT, E])
        before, ones = ph.sb("before", [P, P], BF16), ph.sb("ones", [P, P], BF16)
        b1, b2 = ph.sb("b1", [P, E, ET]), ph.sb("b2", [P, E, CT])
        wr, br = ph.sb("wr", [P, CT, E]), ph.sb("br", [P, E])
        w1 = [ph.sb(f"w1_{i}", [P, CT, HE]) for i in range(2)]
        w2 = [ph.sb(f"w2_{i}", [P, ET, C]) for i in range(2)]
        ps = ph.ps("ps", [P, 8, 512])
        w1_in = [nc_sem for nc_sem in (ph.ctx.enter_context(nc.semaphore(f"moe_w1_in{i}")) for i in range(2))]
        w2_in = [nc_sem for nc_sem in (ph.ctx.enter_context(nc.semaphore(f"moe_w2_in{i}")) for i in range(2))]

        w1_pairs = a["L1_ffn_W1"].rearrange("(e i) c h -> e i c h", i=2)
        w2_pairs = a["L1_ffn_W2"].rearrange("(e i) h c -> e i h c", i=2)
        slot_pairs = slot_in[:].rearrange("p c (e i) b s -> p c e i (b s)", i=2)
        y_pairs = y_slot[:].rearrange("p (e i) b c -> p e i b c", i=2)
        b1_pairs = b1[:].rearrange("p (e i) h -> p e i h", i=2)
        b2_pairs = b2[:].rearrange("p (e i) c -> p e i c", i=2)

        def load_w1(sp, e, i):
            sp.dma_start(w1[i][:], w1_pairs[e, i].rearrange("(t p) h -> p t h", p=P)).then_inc(w1_in[i], 16)

        def load_w2(sp, e, i):
            sp.dma_start(w2[i][:], w2_pairs[e, i].rearrange("(t p) c -> p t c", p=P)).then_inc(w2_in[i], 16)

        made, small = ph.sem("made"), ph.sem("small")
        with ExitStack() as part:
            def sb(name, shape, dt=F32):
                return part.enter_context(nc.sbuf_tensor(f"route_{name}", shape, dt))

            stats, mv = sb("stats", [P, BT, 6]), sb("mv", [P, BT, 2])
            rstd, veps = sb("rstd", [P, BT]), sb("veps", [P, BT])
            xn, xnT = sb("xn", [P, BT, C]), sb("xnT", [P, 2, CT, T])
            logit, prob, rest = sb("logit", [P, BT, E]), sb("prob", [P, BT, E]), sb("rest", [P, BT, E])
            same, key, chosen = sb("same", [P, BT, E]), sb("key", [P, BT, E]), sb("chosen", [P, 2, BT, E])
            top, total = sb("top", [P, BT]), sb("total", [P, BT])
            taken, takenb = sb("taken", [P, BT, E]), sb("takenb", [P, BT, E], BF16)
            onehot = sb("onehot", [P, 2, NT, E, CAP])
            ln_done, var_eps, rstd_done, xn_done = (ph.sem(s) for s in ("ln_done", "var_eps", "rstd_done", "xn_done"))
            xT_mm, xT_act, xT_dve, logit_mm = (ph.sem(s) for s in ("xT_mm", "xT_act", "xT_dve", "logit_mm"))
            step, exp_done, pos_mm, hot_done = (ph.sem(s) for s in ("step", "exp_done", "pos_mm", "hot_done"))
            disp_mm, disp_act, disp_dve = (ph.sem(s) for s in ("disp_mm", "disp_act", "disp_dve"))
            SMALL = 4
            PREP = 3
            ROUTE = 17
            LOGITS, BEFORE = 4, 5
            x_tiles = x_all[:].rearrange("p b t c -> p (b t) c")

            def wide(v):
                return v.unsqueeze(2).to_broadcast([P, BT, E])

            def tiles_of(v):
                return v.rearrange("p b t e -> p (b t) e")

            with nc.Block() as block:
                @block.sync
                def _(sp):
                    with nc.allow_non_contiguous_dma(reason="small columns"):
                        parts = [(wr[:], a["L1_ffn_Wr"].rearrange("(t p) e -> p t e", p=P)),
                                 (br[:], a["L1_ffn_br"][None, :].to_broadcast([P, E])),
                                 (b1[:], a["L1_ffn_b1"].rearrange("e (t p) -> p e t", p=P)),
                                 (b2[:], a["L1_ffn_b2"].rearrange("e (t p) -> p e t", p=P))]
                        assert len(parts) == SMALL
                        for dst, src in parts:
                            sp.dma_start(dst, src).then_inc(small, 16)
                    for i in range(2):
                        load_w1(sp, 0, i)
                        load_w2(sp, 0, i)
                    sp.wait_ge(small, 16 * SMALL)

                @block.gpsimd
                def _(pool):
                    nc.gpsimd.iota(slots[:], pattern=[[0, E], [1, CAP]], base=0, channel_multiplier=0,
                                   allow_small_or_imprecise_dtypes=True).then_inc(made, 1)
                    nc.gpsimd.iota(orders[:], pattern=[[0, BT], [-1, E]], base=E, channel_multiplier=0,
                                   allow_small_or_imprecise_dtypes=True).then_inc(made, 1)
                    nc.gpsimd.memset(ones[:], 1.0).then_inc(made, 1)
                    pool.wait_ge(made, 3)
                    nc.gpsimd.affine_select(out=before[:], in_=ones[:], compare_op=ALU.is_gt, fill=0.0, base=0,
                                            pattern=[[1, P]], channel_multiplier=-1).then_inc(made, 1)
                    pool.wait_ge(ln_done, 2 * BT)
                    nc.gpsimd.tensor_scalar(veps[:], mv[:, :, 1], EPS, None, ALU.add).then_inc(var_eps, 1)
                    pool.wait_ge(var_eps, 1)
                    nc.gpsimd.tensor_tensor(rstd[:], veps[:], k["half"][:, 0:BT], ALU.pow).then_inc(rstd_done, 1)

                @block.vector
                def _(dve):
                    for t in range(BT):
                        nc.vector.bn_stats(stats[:, t], x_tiles[:, t, :]).then_inc(ln_done, 1)
                    for t in range(BT):
                        dve.wait_ge(ln_done, t + 1)
                        nc.vector.bn_aggr(mv[:, t], stats[:, t]).then_inc(ln_done, 1)
                    dve.wait_ge(rstd_done, 1)
                    for b in range(B):
                        for t in range(b * NT, (b + 1) * NT):
                            nc.vector.tensor_scalar(xn[:, t], x_tiles[:, t, :], mv[:, t, 0:1], rstd[:, t:t + 1],
                                                    ALU.subtract, ALU.mult).then_inc(xn_done, 1)
                        dve.wait_ge(xT_mm, CT * b + 1)
                        if b >= 2:
                            dve.wait_ge(logit_mm, b - 1)
                        nc.vector.tensor_copy(xnT[:, b % 2, 0, :], ps[:, CT * (b % 2), :]).then_inc(xT_dve, 1)
                    dve.wait_ge(small, 16 * SMALL)
                    dve.wait_ge(made, 4)
                    dve.wait_ge(logit_mm, B)
                    count = 0

                    def then(ins):
                        nonlocal count
                        count += 1
                        ins.then_inc(step, 1)
                        dve.wait_ge(step, count)

                    then(nc.vector.tensor_tensor(logit[:], ps[:, LOGITS, 0:BT * E].rearrange("p (t e) -> p t e", e=E),
                                                 br[:].unsqueeze(1).to_broadcast([P, BT, E]), ALU.add))
                    then(nc.vector.tensor_reduce(top[:], logit[:], AX_X, ALU.max))
                    then(nc.vector.tensor_tensor(logit[:], logit[:], wide(top[:]), ALU.subtract))
                    assert count == PREP
                    dve.wait_ge(exp_done, 1)
                    then(nc.vector.tensor_reduce(total[:], prob[:], AX_X, ALU.add))
                    then(nc.vector.reciprocal(total[:], total[:]))
                    then(nc.vector.tensor_tensor(prob[:], prob[:], wide(total[:]), ALU.mult))
                    for n in range(2):
                        p = prob if n == 0 else rest
                        then(nc.vector.tensor_reduce(top[:], p[:], AX_X, ALU.max))
                        then(nc.vector.tensor_tensor(same[:], p[:], wide(top[:]), ALU.is_equal))
                        then(nc.vector.tensor_tensor(key[:], same[:], orders[:], ALU.mult))
                        then(nc.vector.tensor_reduce(top[:], key[:], AX_X, ALU.max))
                        then(nc.vector.tensor_tensor(chosen[:, n], key[:], wide(top[:]), ALU.is_equal))
                        if n == 0:
                            then(nc.vector.scalar_tensor_tensor(out=rest[:], in0=chosen[:, 0], scalar=-2.0,
                                                                in1=prob[:], op0=ALU.mult, op1=ALU.add))
                    then(nc.vector.tensor_tensor(taken[:], chosen[:, 0], chosen[:, 1], ALU.add))
                    nc.vector.tensor_tensor(tiles_of(gate[:]), prob[:], taken[:], ALU.mult)
                    then(nc.vector.tensor_copy(takenb[:], taken[:]))
                    then(nc.vector.tensor_scalar(taken[:], taken[:], -OFF, OFF, ALU.mult, ALU.add))
                    assert count == ROUTE + 3
                    dve.wait_ge(pos_mm, 1)
                    then(nc.vector.tensor_tensor(tiles_of(place[:]),
                                                 ps[:, BEFORE, 0:BT * E].rearrange("p (t e) -> p t e", e=E),
                                                 taken[:], ALU.add))

                    def spot(b):
                        if b >= 2:
                            dve.wait_ge(disp_mm, 2 * CT * (b - 1))
                        for t in range(NT):
                            ins = nc.vector.tensor_tensor(onehot[:, b % 2, t], slots[:], place[:, b, t, :].unsqueeze(2)
                                                          .to_broadcast([P, E, CAP]), ALU.is_equal)
                        ins.then_inc(hot_done, 1)

                    spot(0)
                    for b in range(B):
                        if b + 1 < B:
                            spot(b + 1)
                        for half in range(2):
                            dve.wait_ge(disp_mm, 2 * CT * b + half + 1)
                            nc.vector.tensor_copy(slot_in[:, 0, half * EH:(half + 1) * EH, b, :],
                                                  ps[:, half, 0:EH * CAP].rearrange("p (e s) -> p e s", s=CAP)) \
                              .then_inc(disp_dve, 1)

                @block.scalar
                def _(act):
                    for b in range(B):
                        act.wait_ge(xT_mm, CT * b + 2)
                        if b >= 2:
                            act.wait_ge(logit_mm, b - 1)
                        nc.scalar.activation(xnT[:, b % 2, 1, :], ps[:, CT * (b % 2) + 1, :], ACT.Copy) \
                          .then_inc(xT_act, 1)
                    act.wait_ge(step, PREP)
                    nc.scalar.activation(prob[:], logit[:], ACT.Exp).then_inc(exp_done, 1)
                    for b in range(B):
                        for half in range(2):
                            act.wait_ge(disp_mm, 2 * CT * b + 3 + half)
                            nc.scalar.activation(slot_in[:, 1, half * EH:(half + 1) * EH, b, :],
                                                 ps[:, 2 + half, 0:EH * CAP].rearrange("p (e s) -> p e s", s=CAP),
                                                 ACT.Copy).then_inc(disp_act, 1)

                @block.tensor
                def _(pe):
                    pe.wait_ge(small, 16 * SMALL)
                    for b in range(B):
                        pe.wait_ge(xn_done, NT * (b + 1))
                        for c in range(CT):
                            if b >= 2:
                                pe.wait_ge((xT_dve, xT_act)[c], b - 1)
                            for t in range(NT):
                                ins = nc.tensor.transpose(ps[:, CT * (b % 2) + c, t * P:(t + 1) * P],
                                                          xn[:, NT * b + t, c * P:(c + 1) * P], k["ident"][:])
                            ins.then_inc(xT_mm, 1)
                        pe.wait_ge(xT_dve, b + 1)
                        pe.wait_ge(xT_act, b + 1)
                        for t in range(NT):
                            for c in range(CT):
                                ins = nc.tensor.matmul(ps[:, LOGITS, (NT * b + t) * E:(NT * b + t + 1) * E],
                                                       xnT[:, b % 2, c, t * P:(t + 1) * P], wr[:, c, :],
                                                       start=(c == 0), stop=(c == CT - 1))
                        ins.then_inc(logit_mm, 1)
                    pe.wait_ge(made, 4)
                    pe.wait_ge(step, ROUTE + 2)
                    for t in range(BT):
                        first = t - t % NT
                        for n in range(first, t + 1):
                            ins = nc.tensor.matmul(ps[:, BEFORE, t * E:(t + 1) * E], before[:] if n == t else ones[:],
                                                   takenb[:, n, :], start=(n == first), stop=(n == t))
                    ins.then_inc(pos_mm, 1)
                    for b in range(B):
                        pe.wait_ge(hot_done, b + 1)
                        for i in range(2 * CT):
                            c, half = i // 2, i % 2
                            if b:
                                pe.wait_ge((disp_dve, disp_act)[c], 2 * (b - 1) + half + 1)
                            for t in range(NT):
                                ins = nc.tensor.matmul(ps[:, i, 0:EH * CAP], xn[:, NT * b + t, c * P:(c + 1) * P],
                                                       onehot[:, b % 2, t, half * EH:(half + 1) * EH, :],
                                                       start=(t == 0), stop=(t == NT - 1))
                            ins.then_inc(disp_mm, 1)
            ph.clear()

        with ExitStack() as part:
            hid = [part.enter_context(nc.sbuf_tensor(f"moe_hid{i}", [P, ET, B * CAP], F32)) for i in range(2)]
            yT = part.enter_context(nc.sbuf_tensor("moe_yT", [P, 2, CT, B * CAP], F32))
            up_mm, up_out, down_mm, down_out = (ph.sem(s) for s in ("up_mm", "up_out", "down_mm", "down_out"))
            turn_mm, turn_out = ph.sem("yT_mm"), ph.sem("yT_out")
            with nc.Fori(0, E // 2) as e:
                with nc.Block() as block:
                    @block.sync
                    def _(sp):
                        for i in range(2):
                            sp.wait_ge(up_mm, ET * (i + 1))
                            load_w1(sp, (e + 1) % (E // 2), i)
                            sp.wait_ge(down_mm, CT * (i + 1))
                            load_w2(sp, (e + 1) % (E // 2), i)

                    @block.tensor
                    def _(pe):
                        def up(i):
                            pe.wait_ge(w1_in[i], e * 16 + 16)
                            for n in range(ET):
                                m = i * ET + n
                                if m >= 4:
                                    pe.wait_ge(up_out, m - 3)
                                for c in range(CT):
                                    ins = nc.tensor.matmul(ps[:, m % 4, 0:B * CAP], w1[i][:, c, n * P:(n + 1) * P],
                                                           slot_pairs[:, c, e, i, :],
                                                           start=(c == 0), stop=(c == CT - 1))
                                ins.then_inc(up_mm, 1)

                        def down(i):
                            pe.wait_ge(w2_in[i], e * 16 + 16)
                            pe.wait_ge(up_out, ET * (i + 1))
                            for c in range(CT):
                                if i:
                                    pe.wait_ge(down_out, c + 1)
                                for n in range(ET):
                                    ins = nc.tensor.matmul(ps[:, 4 + c, 0:B * CAP], w2[i][:, n, c * P:(c + 1) * P],
                                                           hid[i][:, n, :], start=(n == 0), stop=(n == ET - 1))
                                ins.then_inc(down_mm, 1)

                        def turn(i):
                            pe.wait_ge(down_out, CT * (i + 1))
                            for half in range(2):
                                if i:
                                    pe.wait_ge(turn_out, half + 1)
                                for n in range(B // 2):
                                    b = half * B // 2 + n
                                    for c in range(CT):
                                        ins = nc.tensor.transpose(ps[0:CAP, 6 + half, n * C + c * P:n * C + (c + 1) * P],
                                                                  yT[:, i, c, b * CAP:(b + 1) * CAP], k["ident"][:])
                                ins.then_inc(turn_mm, 1)

                        up(0)
                        down(0)
                        up(1)
                        turn(0)
                        down(1)
                        turn(1)

                    @block.scalar
                    def _(act):
                        for m in range(2 * ET):
                            i, n = m // ET, m % ET
                            act.wait_ge(up_mm, m + 1)
                            nc.scalar.activation(hid[i][:, n, :], ps[:, m % 4, 0:B * CAP], ACT.Relu,
                                                 bias=b1_pairs[:, e, i, n:n + 1]).then_inc(up_out, 1)

                    @block.vector
                    def _(dve):
                        for i in range(2):
                            for c in range(CT):
                                dve.wait_ge(down_mm, CT * i + c + 1)
                                nc.vector.tensor_scalar(yT[:, i, c, :], ps[:, 4 + c, 0:B * CAP],
                                                        b2_pairs[:, e, i, c:c + 1], None, ALU.add).then_inc(down_out, 1)
                            for half in range(2):
                                dve.wait_ge(turn_mm, 2 * i + half + 1)
                                nc.vector.tensor_copy(y_pairs[0:CAP, e, i, half * B // 2:(half + 1) * B // 2, :],
                                                      ps[0:CAP, 6 + half, :].rearrange("p (b c) -> p b c", c=C)) \
                                  .then_inc(turn_out, 1)
                ph.clear()

        with nc.Block() as block:
            @block.sync
            def _(sp):
                for i in range(2):
                    sp.wait_ge(w1_in[i], 16 * (E // 2 + 1))
                    sp.wait_ge(w2_in[i], 16 * (E // 2 + 1))

        with ExitStack() as part:
            pick = part.enter_context(nc.sbuf_tensor("moe_pick", [P, 3, E, CAP], F32))
            pickT = part.enter_context(nc.sbuf_tensor("moe_pickT", [P, 2, E, P], F32))
            fin = part.enter_context(nc.sbuf_tensor("moe_fin", [P, 2, NT, C], F32))
            pick_ok, turn_mm, turn_act, turn_dve, sum_mm, fin_ok, stored = (
                ph.sem(s) for s in ("pick_ok", "turn_mm", "turn_act", "turn_dve", "sum_mm", "fin_ok", "stored"))
            y_batch = y_slot[:].rearrange("p e (h i) c -> p e h i c", i=2)
            place_pairs = place[:].rearrange("p (h i) t e -> p h (i t) e", i=2)
            gate_pairs = gate[:].rearrange("p (h i) t e -> p h (i t) e", i=2)
            x_pairs = x_all[:].rearrange("p (h i) t c -> p h (i t) c", i=2)
            out_pairs = out.rearrange("(h i) t c -> h i t c", i=2)
            tiles = 2 * NT
            with nc.Fori(0, B // 2) as h:
                with nc.Block() as block:
                    @block.vector
                    def _(dve):
                        def choose(m):
                            if m >= 3:
                                dve.wait_ge(turn_mm, m - 2)
                            for n in range(E):
                                ins = nc.vector.tensor_scalar(pick[:, m % 3, n, :], slots[:, n, :],
                                                              place_pairs[:, h, m, n:n + 1], gate_pairs[:, h, m, n:n + 1],
                                                              ALU.is_equal, ALU.mult)
                            ins.then_inc(pick_ok, 1)

                        choose(0)
                        choose(1)
                        for m in range(tiles):
                            dve.wait_ge(turn_mm, m + 1)
                            if m >= 2:
                                dve.wait_ge(sum_mm, m - 1)
                            nc.vector.tensor_copy(pickT[0:CAP, m % 2, EH:E, :], ps[0:CAP, 2 * (m % 2) + 1, :]
                                                  .rearrange("p (e t) -> p e t", t=P)).then_inc(turn_dve, 1)
                            if m + 2 < tiles:
                                choose(m + 2)
                            dve.wait_ge(sum_mm, m + 1)
                            nc.vector.tensor_tensor(fin[:, m // NT, m % NT, :], ps[:, 4 + m % 2, 0:C],
                                                    x_pairs[:, h, m, :], ALU.add).then_inc(fin_ok, 1)

                    @block.scalar
                    def _(act):
                        for m in range(tiles):
                            act.wait_ge(turn_mm, m + 1)
                            if m >= 2:
                                act.wait_ge(sum_mm, m - 1)
                            nc.scalar.activation(pickT[0:CAP, m % 2, 0:EH, :], ps[0:CAP, 2 * (m % 2), :]
                                                 .rearrange("p (e t) -> p e t", t=P), ACT.Copy).then_inc(turn_act, 1)

                    @block.tensor
                    def _(pe):
                        def turn(m):
                            pe.wait_ge(pick_ok, m + 1)
                            if m >= 2:
                                pe.wait_ge(turn_act, m - 1)
                                pe.wait_ge(turn_dve, m - 1)
                            for n in range(E):
                                ins = nc.tensor.transpose(ps[0:CAP, 2 * (m % 2) + n // EH, (n % EH) * P:(n % EH + 1) * P],
                                                          pick[:, m % 3, n, :], k["ident"][:])
                            ins.then_inc(turn_mm, 1)

                        turn(0)
                        for m in range(tiles):
                            if m + 1 < tiles:
                                turn(m + 1)
                            pe.wait_ge(turn_act, m + 1)
                            pe.wait_ge(turn_dve, m + 1)
                            if m >= 2:
                                pe.wait_ge(fin_ok, m - 1)
                            for n in range(E):
                                ins = nc.tensor.matmul(ps[:, 4 + m % 2, 0:C], pickT[0:CAP, m % 2, n, :],
                                                       y_batch[0:CAP, n, h, m // NT, :],
                                                       start=(n == 0), stop=(n == E - 1))
                            ins.then_inc(sum_mm, 1)

                    @block.sync
                    def _(sp):
                        for i in range(2):
                            sp.wait_ge(fin_ok, NT * (i + 1))
                            sp.dma_start(out_pairs[h, i].rearrange("(t p) c -> p t c", p=P), fin[:, i]) \
                              .then_inc(stored, 16)
                        sp.wait_ge(stored, 32)
                ph.clear()


def load_stream(nc, ph, x_all, x):
    loaded = ph.sem("x_loaded")
    with nc.Block() as block:
        @block.sync
        def _(sp):
            sp.dma_start(x_all[:], x.rearrange("b (t p) c -> p b t c", p=P)).then_inc(loaded, 16)
            sp.wait_ge(loaded, 16)
    ph.clear()


def program(nc, a, out):
    with Phase(nc, "all") as ph:
        x_all = ph.sb("x_all", [P, B, NT, C])
        k = setup_constants(nc, ph)
        load_stream(nc, ph, x_all, a["x"])
        def wide(l, q, kk, v, o, bo, bq, bk, bv):
            g = lambda n: a[f"L{l}_xattn_{n}"]
            return dict(wq=g(q), wk=g(kk), wv=g(v), wo=g(o), bq=g(bq), bk=g(bk), bv=g(bv), bo=g(bo) if bo else None)
        wide_attention(nc, k, x_all, "self", None, None,
                       wide(0, "Wq", "Wk", "Wv", "Wp", None, "bq", "bk", "bv"), True)
        wide_attention(nc, k, x_all, "cross", a["x"], a["ctx_512"],
                       wide(0, "Wcq", "Wck", "Wcv", "Wp", "bp", "bcq", "bck", "bcv"), False)
        local_layers(nc, k, x_all, a)
        wide_attention(nc, k, x_all, "late", None, a["ctx_512"],
                       wide(1, "Wq", "Wk", "Wv", "Wo", "bo", "bq", "bk", "bv"), False)
        experts(nc, k, x_all, a, out)


_OUT = ((B, T, C), "float32")


def kernel(**inputs):
    import concourse.bacc as _bacc
    from concourse.bass_utils import run_bass_kernel_spmd as _run

    nc = _bacc.Bacc("TRN2", target_bir_lowering=False, num_devices=1)
    arrays, handles = {}, {}
    for name, value in {**inputs, **constants()}.items():
        value = np.ascontiguousarray(value)
        arrays[f"in_{name}_dram"] = value
        handles[name] = nc.dram_tensor(f"in_{name}_dram", value.shape, mybir.dt.from_np(value.dtype),
                                       kind="ExternalInput").ap()
    out = nc.dram_tensor("out_0_dram", _OUT[0], mybir.dt.from_np(np.dtype(_OUT[1])), kind="ExternalOutput").ap()
    program(nc, handles, out)
    return _run(nc, [arrays], core_ids=[0]).results[0]["out_0_dram"]
```
